# Optimizing a Trainium2 kernel written in Bass

```python
import numpy as np
import jax
import jax.numpy as jnp

def _softmax(x, axis=-1):
    return jax.nn.softmax(x, axis=axis)

def _gelu(x):
    return jax.nn.gelu(x, approximate=True)

def _silu(x):
    return jax.nn.silu(x)

def _sigmoid(x):
    return jax.nn.sigmoid(x)

def _layernorm(x, axis=-1, eps=1e-05):
    m = jnp.mean(x, axis=axis, keepdims=True)
    v = jnp.var(x, axis=axis, keepdims=True)
    return (x - m) / jnp.sqrt(v + eps)

def _scatter_add(tgt, idx, src, axis=0):
    return tgt.at[idx].add(src)

def _segment_sum(src, seg, n):
    return jax.ops.segment_sum(src, seg, n)
kernel_name = 'mk_seq_preln_d1_jaxref_r8_865fb7'

def setup_inputs(seed: int=0):
    np.random.seed(seed)
    _w = jnp.asarray

    def _L0_attn_setup():
        import jax, jax.numpy as jnp
        import numpy as np
        from jax import lax
        B, S, H = (2, 256, 256)
        NH, NKV, HD = (32, 8, 64)
        NG = NH // NKV
        THETA = 500000.0
        GATE_NORM = 16.0

        def _rope_cos_sin(seq_len, dtype):
            inv_freq = 1.0 / THETA ** (jnp.arange(0, HD, 2, dtype=jnp.float32) / HD)
            freqs = jnp.arange(seq_len, dtype=jnp.float32)[:, None] * inv_freq[None, :]
            emb = jnp.concatenate([freqs, freqs], axis=-1)
            return (jnp.cos(emb).astype(dtype), jnp.sin(emb).astype(dtype))

        def _rotate_half(x):
            x1, x2 = jnp.split(x, 2, axis=-1)
            return jnp.concatenate([-x2, x1], axis=-1)

        def _apply_rope(x, cos, sin):
            return x * cos[None, None] + _rotate_half(x) * sin[None, None]

        def _teacher(hs, wq, wk, wv, wo):
            b, s, _ = hs.shape
            q = (hs @ wq.T).reshape(b, s, NH, HD).transpose(0, 2, 1, 3)
            k = (hs @ wk.T).reshape(b, s, NKV, HD).transpose(0, 2, 1, 3)
            v = (hs @ wv.T).reshape(b, s, NKV, HD).transpose(0, 2, 1, 3)
            k = jnp.repeat(k, NG, axis=1)
            v = jnp.repeat(v, NG, axis=1)
            cos, sin = _rope_cos_sin(s, hs.dtype)
            q = _apply_rope(q, cos, sin)
            k = _apply_rope(k, cos, sin)
            scores = jnp.einsum('bhqd,bhkd->bhqk', q, k) / jnp.sqrt(jnp.float32(HD)).astype(hs.dtype)
            causal = jnp.tril(jnp.ones((s, s), dtype=bool))
            scores = jnp.where(causal[None, None], scores, jnp.finfo(scores.dtype).min)
            probs = jax.nn.softmax(scores, axis=-1)
            o = jnp.einsum('bhqk,bhkd->bhqd', probs, v)
            o = o.transpose(0, 2, 1, 3).reshape(b, s, NH * HD)
            return o @ wo.T

        def _gla_scan(q, k, v, g):
            b = q.shape[0]
            to_scan = lambda x: x.transpose(1, 0, 2, 3)
            S0 = jnp.zeros((b, NH, HD, HD), q.dtype)

            def step(Sstate, x):
                qt, kt, vt, gt = x
                Sstate = Sstate * jnp.exp(gt)[..., None] + kt[..., :, None] * vt[..., None, :]
                ot = jnp.einsum('bhk,bhkv->bhv', qt, Sstate)
                return (Sstate, ot)
            _, o = lax.scan(step, S0, (to_scan(q), to_scan(k), to_scan(v), to_scan(g)))
            return o.transpose(1, 0, 2, 3)

        def _student(hs, wq_s, wk_s, wv_s, wo_s):
            b, s, _ = hs.shape
            q = (hs @ wq_s.T).reshape(b, s, NH, HD)
            k = (hs @ wk_s.T).reshape(b, s, NKV, HD)
            v = (hs @ wv_s.T).reshape(b, s, NKV, HD)
            g = k
            k = jnp.repeat(k, NG, axis=2)
            v = jnp.repeat(v, NG, axis=2)
            g = jnp.repeat(g, NG, axis=2)
            q = jax.nn.softmax(q.astype(jnp.float32), axis=-1).astype(v.dtype)
            k = jax.nn.softmax(k.astype(jnp.float32), axis=-1).astype(v.dtype)
            g = (jax.nn.log_sigmoid(g.astype(jnp.float32)) / GATE_NORM).astype(v.dtype)
            o = _gla_scan(q, k, v, g)
            o = o.reshape(b, s, NH * HD)
            return o @ wo_s.T

        def _reference_tuple_inner(hidden_states, wq, wk, wv, wo, wq_s, wk_s, wv_s, wo_s):
            o_teacher = lax.stop_gradient(_teacher(hidden_states, wq, wk, wv, wo))
            o_student = _student(hidden_states, wq_s, wk_s, wv_s, wo_s)
            return (o_teacher, o_student)
        key = jax.random.key(seed)
        ks = jax.random.split(key, 9)
        s = 0.02
        return {'hidden_states': jax.random.normal(ks[0], (B, S, H), jnp.float32), 'wq': jax.random.normal(ks[1], (NH * HD, H), jnp.float32) * s, 'wk': jax.random.normal(ks[2], (NKV * HD, H), jnp.float32) * s, 'wv': jax.random.normal(ks[3], (NKV * HD, H), jnp.float32) * s, 'wo': jax.random.normal(ks[4], (H, NH * HD), jnp.float32) * s, 'wq_s': jax.random.normal(ks[5], (NH * HD, H), jnp.float32) * s, 'wk_s': jax.random.normal(ks[6], (NKV * HD, H), jnp.float32) * s, 'wv_s': jax.random.normal(ks[7], (NKV * HD, H), jnp.float32) * s, 'wo_s': jax.random.normal(ks[8], (H, NH * HD), jnp.float32) * s}
    _L0_attn_in = _L0_attn_setup()

    def _L0_ffn_setup():
        import jax, jax.numpy as jnp
        import numpy as np
        NUM_EXPERTS = 8
        TOP_K = 2
        EMB = 256
        MLP = 512
        B, S = (4, 128)
        key = jax.random.key(seed)
        ks = jax.random.split(key, 5)
        scale_x = 1.0
        return {'x': jax.random.normal(ks[0], (B, S, EMB), dtype=jnp.float32), 'gate_kernel': jax.random.normal(ks[1], (EMB, NUM_EXPERTS), dtype=jnp.float32) / np.sqrt(EMB), 'w0_kernel': jax.random.normal(ks[2], (NUM_EXPERTS, EMB, MLP), dtype=jnp.float32) / np.sqrt(EMB), 'w1_kernel': jax.random.normal(ks[3], (NUM_EXPERTS, EMB, MLP), dtype=jnp.float32) / np.sqrt(EMB), 'wo_kernel': jax.random.normal(ks[4], (NUM_EXPERTS, MLP, EMB), dtype=jnp.float32) / np.sqrt(MLP)}
    _L0_ffn_in = _L0_ffn_setup()
    _d = {'L0_attn_hidden_states': _L0_attn_in['hidden_states'], 'L0_attn_wq': _L0_attn_in['wq'], 'L0_attn_wk': _L0_attn_in['wk'], 'L0_attn_wv': _L0_attn_in['wv'], 'L0_attn_wo': _L0_attn_in['wo'], 'L0_attn_wq_s': _L0_attn_in['wq_s'], 'L0_attn_wk_s': _L0_attn_in['wk_s'], 'L0_attn_wv_s': _L0_attn_in['wv_s'], 'L0_attn_wo_s': _L0_attn_in['wo_s'], 'L0_ffn_gate_kernel': _L0_ffn_in['gate_kernel'], 'L0_ffn_w0_kernel': _L0_ffn_in['w0_kernel'], 'L0_ffn_w1_kernel': _L0_ffn_in['w1_kernel'], 'L0_ffn_wo_kernel': _L0_ffn_in['wo_kernel']}
    _x0 = _d['L0_attn_hidden_states']
    _d['L0_attn_hidden_states'] = jax.random.normal(jax.random.fold_in(jax.random.key(seed), 1), (8, 256, 256), dtype=_x0.dtype)
    del _x0
    return _d

def reference(L0_attn_hidden_states, L0_attn_wq, L0_attn_wk, L0_attn_wv, L0_attn_wo, L0_attn_wq_s, L0_attn_wk_s, L0_attn_wv_s, L0_attn_wo_s, L0_ffn_gate_kernel, L0_ffn_w0_kernel, L0_ffn_w1_kernel, L0_ffn_wo_kernel):

    def _L0_attn_ref(hidden_states, wq, wk, wv, wo, wq_s, wk_s, wv_s, wo_s):
        import jax, jax.numpy as jnp
        import numpy as np
        from jax import lax
        B, S, H = (2, 256, 256)
        NH, NKV, HD = (32, 8, 64)
        NG = NH // NKV
        THETA = 500000.0
        GATE_NORM = 16.0

        def _rope_cos_sin(seq_len, dtype):
            inv_freq = 1.0 / THETA ** (jnp.arange(0, HD, 2, dtype=jnp.float32) / HD)
            freqs = jnp.arange(seq_len, dtype=jnp.float32)[:, None] * inv_freq[None, :]
            emb = jnp.concatenate([freqs, freqs], axis=-1)
            return (jnp.cos(emb).astype(dtype), jnp.sin(emb).astype(dtype))

        def _rotate_half(x):
            x1, x2 = jnp.split(x, 2, axis=-1)
            return jnp.concatenate([-x2, x1], axis=-1)

        def _apply_rope(x, cos, sin):
            return x * cos[None, None] + _rotate_half(x) * sin[None, None]

        def _teacher(hs, wq, wk, wv, wo):
            b, s, _ = hs.shape
            q = (hs @ wq.T).reshape(b, s, NH, HD).transpose(0, 2, 1, 3)
            k = (hs @ wk.T).reshape(b, s, NKV, HD).transpose(0, 2, 1, 3)
            v = (hs @ wv.T).reshape(b, s, NKV, HD).transpose(0, 2, 1, 3)
            k = jnp.repeat(k, NG, axis=1)
            v = jnp.repeat(v, NG, axis=1)
            cos, sin = _rope_cos_sin(s, hs.dtype)
            q = _apply_rope(q, cos, sin)
            k = _apply_rope(k, cos, sin)
            scores = jnp.einsum('bhqd,bhkd->bhqk', q, k) / jnp.sqrt(jnp.float32(HD)).astype(hs.dtype)
            causal = jnp.tril(jnp.ones((s, s), dtype=bool))
            scores = jnp.where(causal[None, None], scores, jnp.finfo(scores.dtype).min)
            probs = jax.nn.softmax(scores, axis=-1)
            o = jnp.einsum('bhqk,bhkd->bhqd', probs, v)
            o = o.transpose(0, 2, 1, 3).reshape(b, s, NH * HD)
            return o @ wo.T

        def _gla_scan(q, k, v, g):
            b = q.shape[0]
            to_scan = lambda x: x.transpose(1, 0, 2, 3)
            S0 = jnp.zeros((b, NH, HD, HD), q.dtype)

            def step(Sstate, x):
                qt, kt, vt, gt = x
                Sstate = Sstate * jnp.exp(gt)[..., None] + kt[..., :, None] * vt[..., None, :]
                ot = jnp.einsum('bhk,bhkv->bhv', qt, Sstate)
                return (Sstate, ot)
            _, o = lax.scan(step, S0, (to_scan(q), to_scan(k), to_scan(v), to_scan(g)))
            return o.transpose(1, 0, 2, 3)

        def _student(hs, wq_s, wk_s, wv_s, wo_s):
            b, s, _ = hs.shape
            q = (hs @ wq_s.T).reshape(b, s, NH, HD)
            k = (hs @ wk_s.T).reshape(b, s, NKV, HD)
            v = (hs @ wv_s.T).reshape(b, s, NKV, HD)
            g = k
            k = jnp.repeat(k, NG, axis=2)
            v = jnp.repeat(v, NG, axis=2)
            g = jnp.repeat(g, NG, axis=2)
            q = jax.nn.softmax(q.astype(jnp.float32), axis=-1).astype(v.dtype)
            k = jax.nn.softmax(k.astype(jnp.float32), axis=-1).astype(v.dtype)
            g = (jax.nn.log_sigmoid(g.astype(jnp.float32)) / GATE_NORM).astype(v.dtype)
            o = _gla_scan(q, k, v, g)
            o = o.reshape(b, s, NH * HD)
            return o @ wo_s.T

        def _reference_tuple_inner(hidden_states, wq, wk, wv, wo, wq_s, wk_s, wv_s, wo_s):
            o_teacher = lax.stop_gradient(_teacher(hidden_states, wq, wk, wv, wo))
            o_student = _student(hidden_states, wq_s, wk_s, wv_s, wo_s)
            return (o_teacher, o_student)
        return _reference_tuple_inner(hidden_states, wq, wk, wv, wo, wq_s, wk_s, wv_s, wo_s)[0]

    def _L0_ffn_ref(x, gate_kernel, w0_kernel, w1_kernel, wo_kernel):
        import jax, jax.numpy as jnp
        import numpy as np
        NUM_EXPERTS = 8
        TOP_K = 2
        EMB = 256
        MLP = 512
        B, S = (4, 128)
        gate_logits = jnp.einsum('bsd,de->bse', x, gate_kernel)
        top_k_weights, top_k_indices = jax.lax.top_k(gate_logits, TOP_K)
        top_k_weights = jax.nn.softmax(top_k_weights.astype(jnp.float32), axis=-1).astype(x.dtype)
        one_hot = jax.nn.one_hot(top_k_indices, NUM_EXPERTS, dtype=x.dtype)
        combine = jnp.einsum('bsk,bske->bse', top_k_weights, one_hot)
        h0 = jnp.einsum('bsd,edm->bsem', x, w0_kernel)
        h1 = jnp.einsum('bsd,edm->bsem', x, w1_kernel)
        inter = jax.nn.silu(h0) * h1
        out = jnp.einsum('bse,bsem,emd->bsd', combine, inter, wo_kernel)
        return out
    x = L0_attn_hidden_states
    x = x + _L0_attn_ref(_layernorm(x, axis=-1), L0_attn_wq, L0_attn_wk, L0_attn_wv, L0_attn_wo, L0_attn_wq_s, L0_attn_wk_s, L0_attn_wv_s, L0_attn_wo_s)
    x = x + _L0_ffn_ref(_layernorm(x, axis=-1), L0_ffn_gate_kernel, L0_ffn_w0_kernel, L0_ffn_w1_kernel, L0_ffn_wo_kernel)
    return x

_drawn_inputs = setup_inputs


def setup_inputs(seed=0):
    import zlib

    import numpy as np

    out = dict(_drawn_inputs(seed))
    spreads = {}
    factors = {'L0_attn_wq': 3.864, 'L0_attn_wk': 3.175}
    for name, (base, spread) in spreads.items():
        noise = np.random.default_rng([zlib.crc32(name.encode()), seed]).standard_normal(out[name].shape)
        drawn = base * np.exp(spread * noise) if base else spread * noise
        out[name] = jnp.asarray(drawn.astype(out[name].dtype))
    for name, factor in factors.items():
        out[name] = (out[name] * factor).astype(out[name].dtype)
    return out
```

```python
from contextlib import ExitStack

import numpy as np

import concourse.bass as bass
import concourse.mybir as mybir

F32 = mybir.dt.float32
F32R = mybir.dt.float32r
BF16 = mybir.dt.bfloat16
I32 = mybir.dt.int32
U32 = mybir.dt.uint32
ALU = mybir.AluOpType
ACT = mybir.ActivationFunctionType
AX = mybir.AxisListType

P = 128
BATCH, SEQ, EMB = 8, 256, 256
HEADS, KV_HEADS, HD = 32, 8, 64
GROUP = HEADS // KV_HEADS
KT = EMB // P
TT = SEQ // P
TILES = BATCH * TT
TOKENS = BATCH * SEQ
QK = (GROUP + 1) * HD
GW = QK + HD
PAIRS = GROUP // 2
THETA = 500000.0
EPS = 1e-5
MASKED = -1e30
STACK = GROUP * P + 3 * HD

EXPERTS, MLP = 8, 512
MT = MLP // P
BLOCKS = TOKENS * 2 // P + EXPERTS - 1
ROWS = BLOCKS * P
RSQRT_MAGIC = 1597463007.0
SILU = ACT.Silu


def shape_constants():
    inv = (np.float32(1.0) / np.power(np.float32(THETA), np.arange(0, HD, 2, dtype=np.float32) / np.float32(HD))).astype(np.float32)
    ang = np.arange(SEQ, dtype=np.float32)[:, None] * inv[None, :]
    cos, sin = np.cos(ang).astype(np.float32), np.sin(ang).astype(np.float32)
    cos2 = np.concatenate([cos, cos], 1).reshape(TT, P, HD).transpose(1, 0, 2)
    sin2 = np.concatenate([-sin, sin], 1).reshape(TT, P, HD).transpose(1, 0, 2)
    q, k = np.arange(P)[:, None], np.arange(P)[None, :]
    mask = np.concatenate([np.zeros((P, P)), np.where(k > q, MASKED, 0.0)], 1).astype(np.float32)
    ident = np.eye(P, dtype=np.float32)
    before = (q < k).astype(np.float32)
    ones = np.ones((P, P), np.float32)
    attn = np.concatenate([cos2.reshape(P, -1), sin2.reshape(P, -1), mask, ident], 1)
    rev = np.tile(EXPERTS - np.arange(EXPERTS, dtype=np.float32), TILES)
    steps = np.tile(P * np.arange(TILES, dtype=np.float32), EXPERTS)
    starts = np.repeat(P * np.arange(BLOCKS + 1, dtype=np.float32), EXPERTS)
    route = np.concatenate([before, ones, np.tile(np.concatenate([rev, steps, starts]), (P, 1))], 1)
    return np.ascontiguousarray(attn, np.float32), np.ascontiguousarray(route, np.float32)


def attention(nc, ctx, t, x_all, debug=None):

    def sb(name, shape, dt=F32):
        return ctx.enter_context(nc.sbuf_tensor(name, shape, dt))

    def sem(name):
        return ctx.enter_context(nc.semaphore(name))

    tables = sb("tables", [P, 2 * TT * HD + 3 * P])
    cos = tables[:, 0:TT * HD].rearrange("p (t d) -> p t d", t=TT)
    sin = tables[:, TT * HD:2 * TT * HD].rearrange("p (t d) -> p t d", t=TT)
    mask = tables[:, 2 * TT * HD:2 * TT * HD + 2 * P]
    ident = tables[:, 2 * TT * HD + 2 * P:2 * TT * HD + 3 * P]

    w_raw = sb("w_raw", [P, 2, KT * GW])
    w_hi = sb("w_hi", [P, KT, KV_HEADS * GW], F32R)
    w_lo = sb("w_lo", [P, KT, KV_HEADS * GW], F32R)
    wo_hi = sb("wo_hi", [P, HEADS // 2 * EMB], F32R)
    wo_lo = sb("wo_lo", [P, HEADS // 2 * EMB], F32R)

    stats = sb("stats", [P, TILES, 6])
    moments = sb("moments", [P, TILES, 2])
    rstd = sb("rstd", [P, TILES])
    newton = sb("newton", [P, 3, TILES])
    xn = sb("xn", [P, TT, EMB])
    xT_hi = sb("xT_hi", [P, KT, SEQ], F32R)
    xT_lo = sb("xT_lo", [P, KT, SEQ], F32R)

    by_cos = sb("by_cos", [P, TT, QK])
    by_sin = sb("by_sin", [P, TT, QK])
    rotated = sb("rotated", [P, TT, QK])
    stack = sb("stack", [P, TT, STACK])
    v_raw = sb("v_raw", [P, TT, HD])
    v_hi = sb("v_hi", [P, 2, TT, 3 * HD], F32R)
    v_lo = sb("v_lo", [P, 2, TT, 3 * HD], F32R)
    qT = sb("qT", [P, TT, GROUP * P], F32R)
    kT = sb("kT", [P, 2, SEQ], F32R)
    masked = sb("masked", [P, 2, 3 * P])
    neg_max = sb("neg_max", [P, 2, TT])
    exps = sb("exps", [P, 2, 3 * P])
    sums = sb("sums", [P, 2, TT])
    inv_sums = sb("inv_sums", [P, 2, TT])
    probs = sb("probs", [P, 2, 3 * P])
    pT_hi = sb("pT_hi", [P, GROUP, 3 * P], F32R)
    pT_lo = sb("pT_lo", [P, GROUP, 3 * P], F32R)
    oT_hi = sb("oT_hi", [P, PAIRS, SEQ], F32R)
    oT_lo = sb("oT_lo", [P, PAIRS, SEQ], F32R)

    def bank(name):
        return ctx.enter_context(nc.psum_tensor(name, [P, 512], F32))

    work = [bank("work0"), bank("work1")]
    s_bank = [bank("scores0"), bank("scores1")]
    p_bank = [bank("probsT0"), bank("probsT1")]
    o_bank = bank("heads_out")
    y_bank = bank("attn_out")

    consts_in = sem("consts_in")
    x_first_in = sem("x_first_in")
    x_rest_in = sem("x_rest_in")
    w_in = [sem("w_in0"), sem("w_in1")]
    w_split = sem("w_split")
    w_hi_done = sem("w_hi_done")
    wo_in = [sem("wo_in0"), sem("wo_in1")]
    wo_hi_done = sem("wo_hi_done")
    wo_split = sem("wo_split")
    zeroed = sem("zeroed")
    step = sem("step")
    dve_passed = sem("dve_passed")
    pool_passed = sem("pool_passed")
    xn_done = sem("xn_done")
    xT_ps = sem("xT_ps")
    xT_hi_done = sem("xT_hi_done")
    xT_lo_done = sem("xT_lo_done")
    proj_ps = sem("proj_ps")
    v_read = sem("v_read")
    v_hi_done = sem("v_hi_done")
    v_done = sem("v_done")
    rope_parts = sem("rope_parts")
    rope_done = sem("rope_done")
    stack_hi = sem("stack_hi")
    stack_lo = sem("stack_lo")
    qT_ps = sem("qT_ps")
    qT_done = sem("qT_done")
    kT_ps = sem("kT_ps")
    kT_done = sem("kT_done")
    s_ps = sem("s_ps")
    s_read = sem("s_read")
    exp_done = sem("exp_done")
    inv_done = sem("inv_done")
    probs_done = sem("probs_done")
    pT_ps = sem("pT_ps")
    pT_hi_done = sem("pT_hi_done")
    pT_lo_done = sem("pT_lo_done")
    o_ps = sem("o_ps")
    o_hi_done = sem("o_hi_done")
    o_lo_done = sem("o_lo_done")
    y_ps = sem("y_ps")
    y_added = sem("y_added")


    TURNS = BATCH * KV_HEADS

    def turns(eng, turn):
        def rounds(b, last_batch):
            with eng.Fori(0, KV_HEADS // 2 - 1) as i:
                turn(b * KV_HEADS + i * 2, 0, i * 2, b, False, False)
                turn(b * KV_HEADS + i * 2 + 1, 1, i * 2 + 1, b, False, False)
            turn(b * KV_HEADS + KV_HEADS - 2, 0, KV_HEADS - 2, b, not last_batch, False)
            turn(b * KV_HEADS + KV_HEADS - 1, 1, KV_HEADS - 1, b, False, last_batch)
        with eng.Fori(0, BATCH - 1) as b:
            rounds(b, False)
        rounds(BATCH - 1, True)

    block = ctx.enter_context(nc.Block())

    @block.sync
    def _(sp):
        sp.dma_start(tables[:, :], t["attn_consts"]).then_inc(consts_in, 16)
        x_dram = t["x"].rearrange("b (t p) e -> p (b t) e", p=P)
        sp.dma_start(x_all[:, TT:2 * TT, :], x_dram[:, 0:TT, :]).then_inc(x_first_in, 16)
        for g in range(2):
            sp.dma_start(w_raw[:, g, :], t["w_qkv"][:, g, :]).then_inc(w_in[g], 16)
        sp.dma_start(x_all[:, 2 * TT:TT + TILES, :], x_dram[:, TT:TILES, :]).then_inc(x_rest_in, 16)
        for g in range(2, KV_HEADS):
            sp.wait_ge(w_split, g - 1)
            sp.dma_start(w_raw[:, g % 2, :], t["w_qkv"][:, g, :]).then_inc(w_in[g % 2], 16)
        for c in range(2):
            sp.wait_ge(w_split, KV_HEADS - 1 + c)
            sp.dma_start(w_raw[:, c, 0:512], t["wo"][:, c * 512:(c + 1) * 512]).then_inc(wo_in[c % 2], 16)
        for c in range(2, 8):
            sp.wait_ge(wo_split, c - 1)
            sp.dma_start(w_raw[:, c % 2, 0:512], t["wo"][:, c * 512:(c + 1) * 512]).then_inc(wo_in[c % 2], 16)

    @block.tensor
    def _(pe):
        def x_transposes(first_tile):
            for tt in range(TT):
                pe.wait_ge(xn_done, first_tile + tt + 1)
                for k in range(KT):
                    mm = nc.tensor.transpose(work[tt][:, k * P:(k + 1) * P], xn[:, tt, k * P:(k + 1) * P], ident)
                mm.then_inc(xT_ps, 1)

        def project(m, parity, g, tt):
            ps = work[(tt + parity) % 2]
            n = 0
            for k in range(KT):
                for a, w in ((xT_hi, w_hi), (xT_lo, w_hi), (xT_hi, w_lo)):
                    mm = nc.tensor.matmul(ps[:, 0:GW], a[:, k, tt * P:(tt + 1) * P], w[:, k, bass.ds(g * GW, GW)],
                                          start=(n == 0), stop=(n == 3 * KT - 1))
                    n += 1
            mm.then_inc(proj_ps, 1)

        def q_transposes(m, parity, tt):
            ps = work[(tt + parity) % 2]
            pe.wait_ge(stack_hi, m * 2 + tt + 1)
            pe.wait_ge(stack_lo, m * 2 + tt + 1)
            for h in range(GROUP):
                mm = nc.tensor.transpose(ps[:, h * P:(h + 1) * P], stack[:, tt, h * P:(h + 1) * P], ident)
            mm.then_inc(qT_ps, 1)

        def k_transposes(m, parity):
            ps = work[parity]
            pe.wait_ge(qT_done, m * 2 + 1)
            for form in range(2):
                at = GROUP * P + form * HD
                for tt in range(TT):
                    mm = nc.tensor.transpose(ps[:, (form * TT + tt) * P:(form * TT + tt + 1) * P],
                                             stack[:, tt, at:at + P], ident)
            mm.then_inc(kT_ps, 1)

        def scores(n, h):
            ps = s_bank[h % 2]
            pe.wait_ge(s_read, n * GROUP + h + 1)
            for tt in range(TT):
                for form in range(2):
                    mm = nc.tensor.matmul(ps[:, tt * SEQ:(tt + 1) * SEQ], qT[:, tt, h * P:(h + 1) * P], kT[:, form, :],
                                          start=(form == 0), stop=(form == 1))
            mm.then_inc(s_ps, 1)

        def prob_transposes(n, h):
            ps = p_bank[h % 2]
            pe.wait_ge(probs_done, n * GROUP + h + 3)
            pe.wait_ge(pT_lo_done, n * GROUP + h + 3)
            for c, (lo, at) in enumerate(((0, 0), (P, P), (2 * P, 2 * P))):
                mm = nc.tensor.transpose(ps[:, at:at + P], probs[:, h % 2, lo:lo + P], ident)
            mm.then_inc(pT_ps, 1)

        def values(n, parity):
            pe.wait_ge(pT_lo_done, n * GROUP + 4)
            pe.wait_ge(v_done, n + 1)
            pe.wait_ge(o_lo_done, n + 1)
            out = o_bank[:, :].rearrange("p (pair q) -> p pair q", pair=PAIRS)
            first = True
            for odd in range(2):
                form = slice(HD, 3 * HD) if odd == 0 else slice(0, 2 * HD)
                for kt in range(TT):
                    for v, pT in ((v_hi, pT_hi), (v_lo, pT_hi), (v_hi, pT_lo)):
                        heads = pT[:, odd:GROUP:2, :]
                        if kt == 0:
                            mm = nc.tensor.matmul(out, v[:, parity, kt, form], heads[:, :, 0:2 * P],
                                                  start=first, stop=False, skip_group_check=True)
                        else:
                            mm = nc.tensor.matmul(out[:, :, P:2 * P], v[:, parity, kt, form], heads[:, :, 2 * P:3 * P],
                                                  start=False, stop=True, skip_group_check=True)
                        first = False
            mm.then_inc(o_ps, 1)

        def output(n, g_prev):
            pe.wait_ge(o_lo_done, n + 2)
            pe.wait_ge(y_added, n + 1)
            for tt in range(TT):
                i = 0
                for pair in range(PAIRS):
                    for o, w in ((oT_hi, wo_hi), (oT_lo, wo_hi), (oT_hi, wo_lo)):
                        mm = nc.tensor.matmul(y_bank[:, tt * EMB:(tt + 1) * EMB], o[:, pair, tt * P:(tt + 1) * P],
                                              w[:, bass.ds((g_prev * PAIRS + pair) * EMB, EMB)],
                                              start=(i == 0), stop=(i == 3 * PAIRS - 1))
                        i += 1
            mm.then_inc(y_ps, 1)

        def turn(n, parity, g, b, prepare, last):
            m, odd = n + 1, 1 - parity
            g_next = (g + 1) % KV_HEADS
            pe.wait_ge(qT_done, n * 2 + 2)
            pe.wait_ge(kT_done, n + 1)
            scores(n, 0)
            scores(n, 1)
            if not last:
                if isinstance(g, int) and g == KV_HEADS - 1:
                    pe.wait_ge(xT_hi_done, b * TT + 2 * TT)
                    pe.wait_ge(xT_lo_done, b * TT + 2 * TT)
                project(m, odd, g_next, 0)
            scores(n, 2)
            if not last:
                project(m, odd, g_next, 1)
            scores(n, 3)
            values(n, odd)
            if not last:
                q_transposes(m, odd, 0)
                q_transposes(m, odd, 1)
            prob_transposes(n, 0)
            output(n, (g + KV_HEADS - 1) % KV_HEADS)
            if not last:
                k_transposes(m, odd)
            prob_transposes(n, 1)
            prob_transposes(n, 2)
            prob_transposes(n, 3)
            if prepare:
                pe.wait_ge(qT_done, m * 2 + 2)
                pe.wait_ge(kT_done, m + 1)
                x_transposes(b * TT + TT)

        pe.wait_ge(consts_in, 16)
        x_transposes(0)
        pe.wait_ge(xT_hi_done, TT)
        pe.wait_ge(xT_lo_done, TT)
        pe.wait_ge(w_split, 1)
        project(0, 0, 0, 0)
        project(0, 0, 0, 1)
        q_transposes(0, 0, 0)
        q_transposes(0, 0, 1)
        k_transposes(0, 0)
        pe.wait_ge(w_split, KV_HEADS)
        pe.wait_ge(wo_split, 8)
        pe.wait_ge(zeroed, 1)
        turns(pe, turn)
        values(TURNS, 1)
        output(TURNS, KV_HEADS - 1)

    @block.scalar
    def _(act):
        def x_hi(tile, tt):
            act.wait_ge(xT_ps, tile + 1)
            nc.scalar.copy(xT_hi[:, :, tt * P:(tt + 1) * P],
                           work[tt][:, 0:KT * P].rearrange("p (k q) -> p k q", k=KT)).then_inc(xT_hi_done, 1)

        def split_stack(m, tt, first=False):
            act.wait_ge(rope_done, m * 2 + tt + 1)
            if not first:
                act.wait_ge(kT_ps, m)
            hi = stack[:, tt, 0:(GROUP + 1) * P].rearrange("p (h two d) -> p h two d", two=2, d=HD)[:, :, 1, :]
            nc.scalar.copy(hi.bitcast(F32R), rotated[:, tt, :].rearrange("p (h d) -> p h d", d=HD)).then_inc(stack_hi, 1)

        def copy_qT(m, parity, tt):
            act.wait_ge(qT_ps, m * 2 + tt + 1)
            nc.scalar.copy(qT[:, tt, :], work[(tt + parity) % 2][:, :]).then_inc(qT_done, 1)

        def exponentials(n, h):
            s = h % 2
            act.wait_ge(s_read, n * GROUP + h + 3)
            act.wait_ge(probs_done, n * GROUP + h + 1)
            nc.scalar.activation(exps[:, s, 0:P], masked[:, s, 0:P], ACT.Exp, bias=neg_max[:, s, 0:1], scale=-1.0,
                                 accum_out=sums[:, s, 0:1])
            nc.scalar.activation(exps[:, s, P:3 * P], masked[:, s, P:3 * P], ACT.Exp, bias=neg_max[:, s, 1:2],
                                 scale=-1.0, accum_out=sums[:, s, 1:2]).then_inc(exp_done, 1)

        def probs_hi(n, h):
            act.wait_ge(pT_ps, n * GROUP + h + 3)
            nc.scalar.copy(pT_hi[:, h, :], p_bank[h % 2][:, 0:3 * P]).then_inc(pT_hi_done, 1)

        def out_hi(n):
            act.wait_ge(o_ps, n + 1)
            nc.scalar.copy(oT_hi[:, :, :], o_bank[:, :].rearrange("p (pair q) -> p pair q", pair=PAIRS)).then_inc(o_hi_done, 1)

        def turn(n, parity, g, b, prepare, last):
            m, odd = n + 1, 1 - parity
            exponentials(n, 0)
            exponentials(n, 1)
            if not last:
                split_stack(m, 0)
            exponentials(n, 2)
            if not last:
                split_stack(m, 1)
            exponentials(n, 3)
            out_hi(n)
            if not last:
                copy_qT(m, odd, 0)
                copy_qT(m, odd, 1)
            for h in range(GROUP):
                probs_hi(n, h)
            if prepare:
                x_hi(b * TT + TT, 0)
                x_hi(b * TT + TT + 1, 1)

        act.sem_inc(exp_done, 2)
        x_hi(0, 0)
        x_hi(1, 1)
        for g in range(KV_HEADS):
            act.wait_ge(w_in[g % 2], 16 * (g // 2 + 1))
            nc.scalar.copy(w_hi[:, :, g * GW:(g + 1) * GW],
                           w_raw[:, g % 2, :].rearrange("p (k n) -> p k n", k=KT)).then_inc(w_hi_done, 1)
            if g == 0:
                split_stack(0, 0, True)
                split_stack(0, 1, True)
                copy_qT(0, 0, 0)
                copy_qT(0, 0, 1)
        for c in range(8):
            act.wait_ge(wo_in[c % 2], 16 * (c // 2 + 1))
            nc.scalar.copy(wo_hi[:, c * 512:(c + 1) * 512], w_raw[:, c % 2, 0:512]).then_inc(wo_hi_done, 1)
        turns(act, turn)
        out_hi(TURNS)

    @block.vector
    def _(dve):
        chain = [0]

        def wait_own(ins):
            chain[0] += 1
            ins.then_inc(step, 1)
            dve.wait_ge(step, chain[0])

        def normalise(tile, tt, first=False):
            if not first:
                dve.wait_ge(xT_ps, tile - 1)
            nc.vector.tensor_scalar(xn[:, tt, :], x_all[:, bass.ds(tile + TT, 1), :].rearrange("p o e -> p (o e)"),
                                    moments[:, bass.ds(tile, 1), 0:1].rearrange("p o e -> p (o e)"), rstd[:, bass.ds(tile, 1)],
                                    ALU.subtract, ALU.mult).then_inc(xn_done, 1)

        def x_lo(tile, tt):
            dve.wait_ge(xT_hi_done, tile + 1)
            nc.vector.tensor_tensor(xT_lo[:, :, tt * P:(tt + 1) * P],
                                    work[tt][:, 0:KT * P].rearrange("p (k q) -> p k q", k=KT),
                                    xT_hi[:, :, tt * P:(tt + 1) * P].bitcast(F32), ALU.subtract).then_inc(xT_lo_done, 1)

        def rope(m, parity, tt, first=False):
            ps = work[(tt + parity) % 2]
            dve.wait_ge(proj_ps, m * 2 + tt + 1)
            if not first:
                dve.wait_ge(v_done, m + 1)
                dve.wait_ge(rope_done, m * 2 + tt - 1)
            nc.vector.tensor_copy(v_raw[:, tt, :], ps[:, QK:GW]).then_inc(v_read, 1)
            x = ps[:, 0:QK].rearrange("p (h two d) -> p h two d", two=2, d=HD // 2)
            o = by_sin[:, tt, :].rearrange("p (h two d) -> p h two d", two=2, d=HD // 2)
            for half in range(2):
                s = sin[:, tt, half * 32:half * 32 + 32].rearrange("p (o d) -> p o d", o=1).to_broadcast([P, GROUP + 1, 32])
                nc.vector.tensor_tensor(o[:, :, half, :], x[:, :, 1 - half, :], s, ALU.mult)
            c = cos[:, tt, :].rearrange("p (o d) -> p o d", o=1).to_broadcast([P, GROUP + 1, HD])
            nc.vector.tensor_tensor(by_cos[:, tt, :].rearrange("p (h d) -> p h d", d=HD),
                                    ps[:, 0:QK].rearrange("p (h d) -> p h d", d=HD), c, ALU.mult).then_inc(rope_parts, 1)

        def maxima(n, h):
            s = h % 2
            dve.wait_ge(consts_in, 16)
            dve.wait_ge(s_ps, n * GROUP + h + 1)
            dve.wait_ge(exp_done, n * GROUP + h + 1)
            dve.sem_inc(dve_passed, 1)
            nc.vector.tensor_tensor_reduce(masked[:, s, 0:P], s_bank[s][:, 0:P], mask[:, P:2 * P], -(HD ** -0.5), 3e38,
                                           ALU.add, ALU.min, neg_max[:, s, 0:1])
            nc.vector.tensor_tensor_reduce(masked[:, s, P:3 * P], s_bank[s][:, SEQ:2 * SEQ], mask[:, 0:2 * P],
                                           -(HD ** -0.5), 3e38, ALU.add, ALU.min, neg_max[:, s, 1:2]).then_inc(s_read, 1)

        def inverses(n, h):
            s = h % 2
            dve.wait_ge(exp_done, n * GROUP + h + 3)
            nc.vector.reciprocal(inv_sums[:, s, :], sums[:, s, :]).then_inc(inv_done, 1)

        def probs_lo(n, h):
            dve.wait_ge(pT_hi_done, n * GROUP + h + 1)
            nc.vector.tensor_tensor(pT_lo[:, h, :], p_bank[h % 2][:, 0:3 * P], pT_hi[:, h, :].bitcast(F32),
                                    ALU.subtract).then_inc(pT_lo_done, 1)

        def out_lo(n):
            dve.wait_ge(o_hi_done, n + 1)
            nc.vector.tensor_tensor(oT_lo[:, :, :], o_bank[:, :].rearrange("p (pair q) -> p pair q", pair=PAIRS),
                                    oT_hi[:, :, :].bitcast(F32), ALU.subtract).then_inc(o_lo_done, 1)

        def copy_kT(m, parity):
            dve.wait_ge(kT_ps, m + 1)
            nc.vector.tensor_copy(kT[:, :, :], work[parity][:, :].rearrange("p (f q) -> p f q", f=2)).then_inc(kT_done, 1)

        def add_out(n, tile_pair):
            dve.wait_ge(y_ps, n + 1)
            dve.wait_ge(y_added, n + 1)
            xs = x_all[:, bass.ds(tile_pair * TT, TT), :]
            nc.vector.tensor_tensor(xs, xs, y_bank[:, :].rearrange("p (t e) -> p t e", t=TT), ALU.add).then_inc(y_added, 1)

        def turn(n, parity, g, b, prepare, last):
            m, odd = n + 1, 1 - parity
            maxima(n, 0)
            maxima(n, 1)
            if not last:
                rope(m, odd, 0)
            maxima(n, 2)
            inverses(n, 0)
            inverses(n, 1)
            if not last:
                rope(m, odd, 1)
            maxima(n, 3)
            inverses(n, 2)
            inverses(n, 3)
            out_lo(n)
            probs_lo(n, 0)
            add_out(n, b + (g + KV_HEADS - 1) // KV_HEADS)
            if not last:
                copy_kT(m, odd)
            probs_lo(n, 1)
            if prepare:
                normalise(b * TT + TT, 0)
                normalise(b * TT + TT + 1, 1)
            probs_lo(n, 2)
            probs_lo(n, 3)
            if prepare:
                x_lo(b * TT + TT, 0)
                x_lo(b * TT + TT + 1, 1)

        dve.sem_inc(s_read, 2)
        dve.sem_inc(y_added, 1)
        dve.sem_inc(o_lo_done, 1)
        dve.sem_inc(pT_lo_done, 4)

        def layernorm_stats(a, b):
            for i in range(a, b):
                ins = nc.vector.bn_stats(stats[:, i, :], x_all[:, i + TT, :])
            wait_own(ins)
            for i in range(a, b):
                ins = nc.vector.bn_aggr(moments[:, i, :], stats[:, i, :])
            wait_own(ins)
            v, y, w = newton[:, 0, a:b], newton[:, 1, a:b], newton[:, 2, a:b]
            wait_own(nc.vector.tensor_scalar(v, moments[:, a:b, 1], EPS, None, ALU.add))
            wait_own(nc.vector.tensor_scalar(w.bitcast(I32), v.bitcast(I32), 1, None, ALU.logical_shift_right))
            wait_own(nc.vector.tensor_scalar(y.bitcast(I32), w.bitcast(I32), -1.0, RSQRT_MAGIC, ALU.mult, ALU.add))
            for i in range(4):
                wait_own(nc.vector.tensor_tensor(w, y, y, ALU.mult))
                wait_own(nc.vector.tensor_tensor(w, w, v, ALU.mult))
                wait_own(nc.vector.tensor_scalar(w, w, -0.5, 1.5, ALU.mult, ALU.add))
                wait_own(nc.vector.tensor_tensor(rstd[:, a:b] if i == 3 else y, y, w, ALU.mult))

        dve.wait_ge(x_first_in, 16)
        layernorm_stats(0, TT)
        normalise(0, 0, True)
        normalise(1, 1, True)
        x_lo(0, 0)
        x_lo(1, 1)
        for g in range(KV_HEADS):
            dve.wait_ge(w_hi_done, g + 1)
            nc.vector.tensor_tensor(w_lo[:, :, g * GW:(g + 1) * GW], w_raw[:, g % 2, :].rearrange("p (k n) -> p k n", k=KT),
                                    w_hi[:, :, g * GW:(g + 1) * GW].bitcast(F32), ALU.subtract).then_inc(w_split, 1)
            if g == 0:
                rope(0, 0, 0, True)
                rope(0, 0, 1, True)
                copy_kT(0, 0)
        for c in range(8):
            dve.wait_ge(wo_hi_done, c + 1)
            nc.vector.tensor_tensor(wo_lo[:, c * 512:(c + 1) * 512], w_raw[:, c % 2, 0:512],
                                    wo_hi[:, c * 512:(c + 1) * 512].bitcast(F32), ALU.subtract).then_inc(wo_split, 1)
        dve.wait_ge(x_rest_in, 16)
        layernorm_stats(TT, TILES)
        turns(dve, turn)
        out_lo(TURNS)
        add_out(TURNS, BATCH)

    @block.gpsimd
    def _(pool):
        def rotate(m, tt, first=False):
            pool.wait_ge(rope_parts, m * 2 + tt + 1)
            if not first:
                pool.wait_ge(stack_hi, m * 2 + tt - 1)
                pool.wait_ge(stack_lo, m * 2 + tt - 1)
            nc.gpsimd.tensor_tensor(rotated[:, tt, :], by_cos[:, tt, :], by_sin[:, tt, :], ALU.add).then_inc(rope_done, 1)

        def stack_low(m, tt):
            pool.wait_ge(stack_hi, m * 2 + tt + 1)
            pool.wait_ge(rope_done, m * 2 + tt + 1)
            pairs = stack[:, tt, 0:(GROUP + 1) * P].rearrange("p (h two d) -> p h two d", two=2, d=HD)
            nc.gpsimd.tensor_tensor(pairs[:, :, 0, :].bitcast(F32R), rotated[:, tt, :].rearrange("p (h d) -> p h d", d=HD),
                                    pairs[:, :, 1, :], ALU.subtract)
            k = GROUP * P
            nc.gpsimd.tensor_tensor(stack[:, tt, k + 2 * HD:k + 3 * HD].bitcast(F32R), rotated[:, tt, GROUP * HD:QK],
                                    stack[:, tt, k + HD:k + 2 * HD], ALU.subtract).then_inc(stack_lo, 1)

        def divide(n, h):
            s = h % 2
            pool.wait_ge(inv_done, n * GROUP + h + 1)
            pool.wait_ge(pT_ps, n * GROUP + h + 1)
            pool.sem_inc(pool_passed, 1)
            nc.gpsimd.tensor_scalar(probs[:, s, 0:P], exps[:, s, 0:P], inv_sums[:, s, 0:1], 1.0, ALU.mult, ALU.mult)
            nc.gpsimd.tensor_scalar(probs[:, s, P:3 * P], exps[:, s, P:3 * P], inv_sums[:, s, 1:2], 1.0,
                                    ALU.mult, ALU.mult).then_inc(probs_done, 1)

        def split_v(m, parity):
            hi, lo = v_hi[:, parity, :, HD:2 * HD], v_lo[:, parity, :, HD:2 * HD]
            pool.wait_ge(v_read, m * 2 + 2)
            pool.sem_inc(pool_passed, 1)
            nc.gpsimd.tensor_copy(hi, v_raw[:, :, :]).then_inc(v_hi_done, 1)
            pool.wait_ge(v_hi_done, m + 1)
            nc.gpsimd.tensor_tensor(lo, v_raw[:, :, :], hi.bitcast(F32), ALU.subtract).then_inc(v_done, 1)

        def turn(n, parity, g, b, prepare, last):
            m, odd = n + 1, 1 - parity
            if not last:
                rotate(m, 0)
            divide(n, 0)
            if not last:
                stack_low(m, 0)
            divide(n, 1)
            if not last:
                rotate(m, 1)
                stack_low(m, 1)
            divide(n, 2)
            divide(n, 3)
            if not last:
                pool.wait_ge(o_ps, n + 1)
                split_v(m, odd)

        pool.sem_inc(probs_done, 2)
        pool.sem_inc(pT_ps, 2)
        pool.sem_inc(v_done, 1)
        for z in (v_hi[:, :, :, :], v_lo[:, :, :, :], pT_hi[:, :, :], pT_lo[:, :, :], x_all[:, 0:TT, :]):
            ins = nc.gpsimd.memset(z.bitcast(F32), 0.0)
        ins.then_inc(zeroed, 1)
        pool.wait_ge(zeroed, 1)
        rotate(0, 0, True)
        stack_low(0, 0)
        rotate(0, 1, True)
        stack_low(0, 1)
        split_v(0, 0)
        turns(pool, turn)


def route(nc, ctx, t, x_all, r):

    def sb(name, shape, dt=F32):
        return ctx.enter_context(nc.sbuf_tensor(name, shape, dt))

    def sem(name):
        return ctx.enter_context(nc.semaphore(name))

    TE = TILES * EXPERTS
    consts = sb("route_tables", [P, 2 * P + TE + TILES * EXPERTS + (BLOCKS + 1) * EXPERTS])
    before, ones = consts[:, 0:P], consts[:, P:2 * P]
    rev = consts[:, 2 * P:2 * P + TE].rearrange("p (t e) -> p t e", e=EXPERTS)
    steps = consts[:, 2 * P + TE:2 * P + 2 * TE].rearrange("p (e t) -> p e t", e=EXPERTS)
    starts = consts[:, 2 * P + 2 * TE:].rearrange("p (b e) -> p b e", e=EXPERTS)
    ident = sb("route_ident", [P, P])
    gate = sb("gate_in", [P, KT, EXPERTS])
    zeros = sb("zeros", [P, EMB])

    stats = sb("stats2", [P, TILES, 6])
    moments = sb("moments2", [P, TILES, 2])
    rstd = sb("rstd2", [P, TILES])
    newton = sb("newton2", [P, 2, TILES])
    xn = sb("xn2", [P, TILES, EMB])
    xT = sb("xT2", [P, 2, KT * P])
    logits = sb("logits", [P, TILES, EXPERTS])
    others = sb("others", [P, TILES, EXPERTS])
    equal = sb("equal", [P, TILES, EXPERTS])
    hot = [sb("hot1", [P, TILES, EXPERTS]), sb("hot2", [P, TILES, EXPERTS])]
    both = sb("both", [P, TILES, EXPERTS])
    best = sb("best", [P, 2, TILES])
    code = sb("code", [P, TILES])
    gap = sb("gap", [P, TILES])
    counts = sb("counts", [P, 2, TILES, EXPERTS])
    full = sb("full", [P, EXPERTS, TILES])
    blocks = sb("blocks", [P, EXPERTS])
    first_block = sb("first_block", [P, EXPERTS + 1])
    place = sb("place", [P, TILES, EXPERTS])
    chosen = sb("chosen", [P, TILES, EXPERTS])
    row = sb("row", [P, 2, TILES])
    later = sb("later", [P, BLOCKS + 1, EXPERTS])
    owner = sb("owner", [P, BLOCKS + 1])

    tr_bank = [ctx.enter_context(nc.psum_tensor(f"tr{i}", [P, 512], F32)) for i in range(2)]
    logit_bank = ctx.enter_context(nc.psum_tensor("logit_bank", [P, 512], F32))
    rank_bank = ctx.enter_context(nc.psum_tensor("rank_bank", [P, 512], F32))

    consts_in = sem("route_consts_in")
    zero_set = sem("zero_set")
    cleared = sem("cleared")
    step = sem("route_step")
    xn_done = sem("xn2_done")
    xT_ps = sem("xT2_ps")
    xT_done = sem("xT2_done")
    logits_ps = sem("logits_ps")
    both_done = sem("both_done")
    ranks_ps = sem("ranks_ps")
    gap_done = sem("gap_done")
    exp_done = sem("gap_exp_done")
    rows_done = sem("rows_done")
    scattered = sem("scattered")

    block = ctx.enter_context(nc.Block())

    @block.sync
    def _(sp):
        sp.dma_start(consts[:, :], t["route_consts"]).then_inc(consts_in, 16)
        sp.dma_start(ident[:, :], t["attn_consts"][:, 2 * TT * HD + 2 * P:]).then_inc(consts_in, 16)
        sp.dma_start(gate[:, :, :], t["gate"].rearrange("p (k e) -> p k e", k=KT)).then_inc(consts_in, 16)
        sp.wait_ge(zero_set, 1)
        src = zeros[:, :].rearrange("p (o e) -> p o e", o=1).to_broadcast([P, BLOCKS, EMB])
        sp.dma_start(t["x_sorted"].rearrange("(b p) e -> p b e", p=P), src).then_inc(cleared, 16)
        sp.wait_ge(cleared, 16)

    @block.gpsimd
    def _(pool):
        nc.gpsimd.memset(zeros[:, :], 0.0).then_inc(zero_set, 1)
        pool.wait_ge(cleared, 16)
        pool.wait_ge(rows_done, 1)
        for tile in range(TILES):
            for c in range(2):
                pool.indirect_dma_start(
                    out=t["x_sorted"], out_offset=bass.IndirectOffsetOnAxis(ap=r["rows"][:, c, tile:tile + 1], axis=0),
                    in_=xn[:, tile, :], in_offset=None).then_inc(scattered, 16)
        pool.wait_ge(scattered, 16 * 2 * TILES)

    @block.tensor
    def _(pe):
        def transposes(i):
            pe.wait_ge(xn_done, i + 1)
            if i >= 2:
                pe.wait_ge(xT_done, i - 1)
            for k in range(KT):
                mm = nc.tensor.transpose(tr_bank[i % 2][:, k * P:(k + 1) * P], xn[:, i, k * P:(k + 1) * P], ident[:, :])
            mm.then_inc(xT_ps, 1)

        def gate_logits(i):
            pe.wait_ge(xT_done, i + 1)
            for k in range(KT):
                mm = nc.tensor.matmul(logit_bank[:, i * EXPERTS:(i + 1) * EXPERTS], xT[:, i % 2, k * P:(k + 1) * P],
                                      gate[:, k, :], start=(k == 0), stop=(k == KT - 1))
            mm.then_inc(logits_ps, 1)

        pe.wait_ge(consts_in, 48)
        for i in range(TILES + 1):
            if i < TILES:
                transposes(i)
            if i >= 1:
                gate_logits(i - 1)
        pe.wait_ge(both_done, 1)
        m = both[:, :, :].rearrange("p t e -> p (t e)")
        nc.tensor.matmul(rank_bank[:, 0:TE], before, m, start=True, stop=True)
        nc.tensor.matmul(rank_bank[:, TE:2 * TE], ones, m, start=True, stop=True).then_inc(ranks_ps, 1)

    @block.scalar
    def _(act):
        for i in range(TILES):
            act.wait_ge(xT_ps, i + 1)
            if i >= 2:
                act.wait_ge(logits_ps, i - 1)
            nc.scalar.copy(xT[:, i % 2, :], tr_bank[i % 2][:, 0:KT * P]).then_inc(xT_done, 1)
        act.wait_ge(gap_done, 1)
        nc.scalar.activation(gap[:, :], gap[:, :], ACT.Exp).then_inc(exp_done, 1)

    @block.vector
    def _(dve):
        chain = [0]

        def wait_own(ins):
            chain[0] += 1
            ins.then_inc(step, 1)
            dve.wait_ge(step, chain[0])

        for i in range(TILES):
            ins = nc.vector.bn_stats(stats[:, i, :], x_all[:, i + TT, :])
        wait_own(ins)
        for i in range(TILES):
            ins = nc.vector.bn_aggr(moments[:, i, :], stats[:, i, :])
        wait_own(ins)
        v, y, w = newton[:, 0, :], rstd[:, :], newton[:, 1, :]
        wait_own(nc.vector.tensor_scalar(v, moments[:, :, 1], EPS, None, ALU.add))
        wait_own(nc.vector.tensor_scalar(w.bitcast(I32), v.bitcast(I32), 1, None, ALU.logical_shift_right))
        wait_own(nc.vector.tensor_scalar(y.bitcast(I32), w.bitcast(I32), -1.0, RSQRT_MAGIC, ALU.mult, ALU.add))
        for i in range(4):
            wait_own(nc.vector.tensor_tensor(w, y, y, ALU.mult))
            wait_own(nc.vector.tensor_tensor(w, w, v, ALU.mult))
            wait_own(nc.vector.tensor_scalar(w, w, -0.5, 1.5, ALU.mult, ALU.add))
            wait_own(nc.vector.tensor_tensor(y, y, w, ALU.mult))
        for i in range(TILES):
            nc.vector.tensor_scalar(xn[:, i, :], x_all[:, i + TT, :], moments[:, i, 0:1], rstd[:, i:i + 1],
                                    ALU.subtract, ALU.mult).then_inc(xn_done, 1)

        def over_experts(a):
            return a.rearrange("p (t o) -> p t o", o=1).to_broadcast([P, TILES, EXPERTS])

        def choose(c, scores):
            wait_own(nc.vector.tensor_reduce(best[:, c, :], scores, AX.X, ALU.max))
            wait_own(nc.vector.tensor_tensor(equal[:, :, :], scores, over_experts(best[:, c, :]), ALU.is_equal))
            wait_own(nc.vector.tensor_tensor(equal[:, :, :], equal[:, :, :], rev, ALU.mult))
            wait_own(nc.vector.tensor_reduce(code[:, :], equal[:, :, :], AX.X, ALU.max))
            wait_own(nc.vector.tensor_tensor(hot[c][:, :, :], rev, over_experts(code[:, :]), ALU.is_equal))

        dve.wait_ge(logits_ps, TILES)
        wait_own(nc.vector.tensor_copy(logits[:, :, :], logit_bank[:, 0:TE].rearrange("p (t e) -> p t e", e=EXPERTS)))
        dve.wait_ge(consts_in, 48)
        choose(0, logits[:, :, :])
        wait_own(nc.vector.scalar_tensor_tensor(out=others[:, :, :], in0=hot[0][:, :, :], scalar=-3e38,
                                                in1=logits[:, :, :], op0=ALU.mult, op1=ALU.add))
        choose(1, others[:, :, :])
        nc.vector.tensor_tensor(both[:, :, :], hot[0][:, :, :], hot[1][:, :, :], ALU.add).then_inc(both_done, 1)
        nc.vector.tensor_tensor(gap[:, :], best[:, 1, :], best[:, 0, :], ALU.subtract).then_inc(gap_done, 1)
        dve.wait_ge(exp_done, 1)
        wait_own(nc.vector.tensor_scalar(code[:, :], gap[:, :], 1.0, None, ALU.add))
        wait_own(nc.vector.reciprocal(r["weights"][:, 0, :], code[:, :]))
        nc.vector.tensor_tensor(r["weights"][:, 1, :], gap[:, :], r["weights"][:, 0, :], ALU.mult)

        dve.wait_ge(ranks_ps, 1)
        total = rank_bank[:, TE:2 * TE].rearrange("p (t e) -> p t e", e=EXPERTS)
        wait_own(nc.vector.tensor_copy(counts[:, 0, :, :], total))
        side = 0
        for s in (1, 2, 4, 8):
            wait_own(nc.vector.tensor_copy(counts[:, 1 - side, 0:s, :], counts[:, side, 0:s, :]))
            wait_own(nc.vector.tensor_tensor(counts[:, 1 - side, s:TILES, :], counts[:, side, s:TILES, :],
                                             counts[:, side, 0:TILES - s, :], ALU.add))
            side = 1 - side
        all_counts = counts[:, side, TILES - 1, :].rearrange("p (e o) -> p e o", o=1).to_broadcast([P, EXPERTS, TILES])
        wait_own(nc.vector.tensor_tensor(full[:, :, :], all_counts, steps, ALU.is_gt))
        wait_own(nc.vector.tensor_reduce(blocks[:, :], full[:, :, :], AX.X, ALU.add))
        wait_own(nc.vector.memset(first_block[:, 0:1], 0.0))
        for e in range(EXPERTS):
            wait_own(nc.vector.tensor_tensor(first_block[:, e + 1:e + 2], first_block[:, e:e + 1], blocks[:, e:e + 1], ALU.add))
        wait_own(nc.vector.tensor_scalar(first_block[:, :], first_block[:, :], float(P), None, ALU.mult))
        earlier = counts[:, 1 - side, :, :]
        wait_own(nc.vector.tensor_tensor(earlier, counts[:, side, :, :], total, ALU.subtract))
        firsts = first_block[:, 0:EXPERTS].rearrange("p (o e) -> p o e", o=1).to_broadcast([P, TILES, EXPERTS])
        wait_own(nc.vector.tensor_tensor(place[:, :, :], earlier, firsts, ALU.add))
        wait_own(nc.vector.tensor_tensor(place[:, :, :], place[:, :, :],
                                         rank_bank[:, 0:TE].rearrange("p (t e) -> p t e", e=EXPERTS), ALU.add))
        for c in range(2):
            wait_own(nc.vector.tensor_tensor(chosen[:, :, :], hot[c][:, :, :], place[:, :, :], ALU.mult))
            wait_own(nc.vector.tensor_reduce(row[:, c, :], chosen[:, :, :], AX.X, ALU.add))
        nc.vector.tensor_copy(r["rows"][:, :, :], row[:, :, :]).then_inc(rows_done, 1)
        bounds = first_block[:, 0:EXPERTS].rearrange("p (o e) -> p o e", o=1).to_broadcast([P, BLOCKS + 1, EXPERTS])
        wait_own(nc.vector.tensor_tensor(later[:, :, :], starts, bounds, ALU.is_ge))
        wait_own(nc.vector.tensor_reduce(owner[:, :], later[:, :, :], AX.X, ALU.add))
        wait_own(nc.vector.tensor_scalar(r["owners"][:, :], owner[:, :], -1.0, None, ALU.add))


def experts(nc, ctx, t, x_all, r):

    def sb(name, shape, dt=F32):
        return ctx.enter_context(nc.sbuf_tensor(name, shape, dt))

    def sem(name):
        return ctx.enter_context(nc.semaphore(name))

    WI, WO = 2 * KT * MLP, MT * EMB
    w_in = sb("w_in_all", [P, EXPERTS * WI])
    w_out = sb("w_out_all", [P, EXPERTS * WO])
    ident = sb("experts_ident", [P, P])
    xs = sb("xs", [P, 2, EMB])
    xT = sb("xsT", [P, 2, KT * P])
    act_h = sb("act_h", [P, MLP])
    gated = sb("gated", [P, MLP])
    gT = sb("gT", [P, MT * P])
    y = sb("y", [P, 2, EMB])
    ya = sb("ya", [P, 2, TILES, EMB])

    def bank(name):
        return ctx.enter_context(nc.psum_tensor(name, [P, 512], F32))

    tx, h0, h1, tg, yb = bank("tx"), bank("h0"), bank("h1"), bank("tg"), bank("yb")

    weights_in = sem("weights_in")
    xs_in = [sem("xs_in0"), sem("xs_in1")]
    xT_ps = sem("xsT_ps")
    xT_done = sem("xsT_done")
    h0_ps = sem("h0_ps")
    h1_ps = sem("h1_ps")
    silu_done = sem("silu_done")
    gated_done = sem("gated_done")
    gT_ps = sem("gT_ps")
    gT_done = sem("gT_done")
    yb_ps = sem("yb_ps")
    y_done = sem("y_done")
    y_out = [sem("y_out0"), sem("y_out1")]
    gathered = [sem(f"gathered{i}") for i in range(TILES)]
    weighed = sem("weighed")
    summed = sem("summed")
    stored = sem("stored")

    block = ctx.enter_context(nc.Block())
    x_sorted = t["x_sorted"].rearrange("(b p) e -> b p e", p=P)
    y_sorted = t["y_sorted"].rearrange("(b p) e -> b p e", p=P)

    @block.sync
    def _(sp):
        def load(j, p):
            sp.dma_start(xs[:, p, :], x_sorted[bass.ds(j, 1), :, :].rearrange("o p e -> (o p) e")).then_inc(xs_in[p], 16)

        load(0, 0)
        sp.dma_start(ident[:, :], t["attn_consts"][:, 2 * TT * HD + 2 * P:]).then_inc(weights_in, 16)
        for e in range(EXPERTS):
            sp.dma_start(w_in[:, e * WI:(e + 1) * WI], t["w_in"][:, e * WI:(e + 1) * WI]).then_inc(weights_in, 16)
        sp.dma_start(w_out[:, :], t["w_out"]).then_inc(weights_in, 16)

        load(1, 1)
        with sp.Fori(0, (BLOCKS - 3) // 2) as i:
            sp.wait_ge(xT_ps, i * 2 + 1)
            load(i * 2 + 2, 0)
            sp.wait_ge(xT_ps, i * 2 + 2)
            load(i * 2 + 3, 1)
        sp.wait_ge(xT_ps, BLOCKS - 2)
        load(BLOCKS - 1, 0)
        for i in range(TILES):
            sp.wait_ge(summed, i + 1)
            sp.dma_start(t["out"].rearrange("b (t p) e -> (b t) p e", p=P)[i], x_all[:, i + TT, :]).then_inc(stored, 16)
        sp.wait_ge(stored, 16 * TILES)

    @block.tensor
    def _(pe):
        def x_transposes(j, p, first=False):
            pe.wait_ge(xs_in[p], (j - p) * 8 + 16)
            if not first:
                pe.wait_ge(xT_done, j)
            for k in range(KT):
                mm = nc.tensor.transpose(tx[:, k * P:(k + 1) * P], xs[:, p, k * P:(k + 1) * P], ident[:, :])
            mm.then_inc(xT_ps, 1)

        def hidden(j, p, expert, which):
            ps, done = ((h0, h0_ps), (h1, h1_ps))[which]
            for k in range(KT):
                mm = nc.tensor.matmul(ps[:, :], xT[:, p, k * P:(k + 1) * P],
                                      w_in[:, bass.ds(expert * WI + (which * KT + k) * MLP, MLP)],
                                      start=(k == 0), stop=(k == KT - 1))
            mm.then_inc(done, 1)

        def g_transposes(j):
            pe.wait_ge(gated_done, j + 1)
            for k in range(MT):
                mm = nc.tensor.transpose(tg[:, k * P:(k + 1) * P], gated[:, k * P:(k + 1) * P], ident[:, :])
            mm.then_inc(gT_ps, 1)

        def output(j, expert, first=False):
            pe.wait_ge(gT_done, j + 1)
            if not first:
                pe.wait_ge(y_done, j)
            for k in range(MT):
                mm = nc.tensor.matmul(yb[:, 0:EMB], gT[:, k * P:(k + 1) * P], w_out[:, bass.ds(expert * WO + k * EMB, EMB)],
                                      start=(k == 0), stop=(k == MT - 1))
            mm.then_inc(yb_ps, 1)

        def owner(j):
            return pe.value_load(r["owners"][0:1, bass.ds(j, 1)], min_val=0, max_val=EXPERTS - 1)

        def turn(j, p, last=False):
            expert, last_expert = owner(j), owner(j - 1)
            pe.wait_ge(xT_done, j + 1)
            pe.wait_ge(gated_done, j)
            hidden(j, p, expert, 0)
            g_transposes(j - 1)
            hidden(j, p, expert, 1)
            if not last:
                x_transposes(j + 1, 1 - p)
            output(j - 1, last_expert)

        pe.wait_ge(weights_in, 16 * (EXPERTS + 2))
        x_transposes(0, 0, True)

        expert = owner(0)
        pe.wait_ge(xT_done, 1)
        hidden(0, 0, expert, 0)
        hidden(0, 0, expert, 1)
        x_transposes(1, 1)
        with pe.Fori(0, (BLOCKS - 3) // 2) as i:
            turn(i * 2 + 1, 1)
            turn(i * 2 + 2, 0)
        turn(BLOCKS - 2, 1)
        turn(BLOCKS - 1, 0, last=True)
        g_transposes(BLOCKS - 1)
        output(BLOCKS - 1, owner(BLOCKS - 1))

    @block.scalar
    def _(act):
        def x_copy(j, p):
            act.wait_ge(xT_ps, j + 1)
            nc.scalar.copy(xT[:, p, :], tx[:, 0:KT * P]).then_inc(xT_done, 1)

        def silu(j):
            act.wait_ge(h0_ps, j + 1)
            nc.scalar.activation(act_h[:, :], h0[:, :], SILU).then_inc(silu_done, 1)

        def g_copy(j):
            act.wait_ge(gT_ps, j + 1)
            nc.scalar.copy(gT[:, :], tg[:, :]).then_inc(gT_done, 1)

        def turn(j, p, last=False):
            act.wait_ge(gated_done, j)
            silu(j)
            g_copy(j - 1)
            if not last:
                x_copy(j + 1, 1 - p)

        x_copy(0, 0)
        silu(0)
        x_copy(1, 1)
        with act.Fori(0, (BLOCKS - 3) // 2) as i:
            turn(i * 2 + 1, 1)
            turn(i * 2 + 2, 0)
        turn(BLOCKS - 2, 1)
        turn(BLOCKS - 1, 0, last=True)
        g_copy(BLOCKS - 1)

    @block.vector
    def _(dve):
        def gate_rows(j, first=False):
            dve.wait_ge(silu_done, j + 1)
            dve.wait_ge(h1_ps, j + 1)
            if not first:
                dve.wait_ge(gT_ps, j)
            nc.vector.tensor_tensor(gated[:, :], h1[:, :], act_h[:, :], ALU.mult).then_inc(gated_done, 1)

        def y_copy(j, p, fresh=False):
            dve.wait_ge(yb_ps, j + 1)
            if not fresh:
                dve.wait_ge(y_out[p], (j - p) * 8)
            nc.vector.tensor_copy(y[:, p, :], yb[:, 0:EMB]).then_inc(y_done, 1)

        gate_rows(0, True)
        gate_rows(1)
        y_copy(0, 0, True)
        gate_rows(2)
        y_copy(1, 1, True)
        with dve.Fori(0, (BLOCKS - 3) // 2) as i:
            gate_rows(i * 2 + 3)
            y_copy(i * 2 + 2, 0)
            gate_rows(i * 2 + 4)
            y_copy(i * 2 + 3, 1)
        y_copy(BLOCKS - 1, 0)
        for i in range(TILES):
            xt = x_all[:, i + TT, :]
            dve.wait_ge(gathered[i], 32)
            nc.vector.scalar_tensor_tensor(out=xt, in0=ya[:, 0, i, :], scalar=r["weights"][:, 0, i:i + 1], in1=xt,
                                           op0=ALU.mult, op1=ALU.add).then_inc(weighed, 1)
            dve.wait_ge(weighed, i + 1)
            nc.vector.scalar_tensor_tensor(out=xt, in0=ya[:, 1, i, :], scalar=r["weights"][:, 1, i:i + 1], in1=xt,
                                           op0=ALU.mult, op1=ALU.add).then_inc(summed, 1)

    @block.gpsimd
    def _(pool):
        def store(j, p):
            pool.wait_ge(y_done, j + 1)
            pool.dma_start(y_sorted[bass.ds(j, 1), :, :].rearrange("o p e -> (o p) e"), y[:, p, :]).then_inc(y_out[p], 16)

        store(0, 0)
        with pool.Fori(0, (BLOCKS - 1) // 2) as i:
            store(i * 2 + 1, 1)
            store(i * 2 + 2, 0)
        pool.wait_ge(y_out[0], 16 * ((BLOCKS + 1) // 2))
        pool.wait_ge(y_out[1], 16 * (BLOCKS // 2))
        for i in range(TILES):
            for c in range(2):
                pool.indirect_dma_start(
                    out=ya[:, c, i, :], out_offset=None, in_=t["y_sorted"],
                    in_offset=bass.IndirectOffsetOnAxis(ap=r["rows"][:, c, i:i + 1], axis=0)).then_inc(gathered[i], 16)


def program(nc, t):
    t = dict(t)
    t["x_sorted"] = nc.dram_tensor("x_sorted", [ROWS, EMB], F32).ap()
    t["y_sorted"] = nc.dram_tensor("y_sorted", [ROWS, EMB], F32).ap()
    with ExitStack() as outer:
        x_all = outer.enter_context(nc.sbuf_tensor("x_all", [P, TT + TILES, EMB], F32))
        r = {
            "rows": outer.enter_context(nc.sbuf_tensor("rows", [P, 2, TILES], U32)),
            "weights": outer.enter_context(nc.sbuf_tensor("weights", [P, 2, TILES], F32)),
            "owners": outer.enter_context(nc.sbuf_tensor("owners", [P, BLOCKS + 1], I32)),
        }
        with ExitStack() as ctx:
            attention(nc, ctx, t, x_all)
        with ExitStack() as ctx:
            route(nc, ctx, t, x_all, r)
        with ExitStack() as ctx:
            experts(nc, ctx, t, x_all, r)


def laid_out(x, wq, wk, wv, wo, gate, w0, w1, w2):
    wqT = wq.T.reshape(KT, P, KV_HEADS, GROUP * HD)
    wkT = wk.T.reshape(KT, P, KV_HEADS, HD)
    wvT = wv.T.reshape(KT, P, KV_HEADS, HD)
    w_qkv = np.concatenate([wqT, wkT, wvT], 3).transpose(1, 2, 0, 3).reshape(P, KV_HEADS, KT * GW)
    wo_t = wo.T.reshape(HEADS // 2, P, EMB).transpose(1, 0, 2).reshape(P, HEADS // 2 * EMB)
    attn, route = shape_constants()
    return {
        "x": x, "w_qkv": w_qkv, "wo": wo_t, "attn_consts": attn, "route_consts": route,
        "gate": gate.reshape(KT, P, EXPERTS).transpose(1, 0, 2).reshape(P, KT * EXPERTS),
        "w_in": np.concatenate([w0.reshape(EXPERTS, KT, P, MLP), w1.reshape(EXPERTS, KT, P, MLP)], 1)
        .transpose(2, 0, 1, 3).reshape(P, EXPERTS * 2 * KT * MLP),
        "w_out": w2.reshape(EXPERTS, MT, P, EMB).transpose(2, 0, 1, 3).reshape(P, EXPERTS * MT * EMB),
    }


def kernel(L0_attn_hidden_states, L0_attn_wq, L0_attn_wk, L0_attn_wv, L0_attn_wo, L0_attn_wq_s, L0_attn_wk_s,
           L0_attn_wv_s, L0_attn_wo_s, L0_ffn_gate_kernel, L0_ffn_w0_kernel, L0_ffn_w1_kernel, L0_ffn_wo_kernel):
    import concourse.bacc as bacc
    from concourse.bass_utils import run_bass_kernel_spmd

    arrays = laid_out(L0_attn_hidden_states, L0_attn_wq, L0_attn_wk, L0_attn_wv, L0_attn_wo,
                      L0_ffn_gate_kernel, L0_ffn_w0_kernel, L0_ffn_w1_kernel, L0_ffn_wo_kernel)
    arrays = {name: np.ascontiguousarray(a) for name, a in arrays.items()}
    nc = bacc.Bacc("TRN2", target_bir_lowering=False, num_devices=1)
    t = {name: nc.dram_tensor(name, a.shape, mybir.dt.from_np(a.dtype), kind="ExternalInput").ap()
         for name, a in arrays.items()}
    t["out"] = nc.dram_tensor("out", (BATCH, SEQ, EMB), F32, kind="ExternalOutput").ap()
    program(nc, t)
    return run_bass_kernel_spmd(nc, [arrays], core_ids=[0]).results[0]["out"]
```

```python
from contextlib import ExitStack

import numpy as np

import concourse.bass as bass
import concourse.mybir as mybir

F32 = mybir.dt.float32
F32R = mybir.dt.float32r
BF16 = mybir.dt.bfloat16
I32 = mybir.dt.int32
U32 = mybir.dt.uint32
ALU = mybir.AluOpType
ACT = mybir.ActivationFunctionType
AX = mybir.AxisListType

P = 128
BATCH, SEQ, EMB = 8, 256, 256
HEADS, KV_HEADS, HD = 32, 8, 64
GROUP = HEADS // KV_HEADS
KT = EMB // P
TT = SEQ // P
TILES = BATCH * TT
TOKENS = BATCH * SEQ
QK = (GROUP + 1) * HD
GW = QK + HD
PAIRS = GROUP // 2
THETA = 500000.0
EPS = 1e-5
MASKED = -1e30
STACK = GROUP * P + 3 * HD

EXPERTS, MLP = 8, 512
MT = MLP // P
BLOCKS = TOKENS * 2 // P + EXPERTS - 1
PAIRS_ALL = 2 * TOKENS
RSQRT_MAGIC = 1597463007.0
SILU = ACT.Silu
RING = 3
WI, WO = 2 * KT * MLP, MT * EMB
PIECES = 2 * EXPERTS
PIECE = EXPERTS * WI // PIECES
RAW = 3


def shape_constants():
    inv = (np.float32(1.0) / np.power(np.float32(THETA), np.arange(0, HD, 2, dtype=np.float32) / np.float32(HD))).astype(np.float32)
    ang = np.arange(SEQ, dtype=np.float32)[:, None] * inv[None, :]
    cos, sin = np.cos(ang).astype(np.float32), np.sin(ang).astype(np.float32)
    cos2 = np.concatenate([cos, cos], 1).reshape(TT, P, HD).transpose(1, 0, 2)
    sin2 = np.concatenate([-sin, sin], 1).reshape(TT, P, HD).transpose(1, 0, 2)
    q, k = np.arange(P)[:, None], np.arange(P)[None, :]
    mask = np.concatenate([np.zeros((P, P)), np.where(k > q, MASKED, 0.0)], 1).astype(np.float32)
    ident = np.eye(P, dtype=np.float32)
    before = (q < k).astype(np.float32)
    ones = np.ones((P, P), np.float32)
    attn = np.concatenate([cos2.reshape(P, -1), sin2.reshape(P, -1), mask, ident], 1)
    rev = np.tile(EXPERTS - np.arange(EXPERTS, dtype=np.float32), TILES)
    steps = np.tile(P * np.arange(TILES, dtype=np.float32), EXPERTS)
    starts = np.repeat(P * np.arange(BLOCKS + 1, dtype=np.float32), EXPERTS)
    lanes = np.arange(P, dtype=np.float32)
    groups = np.arange(1, 2 * TILES + 1, dtype=np.float32)
    route = np.concatenate([before, ones, np.tile(np.concatenate([rev, steps, starts]), (P, 1)),
                            np.tile(np.concatenate([lanes, groups]), (P, 1)), lanes[:, None]], 1)
    return np.ascontiguousarray(attn, np.float32), np.ascontiguousarray(route, np.float32)


def attention(nc, ctx, t, x_all, r=None):

    def sb(name, shape, dt=F32):
        return ctx.enter_context(nc.sbuf_tensor(name, shape, dt))

    def sem(name):
        return ctx.enter_context(nc.semaphore(name))

    tables = sb("tables", [P, 2 * TT * HD + 3 * P])
    cos = tables[:, 0:TT * HD].rearrange("p (t d) -> p t d", t=TT)
    sin = tables[:, TT * HD:2 * TT * HD].rearrange("p (t d) -> p t d", t=TT)
    mask = tables[:, 2 * TT * HD:2 * TT * HD + 2 * P]
    ident = tables[:, 2 * TT * HD + 2 * P:2 * TT * HD + 3 * P]

    w_raw = sb("w_raw", [P, 2, KT * GW])
    wo_raw = sb("wo_raw", [P, 2, PAIRS * EMB])
    w_hi = sb("w_hi", [P, KT, KV_HEADS * GW], F32R)
    w_lo = sb("w_lo", [P, KT, KV_HEADS * GW], F32R)
    wo_hi = sb("wo_hi", [P, HEADS // 2 * EMB], F32R)
    wo_lo = sb("wo_lo", [P, HEADS // 2 * EMB], F32R)

    stats = sb("stats", [P, TILES, 6])
    moments = sb("moments", [P, TILES, 2])
    rstd = sb("rstd", [P, TILES])
    newton = sb("newton", [P, 3, TILES])
    xn = sb("xn", [P, TT, EMB])
    xT_hi = sb("xT_hi", [P, KT, SEQ], F32R)
    xT_lo = sb("xT_lo", [P, KT, SEQ], F32R)

    by_cos = sb("by_cos", [P, TT, QK])
    by_sin = sb("by_sin", [P, TT, QK])
    rotated = sb("rotated", [P, TT, QK])
    stack = sb("stack", [P, TT, STACK])
    v_raw = sb("v_raw", [P, TT, HD])
    v_hi = sb("v_hi", [P, 2, TT, 3 * HD], F32R)
    v_lo = sb("v_lo", [P, 2, TT, 3 * HD], F32R)
    qT = sb("qT", [P, TT, GROUP * P], F32R)
    kT = sb("kT", [P, 2, SEQ], F32R)
    masked = sb("masked", [P, 2, 3 * P])
    neg_max = sb("neg_max", [P, 2, TT])
    exps = sb("exps", [P, 2, 3 * P])
    sums = sb("sums", [P, 2, TT])
    inv_sums = sb("inv_sums", [P, 2, TT])
    probs = sb("probs", [P, GROUP, 3 * P])
    pT_hi = sb("pT_hi", [P, GROUP, 3 * P], F32R)
    pT_lo = sb("pT_lo", [P, GROUP, 3 * P], F32R)
    oT_hi = sb("oT_hi", [P, PAIRS, SEQ], F32R)
    oT_lo = sb("oT_lo", [P, PAIRS, SEQ], F32R)

    def bank(name):
        return ctx.enter_context(nc.psum_tensor(name, [P, 512], F32))

    work = [bank("work0"), bank("work1")]
    s_bank = [bank("scores0"), bank("scores1")]
    p_bank = [bank("probsT0"), bank("probsT1")]
    o_bank = bank("heads_out")
    y_bank = bank("attn_out")

    consts_in = sem("consts_in")
    x_first_in = sem("x_first_in")
    x_rest_in = sem("x_rest_in")
    w_in = [sem("w_in0"), sem("w_in1")]
    w_split = sem("w_split")
    w_hi_done = sem("w_hi_done")
    wo_in = [sem("wo_in0"), sem("wo_in1")]
    wo_hi_done = sem("wo_hi_done")
    wo_split = sem("wo_split")
    zeroed = sem("zeroed")
    step = sem("step")
    dve_passed = sem("dve_passed")
    pool_passed = sem("pool_passed")
    xn_done = sem("xn_done")
    xT_ps = sem("xT_ps")
    xT_hi_done = sem("xT_hi_done")
    xT_lo_done = sem("xT_lo_done")
    proj_ps = sem("proj_ps")
    v_read = sem("v_read")
    v_hi_done = sem("v_hi_done")
    v_done = sem("v_done")
    rope_parts = sem("rope_parts")
    rope_done = sem("rope_done")
    stack_hi = sem("stack_hi")
    stack_lo = sem("stack_lo")
    qT_ps = sem("qT_ps")
    qT_done = sem("qT_done")
    kT_ps = sem("kT_ps")
    kT_done = sem("kT_done")
    s_ps = sem("s_ps")
    s_read = sem("s_read")
    exp_done = sem("exp_done")
    inv_done = sem("inv_done")
    probs_done = sem("probs_done")
    pT_ps = sem("pT_ps")
    pT_hi_done = sem("pT_hi_done")
    pT_lo_done = sem("pT_lo_done")
    o_ps = sem("o_ps")
    o_hi_done = sem("o_hi_done")
    o_lo_done = sem("o_lo_done")
    y_ps = sem("y_ps")
    y_added = sem("y_added")


    GO = PAIRS * EMB
    TURNS = BATCH * KV_HEADS

    def past(n, k):
        return not isinstance(n, int) or n >= k

    def turns(eng, turn):
        def pair(b, i, prepare, last):
            turn(b * KV_HEADS + i * 2, 0, i * 2, b, prepare, False)
            turn(b * KV_HEADS + i * 2 + 1, 1, i * 2 + 1, b, False, last)

        def rounds(b, last_batch):
            with eng.Fori(0, KV_HEADS // 2 - 1) as i:
                pair(b, i, False, False)
            pair(b, KV_HEADS // 2 - 1, not last_batch, last_batch)
        pair(0, 0, False, False)
        with eng.Fori(1, KV_HEADS // 2 - 1) as i:
            pair(0, i, False, False)
        pair(0, KV_HEADS // 2 - 1, True, False)
        with eng.Fori(1, BATCH - 1) as b:
            rounds(b, False)
        rounds(BATCH - 1, True)

    block = ctx.enter_context(nc.Block())

    @block.sync
    def _(sp):
        sp.dma_start(tables[:, :], t["attn_consts"]).then_inc(consts_in, 16)
        x_dram = t["x"].rearrange("b (t p) e -> p (b t) e", p=P)
        sp.dma_start(x_all[:, 0:TT, :], x_dram[:, 0:TT, :]).then_inc(x_first_in, 16)
        for g in range(KV_HEADS):
            if g >= 2:
                sp.wait_ge(w_split, g - 1)
            sp.dma_start(w_raw[:, g % 2, :], t["w_qkv"][:, g, :]).then_inc(w_in[g % 2], 16)
            if g == 0:
                sp.dma_start(x_all[:, TT:TILES, :], x_dram[:, TT:TILES, :]).then_inc(x_rest_in, 16)
            if g >= 2:
                sp.wait_ge(wo_split, g - 1)
            sp.dma_start(wo_raw[:, g % 2, :], t["wo"][:, g * GO:(g + 1) * GO]).then_inc(wo_in[g % 2], 16)

    @block.tensor
    def _(pe):
        def x_transposes(first_tile):
            for tt in range(TT):
                pe.wait_ge(xn_done, first_tile + tt + 1)
                for k in range(KT):
                    mm = nc.tensor.transpose(work[tt][:, k * P:(k + 1) * P], xn[:, tt, k * P:(k + 1) * P], ident)
                mm.then_inc(xT_ps, 1)

        def project(m, parity, g, tt):
            ps = work[(tt + parity) % 2]
            n = 0
            for k in range(KT):
                for a, w in ((xT_hi, w_hi), (xT_lo, w_hi), (xT_hi, w_lo)):
                    mm = nc.tensor.matmul(ps[:, 0:GW], a[:, k, tt * P:(tt + 1) * P], w[:, k, bass.ds(g * GW, GW)],
                                          start=(n == 0), stop=(n == 3 * KT - 1))
                    n += 1
            mm.then_inc(proj_ps, 1)

        def q_transposes(m, parity, tt):
            ps = work[(tt + parity) % 2]
            pe.wait_ge(stack_hi, m * 2 + tt + 1)
            pe.wait_ge(stack_lo, m * 2 + tt + 1)
            for h in range(GROUP):
                mm = nc.tensor.transpose(ps[:, h * P:(h + 1) * P], stack[:, tt, h * P:(h + 1) * P], ident)
            mm.then_inc(qT_ps, 1)

        def k_transposes(m, parity):
            ps = work[parity]
            pe.wait_ge(qT_done, m * 2 + 1)
            for form in range(2):
                at = GROUP * P + form * HD
                for tt in range(TT):
                    mm = nc.tensor.transpose(ps[:, (form * TT + tt) * P:(form * TT + tt + 1) * P],
                                             stack[:, tt, at:at + P], ident)
            mm.then_inc(kT_ps, 1)

        def scores(n, h):
            ps = s_bank[h % 2]
            pe.wait_ge(s_read, n * GROUP + h + 1)
            for tt in range(TT):
                for form in range(2):
                    mm = nc.tensor.matmul(ps[:, tt * SEQ:(tt + 1) * SEQ], qT[:, tt, h * P:(h + 1) * P], kT[:, form, :],
                                          start=(form == 0), stop=(form == 1))
            mm.then_inc(s_ps, 1)

        def prob_transposes(n, h):
            ps = p_bank[h % 2]
            pe.wait_ge(probs_done, n * GROUP + h + 3)
            pe.wait_ge(pT_lo_done, n * GROUP + h + 3)
            for c, (lo, at) in enumerate(((0, 0), (P, P), (2 * P, 2 * P))):
                mm = nc.tensor.transpose(ps[:, at:at + P], probs[:, h, lo:lo + P], ident)
            mm.then_inc(pT_ps, 1)

        def values(n, parity, odd):
            pe.wait_ge(pT_lo_done, n * GROUP + 3 + odd)
            if not odd:
                pe.wait_ge(v_done, n)
                if past(n, 2):
                    pe.wait_ge(o_lo_done, n - 1)
            out = o_bank[:, :].rearrange("p (pair q) -> p pair q", pair=PAIRS)
            first = not odd
            form = slice(0, 2 * HD) if odd else slice(HD, 3 * HD)
            for kt in range(TT):
                for v, pT in ((v_hi, pT_hi), (v_lo, pT_hi), (v_hi, pT_lo)):
                    heads = pT[:, odd:GROUP:2, :]
                    if kt == 0:
                        mm = nc.tensor.matmul(out, v[:, parity, kt, form], heads[:, :, 0:2 * P],
                                              start=first, stop=False, skip_group_check=True)
                    else:
                        mm = nc.tensor.matmul(out[:, :, P:2 * P], v[:, parity, kt, form], heads[:, :, 2 * P:3 * P],
                                              start=False, stop=True, skip_group_check=True)
                    first = False
            if odd:
                mm.then_inc(o_ps, 1)

        def output(n, g_out, tt):
            if tt == 0:
                pe.wait_ge(o_lo_done, n - 1)
                pe.wait_ge(y_added, n - 1)
            i = 0
            for pair in range(PAIRS):
                for o, w in ((oT_hi, wo_hi), (oT_lo, wo_hi), (oT_hi, wo_lo)):
                    mm = nc.tensor.matmul(y_bank[:, tt * EMB:(tt + 1) * EMB], o[:, pair, tt * P:(tt + 1) * P],
                                          w[:, bass.ds((g_out * PAIRS + pair) * EMB, EMB)],
                                          start=(i == 0), stop=(i == 3 * PAIRS - 1))
                    i += 1
            if tt == TT - 1:
                mm.then_inc(y_ps, 1)

        def turn(n, parity, g, b, prepare, last):
            m, odd = n + 1, 1 - parity
            g_next = (g + 1) % KV_HEADS
            pe.wait_ge(qT_done, n * 2 + 2)
            pe.wait_ge(kT_done, n + 1)
            scores(n, 0)
            if not last:
                if isinstance(b, int) and b == 0 and not (isinstance(g, int) and g == KV_HEADS - 1):
                    pe.wait_ge(w_split, g + 2)
                if isinstance(g, int) and g == KV_HEADS - 1:
                    pe.wait_ge(xT_hi_done, b * TT + 2 * TT)
                    pe.wait_ge(xT_lo_done, b * TT + 2 * TT)
                project(m, odd, g_next, 0)
            if past(n, 1):
                prob_transposes(n - 1, 2)
            scores(n, 1)
            if past(n, 1):
                prob_transposes(n - 1, 3)
            if not last:
                project(m, odd, g_next, 1)
            if past(n, 2):
                if isinstance(b, int) and b == 0:
                    pe.wait_ge(wo_split, g - 1)
                output(n, (g + KV_HEADS - 2) % KV_HEADS, 0)
            scores(n, 2)
            scores(n, 3)
            if past(n, 1):
                if isinstance(n, int) and n == 1:
                    pe.wait_ge(zeroed, 1)
                values(n, odd, 0)
            if past(n, 2):
                output(n, (g + KV_HEADS - 2) % KV_HEADS, 1)
            if not last:
                q_transposes(m, odd, 0)
            prob_transposes(n, 0)
            if not last:
                q_transposes(m, odd, 1)
                k_transposes(m, odd)
            if past(n, 1):
                values(n, odd, 1)
            prob_transposes(n, 1)
            if prepare:
                pe.wait_ge(qT_done, m * 2 + 2)
                pe.wait_ge(kT_done, m + 1)
                x_transposes(b * TT + TT)
            if isinstance(n, int) and n == KV_HEADS - 1:
                pe.wait_ge(wo_split, KV_HEADS)

        pe.wait_ge(consts_in, 16)
        x_transposes(0)
        pe.wait_ge(xT_hi_done, TT)
        pe.wait_ge(xT_lo_done, TT)
        pe.wait_ge(w_split, 1)
        project(0, 0, 0, 0)
        project(0, 0, 0, 1)
        q_transposes(0, 0, 0)
        q_transposes(0, 0, 1)
        k_transposes(0, 0)
        turns(pe, turn)
        prob_transposes(TURNS - 1, 2)
        prob_transposes(TURNS - 1, 3)
        output(TURNS, KV_HEADS - 2, 0)
        output(TURNS, KV_HEADS - 2, 1)
        values(TURNS, 1, 0)
        values(TURNS, 1, 1)
        output(TURNS + 1, KV_HEADS - 1, 0)
        output(TURNS + 1, KV_HEADS - 1, 1)

    @block.scalar
    def _(act):
        def x_hi(tile, tt):
            act.wait_ge(xT_ps, tile + 1)
            nc.scalar.copy(xT_hi[:, :, tt * P:(tt + 1) * P],
                           work[tt][:, 0:KT * P].rearrange("p (k q) -> p k q", k=KT)).then_inc(xT_hi_done, 1)

        def split_stack(m, tt, first=False):
            act.wait_ge(rope_done, m * 2 + tt + 1)
            if not first:
                act.wait_ge(kT_ps, m)
            hi = stack[:, tt, 0:(GROUP + 1) * P].rearrange("p (h two d) -> p h two d", two=2, d=HD)[:, :, 1, :]
            nc.scalar.copy(hi.bitcast(F32R), rotated[:, tt, :].rearrange("p (h d) -> p h d", d=HD)).then_inc(stack_hi, 1)

        def copy_qT(m, parity, tt):
            act.wait_ge(qT_ps, m * 2 + tt + 1)
            nc.scalar.copy(qT[:, tt, :], work[(tt + parity) % 2][:, :]).then_inc(qT_done, 1)

        def copy_kT(m, parity):
            act.wait_ge(kT_ps, m + 1)
            nc.scalar.copy(kT[:, :, :], work[parity][:, :].rearrange("p (f q) -> p f q", f=2)).then_inc(kT_done, 1)

        def exponentials(n, h):
            s = h % 2
            act.wait_ge(s_read, n * GROUP + h + 3)
            act.wait_ge(probs_done, n * GROUP + h + 1)
            nc.scalar.activation(exps[:, s, 0:P], masked[:, s, 0:P], ACT.Exp, bias=neg_max[:, s, 0:1], scale=-1.0,
                                 accum_out=sums[:, s, 0:1])
            nc.scalar.activation(exps[:, s, P:3 * P], masked[:, s, P:3 * P], ACT.Exp, bias=neg_max[:, s, 1:2],
                                 scale=-1.0, accum_out=sums[:, s, 1:2]).then_inc(exp_done, 1)

        def probs_hi(n, h):
            act.wait_ge(pT_ps, n * GROUP + h + 5)
            nc.scalar.copy(pT_hi[:, h, :], p_bank[h % 2][:, 0:3 * P]).then_inc(pT_hi_done, 1)

        def out_hi(n):
            act.wait_ge(o_ps, n)
            nc.scalar.copy(oT_hi[:, :, :], o_bank[:, :].rearrange("p (pair q) -> p pair q", pair=PAIRS)).then_inc(o_hi_done, 1)

        def split_w(p, g):
            act.wait_ge(w_in[p], g * 8 - p * 8 + 16)
            nc.scalar.copy(w_hi[:, :, bass.ds(g * GW, GW)],
                           w_raw[:, p, :].rearrange("p (k n) -> p k n", k=KT)).then_inc(w_hi_done, 1)

        def split_wo(p, g):
            act.wait_ge(wo_in[p], g * 8 - p * 8 + 16)
            nc.scalar.copy(wo_hi[:, bass.ds(g * GO, GO)], wo_raw[:, p, :]).then_inc(wo_hi_done, 1)

        def turn(n, parity, g, b, prepare, last):
            m, odd = n + 1, 1 - parity
            if past(n, 1):
                probs_hi(n - 1, 2)
            exponentials(n, 0)
            if past(n, 1):
                probs_hi(n - 1, 3)
            if not last:
                split_stack(m, 0)
            exponentials(n, 1)
            exponentials(n, 2)
            if not last:
                split_stack(m, 1)
            if isinstance(b, int) and b == 0:
                if not (isinstance(g, int) and g >= KV_HEADS - 2):
                    split_w(parity, g + 2)
                split_wo(parity, g)
            if not last:
                copy_qT(m, odd, 0)
            exponentials(n, 3)
            probs_hi(n, 0)
            if not last:
                copy_kT(m, odd)
                copy_qT(m, odd, 1)
            if past(n, 1):
                out_hi(n)
            probs_hi(n, 1)
            if prepare:
                x_hi(b * TT + TT, 0)
                x_hi(b * TT + TT + 1, 1)

        act.sem_inc(exp_done, 2)
        x_hi(0, 0)
        x_hi(1, 1)
        split_w(0, 0)
        split_stack(0, 0, True)
        split_stack(0, 1, True)
        copy_qT(0, 0, 0)
        copy_qT(0, 0, 1)
        copy_kT(0, 0)
        split_w(1, 1)
        turns(act, turn)
        probs_hi(TURNS - 1, 2)
        probs_hi(TURNS - 1, 3)
        out_hi(TURNS)

    @block.vector
    def _(dve):
        chain = [0]

        def wait_own(ins):
            chain[0] += 1
            ins.then_inc(step, 1)
            dve.wait_ge(step, chain[0])

        def normalise(tile, tt, first=False):
            if not first:
                dve.wait_ge(xT_ps, tile - 1)
            nc.vector.tensor_scalar(xn[:, tt, :], x_all[:, bass.ds(tile, 1), :].rearrange("p o e -> p (o e)"),
                                    moments[:, bass.ds(tile, 1), 0:1].rearrange("p o e -> p (o e)"), rstd[:, bass.ds(tile, 1)],
                                    ALU.subtract, ALU.mult).then_inc(xn_done, 1)

        def x_lo(tile, tt):
            dve.wait_ge(xT_hi_done, tile + 1)
            nc.vector.tensor_tensor(xT_lo[:, :, tt * P:(tt + 1) * P],
                                    work[tt][:, 0:KT * P].rearrange("p (k q) -> p k q", k=KT),
                                    xT_hi[:, :, tt * P:(tt + 1) * P].bitcast(F32), ALU.subtract).then_inc(xT_lo_done, 1)

        def rope(m, parity, tt, first=False):
            ps = work[(tt + parity) % 2]
            dve.wait_ge(proj_ps, m * 2 + tt + 1)
            if not first:
                dve.wait_ge(v_done, m)
                dve.wait_ge(rope_done, m * 2 + tt - 1)
            nc.vector.tensor_copy(v_raw[:, tt, :], ps[:, QK:GW]).then_inc(v_read, 1)
            x = ps[:, 0:QK].rearrange("p (h two d) -> p h two d", two=2, d=HD // 2)
            o = by_sin[:, tt, :].rearrange("p (h two d) -> p h two d", two=2, d=HD // 2)
            for half in range(2):
                s = sin[:, tt, half * 32:half * 32 + 32].rearrange("p (o d) -> p o d", o=1).to_broadcast([P, GROUP + 1, 32])
                nc.vector.tensor_tensor(o[:, :, half, :], x[:, :, 1 - half, :], s, ALU.mult)
            c = cos[:, tt, :].rearrange("p (o d) -> p o d", o=1).to_broadcast([P, GROUP + 1, HD])
            nc.vector.tensor_tensor(by_cos[:, tt, :].rearrange("p (h d) -> p h d", d=HD),
                                    ps[:, 0:QK].rearrange("p (h d) -> p h d", d=HD), c, ALU.mult).then_inc(rope_parts, 1)

        def stack_low(m, tt):
            dve.wait_ge(stack_hi, m * 2 + tt + 1)
            pairs = stack[:, tt, 0:(GROUP + 1) * P].rearrange("p (h two d) -> p h two d", two=2, d=HD)
            nc.vector.tensor_tensor(pairs[:, :, 0, :].bitcast(F32R), rotated[:, tt, :].rearrange("p (h d) -> p h d", d=HD),
                                    pairs[:, :, 1, :], ALU.subtract)
            k = GROUP * P
            nc.vector.tensor_tensor(stack[:, tt, k + 2 * HD:k + 3 * HD].bitcast(F32R), rotated[:, tt, GROUP * HD:QK],
                                    stack[:, tt, k + HD:k + 2 * HD], ALU.subtract).then_inc(stack_lo, 1)

        def maxima(n, h):
            s = h % 2
            dve.wait_ge(consts_in, 16)
            dve.wait_ge(s_ps, n * GROUP + h + 1)
            dve.wait_ge(exp_done, n * GROUP + h + 1)
            dve.sem_inc(dve_passed, 1)
            nc.vector.tensor_tensor_reduce(masked[:, s, 0:P], s_bank[s][:, 0:P], mask[:, P:2 * P], -(HD ** -0.5), 3e38,
                                           ALU.add, ALU.min, neg_max[:, s, 0:1])
            nc.vector.tensor_tensor_reduce(masked[:, s, P:3 * P], s_bank[s][:, SEQ:2 * SEQ], mask[:, 0:2 * P],
                                           -(HD ** -0.5), 3e38, ALU.add, ALU.min, neg_max[:, s, 1:2]).then_inc(s_read, 1)

        def inverses(n, h):
            s = h % 2
            dve.wait_ge(exp_done, n * GROUP + h + 3)
            nc.vector.reciprocal(inv_sums[:, s, :], sums[:, s, :]).then_inc(inv_done, 1)

        def probs_lo(n, h):
            dve.wait_ge(pT_hi_done, n * GROUP + h + 1)
            nc.vector.tensor_tensor(pT_lo[:, h, :], p_bank[h % 2][:, 0:3 * P], pT_hi[:, h, :].bitcast(F32),
                                    ALU.subtract).then_inc(pT_lo_done, 1)

        def out_lo(n):
            dve.wait_ge(o_hi_done, n)
            nc.vector.tensor_tensor(oT_lo[:, :, :], o_bank[:, :].rearrange("p (pair q) -> p pair q", pair=PAIRS),
                                    oT_hi[:, :, :].bitcast(F32), ALU.subtract).then_inc(o_lo_done, 1)

        def add_out(n, b):
            dve.wait_ge(y_ps, n - 1)
            dve.wait_ge(y_added, n - 1)
            xs = x_all[:, bass.ds(b * TT, TT), :]
            nc.vector.tensor_tensor(xs, xs, y_bank[:, :].rearrange("p (t e) -> p t e", t=TT), ALU.add).then_inc(y_added, 1)

        def split_w(p, g):
            dve.wait_ge(w_hi_done, g + 1)
            nc.vector.tensor_tensor(w_lo[:, :, bass.ds(g * GW, GW)], w_raw[:, p, :].rearrange("p (k n) -> p k n", k=KT),
                                    w_hi[:, :, bass.ds(g * GW, GW)].bitcast(F32), ALU.subtract).then_inc(w_split, 1)

        def split_wo(p, g):
            dve.wait_ge(wo_hi_done, g + 1)
            nc.vector.tensor_tensor(wo_lo[:, bass.ds(g * GO, GO)], wo_raw[:, p, :],
                                    wo_hi[:, bass.ds(g * GO, GO)].bitcast(F32), ALU.subtract).then_inc(wo_split, 1)

        def turn(n, parity, g, b, prepare, last):
            m, odd = n + 1, 1 - parity
            maxima(n, 0)
            if not last:
                rope(m, odd, 0)
            if past(n, 1):
                probs_lo(n - 1, 2)
            maxima(n, 1)
            inverses(n, 0)
            if not last:
                rope(m, odd, 1)
            maxima(n, 2)
            if not last:
                stack_low(m, 0)
            inverses(n, 1)
            maxima(n, 3)
            if not last:
                stack_low(m, 1)
            if past(n, 1):
                probs_lo(n - 1, 3)
            if past(n, 2):
                add_out(n, b + (g + KV_HEADS - 2) // KV_HEADS - 1)
            inverses(n, 2)
            if prepare:
                normalise(b * TT + TT, 0)
                normalise(b * TT + TT + 1, 1)
            inverses(n, 3)
            probs_lo(n, 0)
            if isinstance(b, int) and b == 0:
                if not (isinstance(g, int) and g >= KV_HEADS - 2):
                    split_w(parity, g + 2)
                split_wo(parity, g)
            if past(n, 1):
                out_lo(n)
            probs_lo(n, 1)
            if isinstance(g, int) and g == KV_HEADS - 1 and not (isinstance(b, int) and b == 0):
                dve.wait_ge(y_added, n - 1)
                for tile in range(TT):
                    at = (b - 1) * TT + tile
                    nc.vector.bn_stats(r["stats"][:, bass.ds(at, 1), :].rearrange("p o s -> p (o s)"),
                                       x_all[:, bass.ds(at, 1), :].rearrange("p o e -> p (o e)"))
            if prepare:
                x_lo(b * TT + TT, 0)
                x_lo(b * TT + TT + 1, 1)

        dve.sem_inc(s_read, 2)
        dve.sem_inc(y_added, 1)
        dve.sem_inc(pT_lo_done, 4)

        def layernorm_moments(a, b):
            for i in range(a, b):
                ins = nc.vector.bn_aggr(moments[:, i, :], stats[:, i, :])
            wait_own(ins)
            v, y, w = newton[:, 0, a:b], newton[:, 1, a:b], newton[:, 2, a:b]
            wait_own(nc.vector.tensor_scalar(v, moments[:, a:b, 1], EPS, None, ALU.add))
            wait_own(nc.vector.tensor_scalar(w.bitcast(I32), v.bitcast(I32), 1, None, ALU.logical_shift_right))
            wait_own(nc.vector.tensor_scalar(y.bitcast(I32), w.bitcast(I32), -1.0, RSQRT_MAGIC, ALU.mult, ALU.add))
            for i in range(4):
                wait_own(nc.vector.tensor_tensor(w, y, y, ALU.mult))
                wait_own(nc.vector.tensor_tensor(w, w, v, ALU.mult))
                wait_own(nc.vector.tensor_scalar(w, w, -0.5, 1.5, ALU.mult, ALU.add))
                wait_own(nc.vector.tensor_tensor(rstd[:, a:b] if i == 3 else y, y, w, ALU.mult))

        dve.wait_ge(x_first_in, 16)
        for i in range(TT):
            ins = nc.vector.bn_stats(stats[:, i, :], x_all[:, i, :])
        wait_own(ins)
        layernorm_moments(0, TT)
        normalise(0, 0, True)
        normalise(1, 1, True)
        x_lo(0, 0)
        x_lo(1, 1)
        split_w(0, 0)
        dve.wait_ge(x_rest_in, 16)
        for i in range(TT, TT + 6):
            nc.vector.bn_stats(stats[:, i, :], x_all[:, i, :])
        rope(0, 0, 0, True)
        rope(0, 0, 1, True)
        stack_low(0, 0)
        stack_low(0, 1)
        for i in range(TT + 6, TILES):
            ins = nc.vector.bn_stats(stats[:, i, :], x_all[:, i, :])
        wait_own(ins)
        split_w(1, 1)
        layernorm_moments(TT, TILES)
        turns(dve, turn)
        probs_lo(TURNS - 1, 2)
        probs_lo(TURNS - 1, 3)
        add_out(TURNS, BATCH - 1)
        out_lo(TURNS)
        add_out(TURNS + 1, BATCH - 1)

    @block.gpsimd
    def _(pool):
        def rotate(m, tt, first=False):
            pool.wait_ge(rope_parts, m * 2 + tt + 1)
            if not first:
                pool.wait_ge(stack_hi, m * 2 + tt - 1)
                pool.wait_ge(stack_lo, m * 2 + tt - 1)
            nc.gpsimd.tensor_tensor(rotated[:, tt, :], by_cos[:, tt, :], by_sin[:, tt, :], ALU.add).then_inc(rope_done, 1)

        def divide(n, h):
            s = h % 2
            pool.wait_ge(inv_done, n * GROUP + h + 1)
            pool.wait_ge(pT_ps, n * GROUP + h + 1)
            pool.sem_inc(pool_passed, 1)
            nc.gpsimd.tensor_scalar(probs[:, h, 0:P], exps[:, s, 0:P], inv_sums[:, s, 0:1], 1.0, ALU.mult, ALU.mult)
            nc.gpsimd.tensor_scalar(probs[:, h, P:3 * P], exps[:, s, P:3 * P], inv_sums[:, s, 1:2], 1.0,
                                    ALU.mult, ALU.mult).then_inc(probs_done, 1)

        def split_v(m, parity):
            hi, lo = v_hi[:, parity, :, HD:2 * HD], v_lo[:, parity, :, HD:2 * HD]
            if past(m, 2):
                pool.wait_ge(o_ps, m - 1)
            pool.wait_ge(v_read, m * 2 + 2)
            pool.sem_inc(pool_passed, 1)
            nc.gpsimd.tensor_copy(hi, v_raw[:, :, :]).then_inc(v_hi_done, 1)
            pool.wait_ge(v_hi_done, m + 1)
            nc.gpsimd.tensor_tensor(lo, v_raw[:, :, :], hi.bitcast(F32), ALU.subtract).then_inc(v_done, 1)

        def turn(n, parity, g, b, prepare, last):
            m = n + 1
            split_v(n, parity)
            if not last:
                rotate(m, 0)
            divide(n, 0)
            if not last:
                rotate(m, 1)
            divide(n, 1)
            divide(n, 2)
            divide(n, 3)

        pool.sem_inc(probs_done, 2)
        pool.sem_inc(pT_ps, GROUP)
        for z in (v_hi[:, :, :, :], v_lo[:, :, :, :]):
            ins = nc.gpsimd.memset(z.bitcast(F32), 0.0)
        ins.then_inc(zeroed, 1)
        pool.wait_ge(zeroed, 1)
        rotate(0, 0, True)
        rotate(0, 1, True)
        turns(pool, turn)


def route(nc, ctx, t, x_all, r):

    def sb(name, shape, dt=F32):
        return ctx.enter_context(nc.sbuf_tensor(name, shape, dt))

    def sem(name):
        return ctx.enter_context(nc.semaphore(name))

    TE = TILES * EXPERTS
    at = 2 * P + 2 * TE + (BLOCKS + 1) * EXPERTS
    consts = sb("route_tables", [P, at + P + 2 * TILES + 1])
    before, ones = consts[:, 0:P], consts[:, P:2 * P]
    rev = consts[:, 2 * P:2 * P + TE].rearrange("p (t e) -> p t e", e=EXPERTS)
    steps = consts[:, 2 * P + TE:2 * P + 2 * TE].rearrange("p (e t) -> p e t", e=EXPERTS)
    starts = consts[:, 2 * P + 2 * TE:at].rearrange("p (b e) -> p b e", e=EXPERTS)
    lanes, groups, lane = consts[:, at:at + P], consts[:, at + P:at + P + 2 * TILES], consts[:, at + P + 2 * TILES:]
    ident = sb("route_ident", [P, P])
    gate = sb("gate_in", [P, KT, EXPERTS])

    stats = r["stats"]
    moments = sb("moments2", [P, TILES, 2])
    rstd = sb("rstd2", [P, TILES])
    newton = sb("newton2", [P, 2, TILES])
    half = TILES * EMB
    xn = r["w_out"][:, 0:half].rearrange("p (t e) -> p t e", e=EMB)
    w_raw = r["w_out"][:, half:half + RAW * PIECE].rearrange("p (i c) -> p i c", c=PIECE)
    xT = sb("xT2", [P, 2, 2 * KT * P])
    logits = sb("logits", [P, TILES, EXPERTS])
    others = sb("others", [P, TILES, EXPERTS])
    equal = sb("equal", [P, TILES, EXPERTS])
    hot = [sb("hot1", [P, TILES, EXPERTS]), sb("hot2", [P, TILES, EXPERTS])]
    both = sb("both", [P, TILES, EXPERTS])
    best = sb("best", [P, 2, TILES])
    code = sb("code", [P, TILES])
    gap = sb("gap", [P, TILES])
    counts = sb("counts", [P, 2, TILES, EXPERTS])
    full = sb("full", [P, EXPERTS, TILES])
    blocks = sb("blocks", [P, EXPERTS])
    first_block = sb("first_block", [P, EXPERTS + 1])
    place = sb("place", [P, TILES, EXPERTS])
    chosen = sb("chosen", [P, TILES, EXPERTS])
    row = sb("row", [P, 2, TILES])
    later = sb("later", [P, BLOCKS + 1, EXPERTS])
    owner = sb("owner", [P, BLOCKS + 1])
    rows = sb("rows", [P, 2 * TILES], I32)
    row_part = sb("row_part", [P, 2, 2 * TILES], I32)
    row_block = sb("row_block", [P, 2 * TILES])
    row_lane = sb("row_lane", [P, 2 * TILES])
    lane_hot = sb("lane_hot", [P, 2 * TILES, P], BF16)
    block_codes = sb("block_codes", [P, 2 * TILES, 2, BLOCKS], BF16)
    pair_of = sb("pair_of", [P, 2, BLOCKS])

    tr_bank = [ctx.enter_context(nc.psum_tensor(f"tr{i}", [P, 512], F32)) for i in range(2)]
    logit_bank = ctx.enter_context(nc.psum_tensor("logit_bank", [P, 512], F32))
    rank_bank = ctx.enter_context(nc.psum_tensor("rank_bank", [P, 512], F32))
    pair_bank = ctx.enter_context(nc.psum_tensor("pair_bank", [P, 512], F32))

    consts_in = sem("route_consts_in")
    step = sem("route_step")
    xn_done = sem("xn2_done")
    xT_ps = sem("xT2_ps")
    xT_done = sem("xT2_done")
    logits_ps = sem("logits_ps")
    both_done = sem("both_done")
    ranks_ps = sem("ranks_ps")
    gap_done = sem("gap_done")
    exp_done = sem("gap_exp_done")
    block_hot_done = sem("block_hot_done")
    lane_hot_done = sem("lane_hot_done")
    pairs_ps = sem("pairs_ps")
    xn_out = sem("xn_out")
    piece_in = [sem(f"piece_in{i}") for i in range(RAW)]
    piece_hi_done = sem("piece_hi_done")
    piece_split = sem("piece_split")

    block = ctx.enter_context(nc.Block())

    @block.sync
    def _(sp):
        sp.dma_start(consts[:, :], t["route_consts"]).then_inc(consts_in, 16)
        sp.dma_start(ident[:, :], t["attn_consts"][:, 2 * TT * HD + 2 * P:]).then_inc(consts_in, 16)
        sp.dma_start(gate[:, :, :], t["gate"].rearrange("p (k e) -> p k e", k=KT)).then_inc(consts_in, 16)
        for i in range(PIECES):
            if i >= RAW:
                sp.wait_ge(piece_split, i - RAW + 1)
            sp.dma_start(w_raw[:, i % RAW, :], t["w_in"][:, i * PIECE:(i + 1) * PIECE]).then_inc(piece_in[i % RAW], 16)
        sp.wait_ge(xn_out, 16 * TILES // 4)
        sp.wait_ge(xT_ps, TILES // 2)
        sp.dma_start(r["w_out"][:, 0:half], t["w_out"][:, 0:half]).then_inc(r["w_out_in"], 16)
        sp.wait_ge(piece_split, PIECES)
        sp.dma_start(r["w_out"][:, half:2 * half], t["w_out"][:, half:2 * half]).then_inc(r["w_out_in"], 16)

    @block.tensor
    def _(pe):
        def transposes(i):
            pe.wait_ge(xn_done, 2 * i + 2)
            if i >= 2:
                pe.wait_ge(xT_done, i - 1)
            for tile in range(2):
                for k in range(KT):
                    mm = nc.tensor.transpose(tr_bank[i % 2][:, (tile * KT + k) * P:(tile * KT + k + 1) * P],
                                             xn[:, 2 * i + tile, k * P:(k + 1) * P], ident[:, :])
            mm.then_inc(xT_ps, 1)

        def gate_logits(i):
            pe.wait_ge(xT_done, i + 1)
            for tile in range(2):
                at = (2 * i + tile) * EXPERTS
                for k in range(KT):
                    mm = nc.tensor.matmul(logit_bank[:, at:at + EXPERTS], xT[:, i % 2, (tile * KT + k) * P:(tile * KT + k + 1) * P],
                                          gate[:, k, :], start=(k == 0), stop=(k == KT - 1))
            mm.then_inc(logits_ps, 1)

        pe.wait_ge(consts_in, 48)
        for i in range(TILES // 2 + 1):
            if i < TILES // 2:
                transposes(i)
            if i >= 1:
                gate_logits(i - 1)
        pe.wait_ge(both_done, 1)
        m = both[:, :, :].rearrange("p t e -> p (t e)")
        nc.tensor.matmul(rank_bank[:, 0:TE], before, m, start=True, stop=True)
        nc.tensor.matmul(rank_bank[:, TE:2 * TE], ones, m, start=True, stop=True).then_inc(ranks_ps, 1)
        pe.wait_ge(block_hot_done, 1)
        for i in range(2 * TILES):
            pe.wait_ge(lane_hot_done, i // (TILES // 2) + 1)
            mm = nc.tensor.matmul(pair_bank[:, 0:2 * BLOCKS], lane_hot[:, i, :],
                                  block_codes[:, i, :, :].rearrange("p two b -> p (two b)"),
                                  start=(i == 0), stop=(i == 2 * TILES - 1))
        mm.then_inc(pairs_ps, 1)

    @block.scalar
    def _(act):
        def piece_hi(i):
            act.wait_ge(piece_in[i % RAW], 16 * (i // RAW + 1))
            nc.scalar.copy(r["w_hi"][:, i * PIECE:(i + 1) * PIECE], w_raw[:, i % RAW, :]).then_inc(piece_hi_done, 1)

        for i in range(4):
            piece_hi(i)
        for i in range(TILES // 2):
            act.wait_ge(xT_ps, i + 1)
            if i >= 2:
                act.wait_ge(logits_ps, i - 1)
            nc.scalar.copy(xT[:, i % 2, :], tr_bank[i % 2][:, :]).then_inc(xT_done, 1)
            piece_hi(i + 4)
            if i % 2 == 1:
                act.wait_ge(xn_done, 2 * i + 2)
                four = slice(2 * i - 2, 2 * i + 2)
                nc.scalar.dma_start(t["xn"].rearrange("(t p) e -> p t e", p=P)[:, four, :], xn[:, four, :]).then_inc(xn_out, 16)
        for i in range(TILES // 2 + 4, PIECES - 2):
            piece_hi(i)
        act.wait_ge(gap_done, 1)
        nc.scalar.activation(gap[:, :], gap[:, :], ACT.Exp).then_inc(exp_done, 1)
        for i in range(PIECES - 2, PIECES):
            piece_hi(i)
        act.wait_ge(xn_out, 16 * TILES // 4)

    @block.gpsimd
    def _(pool):
        for i in range(PIECES):
            pool.wait_ge(piece_hi_done, i + 1)
            cols = slice(i * PIECE, (i + 1) * PIECE)
            nc.gpsimd.tensor_tensor(r["w_lo"][:, cols], w_raw[:, i % RAW, :], r["w_hi"][:, cols].bitcast(F32),
                                    ALU.subtract).then_inc(piece_split, 1)

    @block.vector
    def _(dve):
        chain = [0]

        def wait_own(ins):
            chain[0] += 1
            ins.then_inc(step, 1)
            dve.wait_ge(step, chain[0])

        for i in range(TILES - TT, TILES):
            ins = nc.vector.bn_stats(stats[:, i, :], x_all[:, i, :])
        wait_own(ins)
        for i in range(TILES):
            ins = nc.vector.bn_aggr(moments[:, i, :], stats[:, i, :])
        wait_own(ins)
        v, y, w = newton[:, 0, :], rstd[:, :], newton[:, 1, :]
        wait_own(nc.vector.tensor_scalar(v, moments[:, :, 1], EPS, None, ALU.add))
        wait_own(nc.vector.tensor_scalar(w.bitcast(I32), v.bitcast(I32), 1, None, ALU.logical_shift_right))
        wait_own(nc.vector.tensor_scalar(y.bitcast(I32), w.bitcast(I32), -1.0, RSQRT_MAGIC, ALU.mult, ALU.add))
        for i in range(4):
            wait_own(nc.vector.tensor_tensor(w, y, y, ALU.mult))
            wait_own(nc.vector.tensor_tensor(w, w, v, ALU.mult))
            wait_own(nc.vector.tensor_scalar(w, w, -0.5, 1.5, ALU.mult, ALU.add))
            wait_own(nc.vector.tensor_tensor(y, y, w, ALU.mult))
        for i in range(TILES):
            nc.vector.tensor_scalar(xn[:, i, :], x_all[:, i, :], moments[:, i, 0:1], rstd[:, i:i + 1],
                                    ALU.subtract, ALU.mult).then_inc(xn_done, 1)

        def over_experts(a):
            return a.rearrange("p (t o) -> p t o", o=1).to_broadcast([P, TILES, EXPERTS])

        def choose(c, scores):
            wait_own(nc.vector.tensor_reduce(best[:, c, :], scores, AX.X, ALU.max))
            wait_own(nc.vector.tensor_tensor(equal[:, :, :], scores, over_experts(best[:, c, :]), ALU.is_equal))
            wait_own(nc.vector.tensor_tensor(equal[:, :, :], equal[:, :, :], rev, ALU.mult))
            wait_own(nc.vector.tensor_reduce(code[:, :], equal[:, :, :], AX.X, ALU.max))
            wait_own(nc.vector.tensor_tensor(hot[c][:, :, :], rev, over_experts(code[:, :]), ALU.is_equal))

        dve.wait_ge(logits_ps, TILES // 2)
        wait_own(nc.vector.tensor_copy(logits[:, :, :], logit_bank[:, 0:TE].rearrange("p (t e) -> p t e", e=EXPERTS)))
        dve.wait_ge(consts_in, 48)
        choose(0, logits[:, :, :])
        wait_own(nc.vector.scalar_tensor_tensor(out=others[:, :, :], in0=hot[0][:, :, :], scalar=-3e38,
                                                in1=logits[:, :, :], op0=ALU.mult, op1=ALU.add))
        choose(1, others[:, :, :])
        nc.vector.tensor_tensor(both[:, :, :], hot[0][:, :, :], hot[1][:, :, :], ALU.add).then_inc(both_done, 1)
        nc.vector.tensor_tensor(gap[:, :], best[:, 1, :], best[:, 0, :], ALU.subtract).then_inc(gap_done, 1)
        dve.wait_ge(exp_done, 1)
        wait_own(nc.vector.tensor_scalar(code[:, :], gap[:, :], 1.0, None, ALU.add))
        wait_own(nc.vector.reciprocal(r["weights"][:, 0, :], code[:, :]))
        nc.vector.tensor_tensor(r["weights"][:, 1, :], gap[:, :], r["weights"][:, 0, :], ALU.mult)

        dve.wait_ge(ranks_ps, 1)
        total = rank_bank[:, TE:2 * TE].rearrange("p (t e) -> p t e", e=EXPERTS)
        wait_own(nc.vector.tensor_copy(counts[:, 0, :, :], total))
        side = 0
        for s in (1, 2, 4, 8):
            wait_own(nc.vector.tensor_copy(counts[:, 1 - side, 0:s, :], counts[:, side, 0:s, :]))
            wait_own(nc.vector.tensor_tensor(counts[:, 1 - side, s:TILES, :], counts[:, side, s:TILES, :],
                                             counts[:, side, 0:TILES - s, :], ALU.add))
            side = 1 - side
        all_counts = counts[:, side, TILES - 1, :].rearrange("p (e o) -> p e o", o=1).to_broadcast([P, EXPERTS, TILES])
        wait_own(nc.vector.tensor_tensor(full[:, :, :], all_counts, steps, ALU.is_gt))
        wait_own(nc.vector.tensor_reduce(blocks[:, :], full[:, :, :], AX.X, ALU.add))
        wait_own(nc.vector.memset(first_block[:, 0:1], 0.0))
        for e in range(EXPERTS):
            wait_own(nc.vector.tensor_tensor(first_block[:, e + 1:e + 2], first_block[:, e:e + 1], blocks[:, e:e + 1], ALU.add))
        wait_own(nc.vector.tensor_scalar(first_block[:, :], first_block[:, :], float(P), None, ALU.mult))
        earlier = counts[:, 1 - side, :, :]
        wait_own(nc.vector.tensor_tensor(earlier, counts[:, side, :, :], total, ALU.subtract))
        firsts = first_block[:, 0:EXPERTS].rearrange("p (o e) -> p o e", o=1).to_broadcast([P, TILES, EXPERTS])
        wait_own(nc.vector.tensor_tensor(place[:, :, :], earlier, firsts, ALU.add))
        wait_own(nc.vector.tensor_tensor(place[:, :, :], place[:, :, :],
                                         rank_bank[:, 0:TE].rearrange("p (t e) -> p t e", e=EXPERTS), ALU.add))
        for c in range(2):
            wait_own(nc.vector.tensor_tensor(chosen[:, :, :], hot[c][:, :, :], place[:, :, :], ALU.mult))
            wait_own(nc.vector.tensor_reduce(row[:, c, :], chosen[:, :, :], AX.X, ALU.add))
        wait_own(nc.vector.tensor_copy(rows[:, :], row[:, :, :].rearrange("p c t -> p (c t)")))
        nc.vector.tensor_scalar(row_part[:, 0, :], rows[:, :], 7, None, ALU.logical_shift_right)
        wait_own(nc.vector.tensor_scalar(row_part[:, 1, :], rows[:, :], P - 1, None, ALU.bitwise_and))
        nc.vector.tensor_copy(row_block[:, :], row_part[:, 0, :])
        wait_own(nc.vector.tensor_copy(row_lane[:, :], row_part[:, 1, :]))

        def spread(a, n):
            return a.rearrange("p (t o) -> p t o", o=1).to_broadcast([P, a.shape[1], n])

        blocks_line = starts[:, 0:BLOCKS, 0].rearrange("p (o b) -> p o b", o=1).to_broadcast([P, 2 * TILES, BLOCKS])
        wait_own(nc.vector.tensor_scalar(row_block[:, :], row_block[:, :], float(P), None, ALU.mult))
        block_hot = block_codes[:, :, 1, :]
        wait_own(nc.vector.tensor_tensor(block_hot, blocks_line, spread(row_block[:, :], BLOCKS), ALU.is_equal))
        wait_own(nc.vector.tensor_tensor(block_codes[:, :, 0, :], block_hot, spread(groups, BLOCKS), ALU.mult))
        nc.vector.tensor_scalar(block_hot, block_hot, lane, None, ALU.mult).then_inc(block_hot_done, 1)
        lanes_line = lanes.rearrange("p (o q) -> p o q", o=1).to_broadcast([P, TILES // 2, P])
        for i in range(0, 2 * TILES, TILES // 2):
            nc.vector.tensor_tensor(lane_hot[:, i:i + TILES // 2, :], lanes_line, spread(row_lane[:, i:i + TILES // 2], P),
                                    ALU.is_equal).then_inc(lane_hot_done, 1)
        bounds = first_block[:, 0:EXPERTS].rearrange("p (o e) -> p o e", o=1).to_broadcast([P, BLOCKS + 1, EXPERTS])
        wait_own(nc.vector.tensor_tensor(later[:, :, :], starts, bounds, ALU.is_ge))
        wait_own(nc.vector.tensor_reduce(owner[:, :], later[:, :, :], AX.X, ALU.add))
        nc.vector.tensor_scalar(r["owners"][:, :], owner[:, :], -1.0, None, ALU.add)
        dve.wait_ge(pairs_ps, 1)
        wait_own(nc.vector.tensor_scalar(pair_of[:, 0, :], pair_bank[:, 0:BLOCKS], float(P), None, ALU.mult))
        wait_own(nc.vector.tensor_tensor(pair_of[:, 0, :], pair_of[:, 0, :], pair_bank[:, BLOCKS:2 * BLOCKS], ALU.add))
        wait_own(nc.vector.tensor_scalar(pair_of[:, 0, :], pair_of[:, 0, :], lane, None, ALU.max))
        nc.vector.tensor_copy(r["to_pair"][:, :], pair_of[:, 0, :])
        wait_own(nc.vector.tensor_scalar(pair_of[:, 1, :], pair_of[:, 0, :], float(TOKENS - P), None, ALU.add))
        wait_own(nc.vector.tensor_copy(r["from_token"][:, :], pair_of[:, 1, :]))
        wait_own(nc.vector.tensor_scalar(r["from_token"][:, :], r["from_token"][:, :], TOKENS - 1, None, ALU.bitwise_and))


def experts(nc, ctx, t, x_all, r):

    def sb(name, shape, dt=F32):
        return ctx.enter_context(nc.sbuf_tensor(name, shape, dt))

    def sem(name):
        return ctx.enter_context(nc.semaphore(name))

    w_hi, w_lo, w_out = r["w_hi"], r["w_lo"], r["w_out"]
    from_now = sb("from_now", [P, RING], U32)
    to_now = sb("to_now", [P, RING], U32)
    ident = sb("experts_ident", [P, P])
    xs = sb("xs", [P, RING, EMB])
    xT_hi = sb("xsT_hi", [P, RING, KT * P], F32R)
    xT_lo = sb("xsT_lo", [P, RING, KT * P], F32R)
    act_h = sb("act_h", [P, MLP])
    gated = sb("gated", [P, MLP])
    gT = sb("gT", [P, MT * P])
    y = sb("y", [P, RING, EMB])

    def bank(name):
        return ctx.enter_context(nc.psum_tensor(name, [P, 512], F32))

    tx, h0, h1, tg, yb = bank("tx"), bank("h0"), bank("h1"), bank("tg"), bank("yb")

    ident_in = sem("experts_ident_in")
    xs_in = [sem(f"xs_in{p}") for p in range(RING)]
    xT_ps = sem("xsT_ps")
    xT_hi_done = sem("xsT_hi_done")
    xT_lo_done = sem("xsT_lo_done")
    h0_ps = sem("h0_ps")
    h1_ps = sem("h1_ps")
    silu_done = sem("silu_done")
    gated_done = sem("gated_done")
    gT_ps = sem("gT_ps")
    gT_done = sem("gT_done")
    yb_ps = sem("yb_ps")
    y_done = sem("y_done")
    y_out = [sem(f"y_out{p}") for p in range(RING)]
    pool_passed = sem("experts_pool_passed")
    from_ready = sem("from_ready")
    to_ready = sem("to_ready")

    block = ctx.enter_context(nc.Block())

    def passes(eng, turn):
        for p in range(RING):
            turn(0, p)
        with eng.Fori(1, BLOCKS // RING - 1) as q:
            for p in range(RING):
                turn(q, p)
        for p in range(RING):
            turn(BLOCKS // RING - 1, p)

    def after(q, p, n=1):
        return q + (p + n) // RING, (p + n) % RING

    def is_block(q, p, j):
        return isinstance(q, int) and q * RING + p == j

    @block.sync
    def _(sp):
        sp.dma_start(ident[:, :], t["attn_consts"][:, 2 * TT * HD + 2 * P:]).then_inc(ident_in, 16)
        for p in range(RING):
            sp.wait_ge(y_out[p], 16 * BLOCKS // RING)

    @block.tensor
    def _(pe):
        def x_transposes(q, p, first=False):
            j = q * RING + p
            pe.wait_ge(xs_in[p], q * 16 + 16)
            if not first:
                pe.wait_ge(xT_lo_done, j)
            for k in range(KT):
                mm = nc.tensor.transpose(tx[:, k * P:(k + 1) * P], xs[:, p, k * P:(k + 1) * P], ident[:, :])
            mm.then_inc(xT_ps, 1)

        def hidden(j, p, expert, which):
            ps, done = ((h0, h0_ps), (h1, h1_ps))[which]
            n = 0
            for k in range(KT):
                for x, w in ((xT_hi, w_hi), (xT_hi, w_lo), (xT_lo, w_hi)):
                    mm = nc.tensor.matmul(ps[:, :], x[:, p, k * P:(k + 1) * P],
                                          w[:, bass.ds(expert * WI + (which * KT + k) * MLP, MLP)],
                                          start=(n == 0), stop=(n == 3 * KT - 1))
                    n += 1
            mm.then_inc(done, 1)

        def g_transposes(j):
            pe.wait_ge(gated_done, j + 1)
            for k in range(MT):
                mm = nc.tensor.transpose(tg[:, k * P:(k + 1) * P], gated[:, k * P:(k + 1) * P], ident[:, :])
            mm.then_inc(gT_ps, 1)

        def output(j, expert, first=False):
            pe.wait_ge(gT_done, j + 1)
            if not first:
                pe.wait_ge(y_done, j)
            for k in range(MT):
                mm = nc.tensor.matmul(yb[:, 0:EMB], gT[:, k * P:(k + 1) * P], w_out[:, bass.ds(expert * WO + k * EMB, EMB)],
                                      start=(k == 0), stop=(k == MT - 1))
            mm.then_inc(yb_ps, 1)

        def owner(j):
            return pe.value_load(r["owners"][0:1, bass.ds(j, 1)], min_val=0, max_val=EXPERTS - 1)

        def turn(q, p):
            j = q * RING + p
            if is_block(q, p, 0):
                hidden(0, 0, owner(0), 0)
                hidden(0, 0, owner(0), 1)
                x_transposes(0, 1)
                pe.wait_ge(r["w_out_in"], 32)
                return
            expert, last_expert = owner(j), owner(j - 1)
            pe.wait_ge(xT_lo_done, j + 1)
            pe.wait_ge(gated_done, j)
            hidden(j, p, expert, 0)
            g_transposes(j - 1)
            hidden(j, p, expert, 1)
            if not is_block(q, p, BLOCKS - 1):
                x_transposes(*after(q, p))
            output(j - 1, last_expert)

        pe.wait_ge(ident_in, 16)
        x_transposes(0, 0, True)
        pe.wait_ge(xT_lo_done, 1)
        passes(pe, turn)
        g_transposes(BLOCKS - 1)
        output(BLOCKS - 1, owner(BLOCKS - 1))

    @block.scalar
    def _(act):
        def x_copy(j, p):
            act.wait_ge(xT_ps, j + 1)
            nc.scalar.copy(xT_hi[:, p, :], tx[:, 0:KT * P]).then_inc(xT_hi_done, 1)

        def silu(j):
            act.wait_ge(h0_ps, j + 1)
            nc.scalar.activation(act_h[:, :], h0[:, :], SILU).then_inc(silu_done, 1)

        def g_copy(j):
            act.wait_ge(gT_ps, j + 1)
            nc.scalar.copy(gT[:, :], tg[:, :]).then_inc(gT_done, 1)

        def turn(q, p):
            j = q * RING + p
            if not is_block(q, p, 0):
                act.wait_ge(gated_done, j)
            silu(j)
            if not is_block(q, p, 0):
                g_copy(j - 1)
            if not is_block(q, p, BLOCKS - 1):
                x_copy(j + 1, (p + 1) % RING)

        x_copy(0, 0)
        passes(act, turn)
        g_copy(BLOCKS - 1)

    @block.vector
    def _(dve):
        def gate_rows(j, first=False):
            dve.wait_ge(silu_done, j + 1)
            dve.wait_ge(h1_ps, j + 1)
            if not first:
                dve.wait_ge(gT_ps, j)
            nc.vector.tensor_tensor(gated[:, :], h1[:, :], act_h[:, :], ALU.mult).then_inc(gated_done, 1)

        def x_lo(j, p):
            dve.wait_ge(xT_hi_done, j + 1)
            nc.vector.tensor_tensor(xT_lo[:, p, :], tx[:, 0:KT * P], xT_hi[:, p, :].bitcast(F32), ALU.subtract).then_inc(xT_lo_done, 1)

        def y_copy(q, p):
            dve.wait_ge(yb_ps, q * RING + p + 1)
            if not isinstance(q, int) or q > 0:
                dve.wait_ge(y_out[p], q * 16)
            nc.vector.tensor_copy(y[:, p, :], yb[:, 0:EMB]).then_inc(y_done, 1)

        def turn(q, p):
            if not is_block(q, p, BLOCKS - 1):
                gate_rows(q * RING + p + 1)
                if not is_block(q, p, BLOCKS - 2):
                    x_lo(q * RING + p + 2, (p + 2) % RING)
            y_copy(q, p)

        x_lo(0, 0)
        gate_rows(0, True)
        x_lo(1, 1)
        passes(dve, turn)

    @block.gpsimd
    def _(pool):
        def gather(q, p):
            j = q * RING + p
            if not isinstance(q, int) or q > 0:
                pool.wait_ge(xT_ps, j - RING + 1)
                pool.sem_inc(pool_passed, 1)
            nc.gpsimd.tensor_copy(from_now[:, p:p + 1], r["from_token"][:, bass.ds(j, 1)]).then_inc(from_ready, 1)
            pool.wait_ge(from_ready, j + 1)
            pool.sem_inc(pool_passed, 1)
            pool.indirect_dma_start(
                out=xs[:, p, :], out_offset=None, in_=t["xn"],
                in_offset=bass.IndirectOffsetOnAxis(ap=from_now[:, p:p + 1], axis=0)).then_inc(xs_in[p], 16)

        def scatter(q, p):
            j = q * RING + p
            pool.wait_ge(y_done, j + 1)
            if not is_block(q, p, 0):
                pool.wait_ge(y_out[(p - 1) % RING], (q + 1 if p else q) * 16)
            pool.sem_inc(pool_passed, 1)
            nc.gpsimd.tensor_copy(to_now[:, p:p + 1], r["to_pair"][:, bass.ds(j, 1)]).then_inc(to_ready, 1)
            pool.wait_ge(to_ready, j + 1)
            pool.sem_inc(pool_passed, 1)
            pool.indirect_dma_start(
                out=t["y_pairs"], out_offset=bass.IndirectOffsetOnAxis(ap=to_now[:, p:p + 1], axis=0),
                in_=y[:, p, :], in_offset=None).then_inc(y_out[p], 16)

        def turn(q, p):
            if not (isinstance(q, int) and q == BLOCKS // RING - 1):
                gather(q + 1, p)
            scatter(q, p)

        for p in range(RING):
            gather(0, p)
        passes(pool, turn)


def combine(nc, ctx, t, x_all, r):
    QUARTERS = 4
    ya = ctx.enter_context(nc.sbuf_tensor("ya", [P, 2, TILES, EMB], F32))
    pairs_in = [ctx.enter_context(nc.semaphore(f"pairs_in{i}")) for i in range(QUARTERS)]
    weighed = ctx.enter_context(nc.semaphore("weighed"))
    summed = ctx.enter_context(nc.semaphore("summed"))
    stored = ctx.enter_context(nc.semaphore("stored"))
    block = ctx.enter_context(nc.Block())

    @block.sync
    def _(sp):
        pairs = t["y_pairs"][P:, :].rearrange("(c t p) e -> p c t e", c=2, p=P)
        step = TILES // QUARTERS
        for i in range(QUARTERS):
            for c in range(2):
                sp.dma_start(ya[:, c, i * step:(i + 1) * step, :], pairs[:, c, i * step:(i + 1) * step, :]).then_inc(pairs_in[i], 16)
        for i in range(TILES):
            sp.wait_ge(summed, i + 1)
            sp.dma_start(t["out"].rearrange("b (t p) e -> (b t) p e", p=P)[i], x_all[:, i, :]).then_inc(stored, 16)
        sp.wait_ge(stored, 16 * TILES)

    @block.vector
    def _(dve):
        for i in range(TILES):
            xt = x_all[:, i, :]
            dve.wait_ge(pairs_in[i * QUARTERS // TILES], 32)
            nc.vector.scalar_tensor_tensor(out=xt, in0=ya[:, 0, i, :], scalar=r["weights"][:, 0, i:i + 1], in1=xt,
                                           op0=ALU.mult, op1=ALU.add).then_inc(weighed, 1)
            dve.wait_ge(weighed, i + 1)
            nc.vector.scalar_tensor_tensor(out=xt, in0=ya[:, 1, i, :], scalar=r["weights"][:, 1, i:i + 1], in1=xt,
                                           op0=ALU.mult, op1=ALU.add).then_inc(summed, 1)


def program(nc, t):
    t = dict(t)
    t["xn"] = nc.dram_tensor("xn_rows", [TOKENS, EMB], F32).ap()
    t["y_pairs"] = nc.dram_tensor("y_pairs", [P + PAIRS_ALL, EMB], F32).ap()
    with ExitStack() as outer:
        x_all = outer.enter_context(nc.sbuf_tensor("x_all", [P, TILES, EMB], F32))
        r = {
            "stats": outer.enter_context(nc.sbuf_tensor("stats2", [P, TILES, 6], F32)),
            "to_pair": outer.enter_context(nc.sbuf_tensor("to_pair", [P, BLOCKS], U32)),
            "from_token": outer.enter_context(nc.sbuf_tensor("from_token", [P, BLOCKS], U32)),
            "weights": outer.enter_context(nc.sbuf_tensor("weights", [P, 2, TILES], F32)),
            "owners": outer.enter_context(nc.sbuf_tensor("owners", [P, BLOCKS + 1], I32)),
        }
        with ExitStack() as ctx:
            attention(nc, ctx, t, x_all, r)
        with ExitStack() as ctx:
            r["w_hi"] = ctx.enter_context(nc.sbuf_tensor("experts_w_hi", [P, EXPERTS * WI], F32R))
            r["w_lo"] = ctx.enter_context(nc.sbuf_tensor("experts_w_lo", [P, EXPERTS * WI], F32R))
            r["w_out"] = ctx.enter_context(nc.sbuf_tensor("experts_w_out", [P, EXPERTS * WO], F32))
            r["w_out_in"] = ctx.enter_context(nc.semaphore("w_out_in"))
            with ExitStack() as part:
                route(nc, part, t, x_all, r)
            with ExitStack() as part:
                experts(nc, part, t, x_all, r)
        with ExitStack() as ctx:
            combine(nc, ctx, t, x_all, r)


def laid_out(x, wq, wk, wv, wo, gate, w0, w1, w2):
    wqT = wq.T.reshape(KT, P, KV_HEADS, GROUP * HD)
    wkT = wk.T.reshape(KT, P, KV_HEADS, HD)
    wvT = wv.T.reshape(KT, P, KV_HEADS, HD)
    w_qkv = np.concatenate([wqT, wkT, wvT], 3).transpose(1, 2, 0, 3).reshape(P, KV_HEADS, KT * GW)
    wo_t = wo.T.reshape(HEADS // 2, P, EMB).transpose(1, 0, 2).reshape(P, HEADS // 2 * EMB)
    attn, route = shape_constants()
    return {
        "x": x, "w_qkv": w_qkv, "wo": wo_t, "attn_consts": attn, "route_consts": route,
        "gate": gate.reshape(KT, P, EXPERTS).transpose(1, 0, 2).reshape(P, KT * EXPERTS),
        "w_in": np.concatenate([w0.reshape(EXPERTS, KT, P, MLP), w1.reshape(EXPERTS, KT, P, MLP)], 1)
        .transpose(2, 0, 1, 3).reshape(P, EXPERTS * 2 * KT * MLP),
        "w_out": w2.reshape(EXPERTS, MT, P, EMB).transpose(2, 0, 1, 3).reshape(P, EXPERTS * MT * EMB),
    }


def kernel(L0_attn_hidden_states, L0_attn_wq, L0_attn_wk, L0_attn_wv, L0_attn_wo, L0_attn_wq_s, L0_attn_wk_s,
           L0_attn_wv_s, L0_attn_wo_s, L0_ffn_gate_kernel, L0_ffn_w0_kernel, L0_ffn_w1_kernel, L0_ffn_wo_kernel):
    import concourse.bacc as bacc
    from concourse.bass_utils import run_bass_kernel_spmd

    arrays = laid_out(L0_attn_hidden_states, L0_attn_wq, L0_attn_wk, L0_attn_wv, L0_attn_wo,
                      L0_ffn_gate_kernel, L0_ffn_w0_kernel, L0_ffn_w1_kernel, L0_ffn_wo_kernel)
    arrays = {name: np.ascontiguousarray(a) for name, a in arrays.items()}
    nc = bacc.Bacc("TRN2", target_bir_lowering=False, num_devices=1)
    t = {name: nc.dram_tensor(name, a.shape, mybir.dt.from_np(a.dtype), kind="ExternalInput").ap()
         for name, a in arrays.items()}
    t["out"] = nc.dram_tensor("out", (BATCH, SEQ, EMB), F32, kind="ExternalOutput").ap()
    program(nc, t)
    return run_bass_kernel_spmd(nc, [arrays], core_ids=[0]).results[0]["out"]
```

```python
from contextlib import ExitStack

import numpy as np

import concourse.bass as bass
import concourse.mybir as mybir

F32 = mybir.dt.float32
F32R = mybir.dt.float32r
BF16 = mybir.dt.bfloat16
I32 = mybir.dt.int32
U32 = mybir.dt.uint32
ALU = mybir.AluOpType
ACT = mybir.ActivationFunctionType
AX = mybir.AxisListType

P = 128
BATCH, SEQ, EMB = 8, 256, 256
HEADS, KV_HEADS, HD = 32, 8, 64
GROUP = HEADS // KV_HEADS
KT = EMB // P
TT = SEQ // P
TILES = BATCH * TT
TOKENS = BATCH * SEQ
QK = (GROUP + 1) * HD
GW = QK + HD
PAIRS = GROUP // 2
THETA = 500000.0
EPS = 1e-5
MASKED = -1e30
STACK = GROUP * P + 3 * HD

EXPERTS, MLP = 8, 512
MT = MLP // P
BLOCKS = TOKENS * 2 // P + EXPERTS - 1
PAIRS_ALL = 2 * TOKENS
RSQRT_MAGIC = 1597463007.0
SILU = ACT.Silu
RING = 3
WI, WO = 2 * KT * MLP, MT * EMB
PIECES = 2 * EXPERTS
PIECE = EXPERTS * WI // PIECES
RAW = 3


def shape_constants():
    exponents = np.arange(0, HD, 2, dtype=np.float32) / np.float32(HD)
    inv = (np.float32(1.0) / np.power(np.float32(THETA), exponents)).astype(np.float32)
    ang = np.arange(SEQ, dtype=np.float32)[:, None] * inv[None, :]
    cos, sin = np.cos(ang).astype(np.float32), np.sin(ang).astype(np.float32)
    cos2 = np.concatenate([cos, cos], 1).reshape(TT, P, HD).transpose(1, 0, 2)
    sin2 = np.concatenate([-sin, sin], 1).reshape(TT, P, HD).transpose(1, 0, 2)
    q, k = np.arange(P)[:, None], np.arange(P)[None, :]
    mask = np.concatenate([np.zeros((P, P)), np.where(k > q, MASKED, 0.0)], 1).astype(np.float32)
    ident = np.eye(P, dtype=np.float32)
    before = (q < k).astype(np.float32)
    ones = np.ones((P, P), np.float32)
    attn = np.concatenate([cos2.reshape(P, -1), sin2.reshape(P, -1), mask, ident], 1)
    rev = np.tile(EXPERTS - np.arange(EXPERTS, dtype=np.float32), TILES)
    steps = np.tile(P * np.arange(TILES, dtype=np.float32), EXPERTS)
    earlier = np.tril(np.ones((EXPERTS, EXPERTS), np.float32), -1).reshape(-1)
    starts = np.repeat(P * np.arange(BLOCKS + 1, dtype=np.float32), EXPERTS)
    lanes = np.arange(P, dtype=np.float32)
    groups = np.arange(1, 2 * TILES + 1, dtype=np.float32)
    route = np.concatenate([before, ones, np.tile(np.concatenate([rev, steps, starts]), (P, 1)),
                            np.tile(np.concatenate([lanes, groups, earlier]), (P, 1)), lanes[:, None]], 1)
    return np.ascontiguousarray(attn, np.float32), np.ascontiguousarray(route, np.float32)


def attention(nc, ctx, t, x_all, r=None):

    def sb(name, shape, dt=F32):
        return ctx.enter_context(nc.sbuf_tensor(name, shape, dt))

    def sem(name):
        return ctx.enter_context(nc.semaphore(name))

    tables = sb("tables", [P, 2 * TT * HD + 3 * P])
    cos = tables[:, 0:TT * HD].rearrange("p (t d) -> p t d", t=TT)
    sin = tables[:, TT * HD:2 * TT * HD].rearrange("p (t d) -> p t d", t=TT)
    mask = tables[:, 2 * TT * HD:2 * TT * HD + 2 * P]
    ident = tables[:, 2 * TT * HD + 2 * P:2 * TT * HD + 3 * P]

    w_raw = sb("w_raw", [P, 2, KT * GW])
    wo_raw = sb("wo_raw", [P, 2, PAIRS * EMB])
    w_hi = sb("w_hi", [P, KT, KV_HEADS * GW], F32R)
    w_lo = sb("w_lo", [P, KT, KV_HEADS * GW], F32R)
    wo_hi = sb("wo_hi", [P, HEADS // 2 * EMB], F32R)
    wo_lo = sb("wo_lo", [P, HEADS // 2 * EMB], F32R)

    stats = sb("stats", [P, TILES, 6])
    moments = sb("moments", [P, TILES, 2])
    rstd = sb("rstd", [P, TILES])
    newton = sb("newton", [P, 3, TILES])
    xn = sb("xn", [P, TT, EMB])
    xT_hi = sb("xT_hi", [P, KT, SEQ], F32R)
    xT_lo = sb("xT_lo", [P, KT, SEQ], F32R)

    by_cos = sb("by_cos", [P, TT, QK])
    by_sin = sb("by_sin", [P, TT, QK])
    rotated = sb("rotated", [P, TT, QK])
    stack = sb("stack", [P, TT, STACK])
    v_raw = sb("v_raw", [P, TT, HD])
    v_hi = sb("v_hi", [P, 2, TT, 3 * HD], F32R)
    v_lo = sb("v_lo", [P, 2, TT, 3 * HD], F32R)
    qT = sb("qT", [P, TT, GROUP * P], F32R)
    kT = sb("kT", [P, 2, SEQ], F32R)
    masked = sb("masked", [P, 2, 3 * P])
    neg_max = sb("neg_max", [P, 2, TT])
    exps = sb("exps", [P, 2, 3 * P])
    sums = sb("sums", [P, 2, TT])
    inv_sums = sb("inv_sums", [P, 2, TT])
    probs = sb("probs", [P, GROUP, 3 * P])
    pT_hi = sb("pT_hi", [P, GROUP, 3 * P], F32R)
    pT_lo = sb("pT_lo", [P, GROUP, 3 * P], F32R)
    oT_hi = sb("oT_hi", [P, PAIRS, SEQ], F32R)
    oT_lo = sb("oT_lo", [P, PAIRS, SEQ], F32R)

    def bank(name):
        return ctx.enter_context(nc.psum_tensor(name, [P, 512], F32))

    work = [bank("work0"), bank("work1")]
    s_bank = [bank("scores0"), bank("scores1")]
    p_bank = [bank("probsT0"), bank("probsT1")]
    o_bank = bank("heads_out")
    y_bank = bank("attn_out")

    consts_in = sem("consts_in")
    x_first_in = sem("x_first_in")
    x_rest_in = sem("x_rest_in")
    w_in = [sem("w_in0"), sem("w_in1")]
    w_split = sem("w_split")
    w_hi_done = sem("w_hi_done")
    wo_in = [sem("wo_in0"), sem("wo_in1")]
    wo_hi_done = sem("wo_hi_done")
    wo_split = sem("wo_split")
    zeroed = sem("zeroed")
    step = sem("step")
    dve_passed = sem("dve_passed")
    pool_passed = sem("pool_passed")
    xn_done = sem("xn_done")
    xT_ps = sem("xT_ps")
    xT_hi_done = sem("xT_hi_done")
    xT_lo_done = sem("xT_lo_done")
    proj_ps = sem("proj_ps")
    v_read = sem("v_read")
    v_hi_done = sem("v_hi_done")
    v_done = sem("v_done")
    rope_parts = sem("rope_parts")
    rope_done = sem("rope_done")
    stack_hi = sem("stack_hi")
    stack_lo = sem("stack_lo")
    qT_ps = sem("qT_ps")
    qT_done = sem("qT_done")
    kT_ps = sem("kT_ps")
    kT_done = sem("kT_done")
    s_ps = sem("s_ps")
    s_read = sem("s_read")
    exp_done = sem("exp_done")
    inv_done = sem("inv_done")
    probs_done = sem("probs_done")
    pT_ps = sem("pT_ps")
    pT_hi_done = sem("pT_hi_done")
    pT_lo_done = sem("pT_lo_done")
    o_ps = sem("o_ps")
    o_hi_done = sem("o_hi_done")
    o_lo_done = sem("o_lo_done")
    y_ps = sem("y_ps")
    y_added = sem("y_added")


    GO = PAIRS * EMB
    TURNS = BATCH * KV_HEADS

    def past(n, k):
        return not isinstance(n, int) or n >= k

    def turns(eng, turn):
        def pair(b, i, prepare, last):
            turn(b * KV_HEADS + i * 2, 0, i * 2, b, prepare, False)
            turn(b * KV_HEADS + i * 2 + 1, 1, i * 2 + 1, b, False, last)

        def rounds(b, last_batch):
            with eng.Fori(0, KV_HEADS // 2 - 1) as i:
                pair(b, i, False, False)
            pair(b, KV_HEADS // 2 - 1, not last_batch, last_batch)
        pair(0, 0, False, False)
        with eng.Fori(1, KV_HEADS // 2 - 1) as i:
            pair(0, i, False, False)
        pair(0, KV_HEADS // 2 - 1, True, False)
        with eng.Fori(1, BATCH - 1) as b:
            rounds(b, False)
        rounds(BATCH - 1, True)

    block = ctx.enter_context(nc.Block())

    @block.sync
    def _(sp):
        sp.dma_start(tables[:, :], t["attn_consts"]).then_inc(consts_in, 16)
        x_dram = t["x"].rearrange("b (t p) e -> p (b t) e", p=P)
        sp.dma_start(x_all[:, 0:TT, :], x_dram[:, 0:TT, :]).then_inc(x_first_in, 16)
        for g in range(KV_HEADS):
            if g >= 2:
                sp.wait_ge(w_split, g - 1)
            sp.dma_start(w_raw[:, g % 2, :], t["w_qkv"][:, g, :]).then_inc(w_in[g % 2], 16)
            if g == 0:
                sp.dma_start(x_all[:, TT:TILES, :], x_dram[:, TT:TILES, :]).then_inc(x_rest_in, 16)
            if g >= 2:
                sp.wait_ge(wo_split, g - 1)
            sp.dma_start(wo_raw[:, g % 2, :], t["wo"][:, g * GO:(g + 1) * GO]).then_inc(wo_in[g % 2], 16)
        for i in range(RAW):
            sp.dma_start(r["w_raw"][:, i, :], t["w_in"][:, i * PIECE:(i + 1) * PIECE]).then_inc(r["piece_in"][i], 16)

    @block.tensor
    def _(pe):
        def x_transposes(b):
            pe.wait_ge(xn_done, b + 1)
            for k in range(KT):
                for tt in range(TT):
                    mm = nc.tensor.transpose(y_bank[:, (k * TT + tt) * P:(k * TT + tt + 1) * P],
                                             xn[:, tt, k * P:(k + 1) * P], ident)
            mm.then_inc(xT_ps, 1)

        def project(m, parity, g, tt):
            ps = work[(tt + parity) % 2]
            n = 0
            for k in range(KT):
                for a, w in ((xT_hi, w_hi), (xT_lo, w_hi), (xT_hi, w_lo)):
                    mm = nc.tensor.matmul(ps[:, 0:GW], a[:, k, tt * P:(tt + 1) * P], w[:, k, bass.ds(g * GW, GW)],
                                          start=(n == 0), stop=(n == 3 * KT - 1))
                    n += 1
            mm.then_inc(proj_ps, 1)

        def q_transposes(m, parity, tt):
            ps = work[(tt + parity) % 2]
            pe.wait_ge(stack_hi, m * 2 + tt + 1)
            pe.wait_ge(stack_lo, m * 2 + tt + 1)
            for h in range(GROUP):
                mm = nc.tensor.transpose(ps[:, h * P:(h + 1) * P], stack[:, tt, h * P:(h + 1) * P], ident)
            mm.then_inc(qT_ps, 1)

        def k_transposes(m, parity):
            ps = work[parity]
            pe.wait_ge(qT_done, m * 2 + 1)
            for form in range(2):
                at = GROUP * P + form * HD
                for tt in range(TT):
                    mm = nc.tensor.transpose(ps[:, (form * TT + tt) * P:(form * TT + tt + 1) * P],
                                             stack[:, tt, at:at + P], ident)
            mm.then_inc(kT_ps, 1)

        def scores(n, h):
            ps = s_bank[h % 2]
            pe.wait_ge(s_read, n * GROUP + h + 1)
            for tt in range(TT):
                for form in range(2):
                    mm = nc.tensor.matmul(ps[:, tt * SEQ:(tt + 1) * SEQ], qT[:, tt, h * P:(h + 1) * P], kT[:, form, :],
                                          start=(form == 0), stop=(form == 1))
            mm.then_inc(s_ps, 1)

        def prob_transposes(n, h):
            ps = p_bank[h % 2]
            pe.wait_ge(probs_done, n * GROUP + h + 3)
            pe.wait_ge(pT_lo_done, n * GROUP + h + 3)
            for c, (lo, at) in enumerate(((0, 0), (P, P), (2 * P, 2 * P))):
                mm = nc.tensor.transpose(ps[:, at:at + P], probs[:, h, lo:lo + P], ident)
            mm.then_inc(pT_ps, 1)

        def values(n, parity, odd):
            pe.wait_ge(pT_lo_done, n * GROUP + 3 + odd)
            if not odd:
                pe.wait_ge(v_done, n)
                if past(n, 2):
                    pe.wait_ge(o_lo_done, n - 1)
            out = o_bank[:, :].rearrange("p (pair q) -> p pair q", pair=PAIRS)
            first = not odd
            form = slice(0, 2 * HD) if odd else slice(HD, 3 * HD)
            for kt in range(TT):
                for v, pT in ((v_hi, pT_hi), (v_lo, pT_hi), (v_hi, pT_lo)):
                    heads = pT[:, odd:GROUP:2, :]
                    if kt == 0:
                        mm = nc.tensor.matmul(out, v[:, parity, kt, form], heads[:, :, 0:2 * P],
                                              start=first, stop=False, skip_group_check=True)
                    else:
                        mm = nc.tensor.matmul(out[:, :, P:2 * P], v[:, parity, kt, form], heads[:, :, 2 * P:3 * P],
                                              start=False, stop=True, skip_group_check=True)
                    first = False
            if odd:
                mm.then_inc(o_ps, 1)

        def output(n, g_out, tt):
            if tt == 0:
                pe.wait_ge(o_lo_done, n - 1)
                pe.wait_ge(y_added, n - 1)
            i = 0
            for pair in range(PAIRS):
                for o, w in ((oT_hi, wo_hi), (oT_lo, wo_hi), (oT_hi, wo_lo)):
                    mm = nc.tensor.matmul(y_bank[:, tt * EMB:(tt + 1) * EMB], o[:, pair, tt * P:(tt + 1) * P],
                                          w[:, bass.ds((g_out * PAIRS + pair) * EMB, EMB)],
                                          start=(i == 0), stop=(i == 3 * PAIRS - 1))
                    i += 1
            if tt == TT - 1:
                mm.then_inc(y_ps, 1)

        def turn(n, parity, g, b, prepare, last):
            m, odd = n + 1, 1 - parity
            g_next = (g + 1) % KV_HEADS
            pe.wait_ge(qT_done, n * 2 + 2)
            pe.wait_ge(kT_done, n + 1)
            scores(n, 0)
            if not last:
                if isinstance(b, int) and b == 0 and not (isinstance(g, int) and g == KV_HEADS - 1):
                    pe.wait_ge(w_split, g + 2)
                if isinstance(g, int) and g == KV_HEADS - 1:
                    pe.wait_ge(xT_lo_done, b + 2)
                project(m, odd, g_next, 0)
            if past(n, 1):
                prob_transposes(n - 1, 2)
            scores(n, 1)
            if past(n, 1):
                prob_transposes(n - 1, 3)
            if not last:
                project(m, odd, g_next, 1)
            if past(n, 2):
                if isinstance(b, int) and b == 0:
                    pe.wait_ge(wo_split, g - 1)
                output(n, (g + KV_HEADS - 2) % KV_HEADS, 0)
            scores(n, 2)
            scores(n, 3)
            if past(n, 1):
                if isinstance(n, int) and n == 1:
                    pe.wait_ge(zeroed, 1)
                values(n, odd, 0)
            if not last:
                q_transposes(m, odd, 0)
            if past(n, 2):
                output(n, (g + KV_HEADS - 2) % KV_HEADS, 1)
            prob_transposes(n, 0)
            if not last:
                q_transposes(m, odd, 1)
                k_transposes(m, odd)
            if past(n, 1):
                values(n, odd, 1)
            if prepare:
                pe.wait_ge(y_added, n)
                x_transposes(b + 1)
            prob_transposes(n, 1)
            if isinstance(n, int) and n == KV_HEADS - 1:
                pe.wait_ge(wo_split, KV_HEADS)

        pe.wait_ge(consts_in, 16)
        x_transposes(0)
        pe.wait_ge(xT_lo_done, 1)
        pe.wait_ge(w_split, 1)
        project(0, 0, 0, 0)
        project(0, 0, 0, 1)
        q_transposes(0, 0, 0)
        q_transposes(0, 0, 1)
        k_transposes(0, 0)
        turns(pe, turn)
        prob_transposes(TURNS - 1, 2)
        prob_transposes(TURNS - 1, 3)
        output(TURNS, KV_HEADS - 2, 0)
        output(TURNS, KV_HEADS - 2, 1)
        values(TURNS, 1, 0)
        values(TURNS, 1, 1)
        output(TURNS + 1, KV_HEADS - 1, 0)
        output(TURNS + 1, KV_HEADS - 1, 1)

    @block.scalar
    def _(act):
        def x_hi(b):
            act.wait_ge(xT_ps, b + 1)
            nc.scalar.copy(xT_hi[:, :, :], y_bank[:, :].rearrange("p (k q) -> p k q", k=KT)).then_inc(xT_hi_done, 1)

        def split_stack(m, tt, first=False):
            act.wait_ge(rope_done, m * 2 + tt + 1)
            if not first:
                act.wait_ge(kT_ps, m)
            hi = stack[:, tt, 0:(GROUP + 1) * P].rearrange("p (h two d) -> p h two d", two=2, d=HD)[:, :, 1, :]
            nc.scalar.copy(hi.bitcast(F32R), rotated[:, tt, :].rearrange("p (h d) -> p h d", d=HD)).then_inc(stack_hi, 1)

        def copy_qT(m, parity, tt):
            act.wait_ge(qT_ps, m * 2 + tt + 1)
            nc.scalar.copy(qT[:, tt, :], work[(tt + parity) % 2][:, :]).then_inc(qT_done, 1)

        def copy_kT(m, parity):
            act.wait_ge(kT_ps, m + 1)
            nc.scalar.copy(kT[:, :, :], work[parity][:, :].rearrange("p (f q) -> p f q", f=2)).then_inc(kT_done, 1)

        def exponentials(n, h):
            s = h % 2
            act.wait_ge(s_read, n * GROUP + h + 3)
            act.wait_ge(probs_done, n * GROUP + h + 1)
            nc.scalar.activation(exps[:, s, 0:P], masked[:, s, 0:P], ACT.Exp, bias=neg_max[:, s, 0:1], scale=-1.0,
                                 accum_out=sums[:, s, 0:1])
            nc.scalar.activation(exps[:, s, P:3 * P], masked[:, s, P:3 * P], ACT.Exp, bias=neg_max[:, s, 1:2],
                                 scale=-1.0, accum_out=sums[:, s, 1:2]).then_inc(exp_done, 1)

        def probs_hi(n, h):
            act.wait_ge(pT_ps, n * GROUP + h + 5)
            nc.scalar.copy(pT_hi[:, h, :], p_bank[h % 2][:, 0:3 * P]).then_inc(pT_hi_done, 1)

        def out_hi(n):
            act.wait_ge(o_ps, n)
            nc.scalar.copy(oT_hi[:, :, :], o_bank[:, :].rearrange("p (pair q) -> p pair q", pair=PAIRS)).then_inc(o_hi_done, 1)

        def split_w(p, g):
            act.wait_ge(w_in[p], g * 8 - p * 8 + 16)
            nc.scalar.copy(w_hi[:, :, bass.ds(g * GW, GW)],
                           w_raw[:, p, :].rearrange("p (k n) -> p k n", k=KT)).then_inc(w_hi_done, 1)

        def split_wo(p, g):
            act.wait_ge(wo_in[p], g * 8 - p * 8 + 16)
            nc.scalar.copy(wo_hi[:, bass.ds(g * GO, GO)], wo_raw[:, p, :]).then_inc(wo_hi_done, 1)

        def turn(n, parity, g, b, prepare, last):
            m, odd = n + 1, 1 - parity
            if past(n, 1):
                probs_hi(n - 1, 2)
            exponentials(n, 0)
            if not last:
                split_stack(m, 0)
            exponentials(n, 1)
            if past(n, 1):
                probs_hi(n - 1, 3)
            exponentials(n, 2)
            if not last:
                split_stack(m, 1)
            if isinstance(b, int) and b == 0:
                if not (isinstance(g, int) and g >= KV_HEADS - 2):
                    split_w(parity, g + 2)
                split_wo(parity, g)
            if not last:
                copy_qT(m, odd, 0)
            exponentials(n, 3)
            probs_hi(n, 0)
            if not last:
                copy_kT(m, odd)
                copy_qT(m, odd, 1)
            if prepare:
                x_hi(b + 1)
            if past(n, 1):
                out_hi(n)
            probs_hi(n, 1)

        act.sem_inc(exp_done, 2)
        x_hi(0)
        split_w(0, 0)
        split_stack(0, 0, True)
        split_stack(0, 1, True)
        copy_qT(0, 0, 0)
        copy_qT(0, 0, 1)
        copy_kT(0, 0)
        split_w(1, 1)
        turns(act, turn)
        probs_hi(TURNS - 1, 2)
        probs_hi(TURNS - 1, 3)
        out_hi(TURNS)

    @block.vector
    def _(dve):
        chain = [0]

        def wait_own(ins):
            chain[0] += 1
            ins.then_inc(step, 1)
            dve.wait_ge(step, chain[0])

        def normalise(b, first=False):
            if not first:
                dve.wait_ge(xT_ps, b)
            for tt in range(TT):
                at = bass.ds(b * TT + tt, 1)
                ins = nc.vector.tensor_scalar(xn[:, tt, :], x_all[:, at, :].rearrange("p o e -> p (o e)"),
                                              moments[:, at, 0:1].rearrange("p o e -> p (o e)"), rstd[:, at],
                                              ALU.subtract, ALU.mult)
            ins.then_inc(xn_done, 1)

        def x_lo(b):
            dve.wait_ge(xT_hi_done, b + 1)
            nc.vector.tensor_tensor(xT_lo[:, :, :], y_bank[:, :].rearrange("p (k q) -> p k q", k=KT),
                                    xT_hi[:, :, :].bitcast(F32), ALU.subtract).then_inc(xT_lo_done, 1)

        def rope(m, parity, tt, first=False):
            ps = work[(tt + parity) % 2]
            dve.wait_ge(proj_ps, m * 2 + tt + 1)
            if not first:
                dve.wait_ge(v_done, m)
                dve.wait_ge(rope_done, m * 2 + tt - 1)
            nc.vector.tensor_copy(v_raw[:, tt, :], ps[:, QK:GW]).then_inc(v_read, 1)
            x = ps[:, 0:QK].rearrange("p (h two d) -> p h two d", two=2, d=HD // 2)
            o = by_sin[:, tt, :].rearrange("p (h two d) -> p h two d", two=2, d=HD // 2)
            for half in range(2):
                s = sin[:, tt, half * 32:half * 32 + 32].rearrange("p (o d) -> p o d", o=1).to_broadcast([P, GROUP + 1, 32])
                nc.vector.tensor_tensor(o[:, :, half, :], x[:, :, 1 - half, :], s, ALU.mult)
            c = cos[:, tt, :].rearrange("p (o d) -> p o d", o=1).to_broadcast([P, GROUP + 1, HD])
            nc.vector.tensor_tensor(by_cos[:, tt, :].rearrange("p (h d) -> p h d", d=HD),
                                    ps[:, 0:QK].rearrange("p (h d) -> p h d", d=HD), c, ALU.mult).then_inc(rope_parts, 1)

        def stack_low(m, tt):
            dve.wait_ge(stack_hi, m * 2 + tt + 1)
            pairs = stack[:, tt, 0:(GROUP + 1) * P].rearrange("p (h two d) -> p h two d", two=2, d=HD)
            nc.vector.tensor_tensor(pairs[:, :, 0, :].bitcast(F32R), rotated[:, tt, :].rearrange("p (h d) -> p h d", d=HD),
                                    pairs[:, :, 1, :], ALU.subtract)
            k = GROUP * P
            nc.vector.tensor_tensor(stack[:, tt, k + 2 * HD:k + 3 * HD].bitcast(F32R), rotated[:, tt, GROUP * HD:QK],
                                    stack[:, tt, k + HD:k + 2 * HD], ALU.subtract).then_inc(stack_lo, 1)

        def maxima(n, h):
            s = h % 2
            dve.wait_ge(consts_in, 16)
            dve.wait_ge(s_ps, n * GROUP + h + 1)
            dve.wait_ge(exp_done, n * GROUP + h + 1)
            dve.sem_inc(dve_passed, 1)
            nc.vector.tensor_tensor_reduce(masked[:, s, 0:P], s_bank[s][:, 0:P], mask[:, P:2 * P], -(HD ** -0.5), 3e38,
                                           ALU.add, ALU.min, neg_max[:, s, 0:1])
            nc.vector.tensor_tensor_reduce(masked[:, s, P:3 * P], s_bank[s][:, SEQ:2 * SEQ], mask[:, 0:2 * P],
                                           -(HD ** -0.5), 3e38, ALU.add, ALU.min, neg_max[:, s, 1:2]).then_inc(s_read, 1)

        def inverses(n, h):
            s = h % 2
            dve.wait_ge(exp_done, n * GROUP + h + 3)
            nc.vector.reciprocal(inv_sums[:, s, :], sums[:, s, :]).then_inc(inv_done, 1)

        def probs_lo(n, h):
            dve.wait_ge(pT_hi_done, n * GROUP + h + 1)
            nc.vector.tensor_tensor(pT_lo[:, h, :], p_bank[h % 2][:, 0:3 * P], pT_hi[:, h, :].bitcast(F32),
                                    ALU.subtract).then_inc(pT_lo_done, 1)

        def out_lo(n):
            dve.wait_ge(o_hi_done, n)
            nc.vector.tensor_tensor(oT_lo[:, :, :], o_bank[:, :].rearrange("p (pair q) -> p pair q", pair=PAIRS),
                                    oT_hi[:, :, :].bitcast(F32), ALU.subtract).then_inc(o_lo_done, 1)

        def add_out(n, b):
            dve.wait_ge(y_ps, n - 1)
            dve.wait_ge(y_added, n - 1)
            xs = x_all[:, bass.ds(b * TT, TT), :]
            nc.vector.tensor_tensor(xs, xs, y_bank[:, :].rearrange("p (t e) -> p t e", t=TT), ALU.add).then_inc(y_added, 1)

        def split_w(p, g):
            dve.wait_ge(w_hi_done, g + 1)
            nc.vector.tensor_tensor(w_lo[:, :, bass.ds(g * GW, GW)], w_raw[:, p, :].rearrange("p (k n) -> p k n", k=KT),
                                    w_hi[:, :, bass.ds(g * GW, GW)].bitcast(F32), ALU.subtract).then_inc(w_split, 1)

        def split_wo(p, g):
            dve.wait_ge(wo_hi_done, g + 1)
            nc.vector.tensor_tensor(wo_lo[:, bass.ds(g * GO, GO)], wo_raw[:, p, :],
                                    wo_hi[:, bass.ds(g * GO, GO)].bitcast(F32), ALU.subtract).then_inc(wo_split, 1)

        def turn(n, parity, g, b, prepare, last):
            m, odd = n + 1, 1 - parity
            maxima(n, 0)
            if not last:
                rope(m, odd, 0)
            maxima(n, 1)
            if past(n, 1):
                probs_lo(n - 1, 2)
            inverses(n, 0)
            if not last:
                rope(m, odd, 1)
            maxima(n, 2)
            if not last:
                stack_low(m, 0)
            inverses(n, 1)
            maxima(n, 3)
            if not last:
                stack_low(m, 1)
            if past(n, 1):
                probs_lo(n - 1, 3)
            inverses(n, 2)
            if prepare:
                normalise(b + 1)
            if past(n, 2):
                add_out(n, b + (g + KV_HEADS - 2) // KV_HEADS - 1)
            if isinstance(b, int) and b == 0:
                if not (isinstance(g, int) and g >= KV_HEADS - 2):
                    split_w(parity, g + 2)
                split_wo(parity, g)
            probs_lo(n, 0)
            inverses(n, 3)
            if isinstance(g, int) and g == KV_HEADS - 1 and not (isinstance(b, int) and b == 0):
                dve.wait_ge(y_added, n - 1)
                for tile in range(TT):
                    at = (b - 1) * TT + tile
                    nc.vector.bn_stats(r["stats"][:, bass.ds(at, 1), :].rearrange("p o s -> p (o s)"),
                                       x_all[:, bass.ds(at, 1), :].rearrange("p o e -> p (o e)"))
            if prepare:
                x_lo(b + 1)
            if past(n, 1):
                out_lo(n)
            probs_lo(n, 1)

        dve.sem_inc(s_read, 2)
        dve.sem_inc(y_added, 1)
        dve.sem_inc(pT_lo_done, 4)

        def layernorm_moments(a, b):
            for i in range(a, b):
                ins = nc.vector.bn_aggr(moments[:, i, :], stats[:, i, :])
            wait_own(ins)
            v, y, w = newton[:, 0, a:b], newton[:, 1, a:b], newton[:, 2, a:b]
            wait_own(nc.vector.tensor_scalar(v, moments[:, a:b, 1], EPS, None, ALU.add))
            wait_own(nc.vector.tensor_scalar(w.bitcast(I32), v.bitcast(I32), 1, None, ALU.logical_shift_right))
            wait_own(nc.vector.tensor_scalar(y.bitcast(I32), w.bitcast(I32), -1.0, RSQRT_MAGIC, ALU.mult, ALU.add))
            for i in range(4):
                wait_own(nc.vector.tensor_tensor(w, y, y, ALU.mult))
                wait_own(nc.vector.tensor_tensor(w, w, v, ALU.mult))
                wait_own(nc.vector.tensor_scalar(w, w, -0.5, 1.5, ALU.mult, ALU.add))
                wait_own(nc.vector.tensor_tensor(rstd[:, a:b] if i == 3 else y, y, w, ALU.mult))

        dve.wait_ge(x_first_in, 16)
        for i in range(TT):
            ins = nc.vector.bn_stats(stats[:, i, :], x_all[:, i, :])
        wait_own(ins)
        layernorm_moments(0, TT)
        normalise(0, True)
        x_lo(0)
        split_w(0, 0)
        dve.wait_ge(x_rest_in, 16)
        for i in range(TT, TT + 6):
            nc.vector.bn_stats(stats[:, i, :], x_all[:, i, :])
        rope(0, 0, 0, True)
        rope(0, 0, 1, True)
        stack_low(0, 0)
        stack_low(0, 1)
        for i in range(TT + 6, TILES):
            ins = nc.vector.bn_stats(stats[:, i, :], x_all[:, i, :])
        wait_own(ins)
        split_w(1, 1)
        layernorm_moments(TT, TILES)
        turns(dve, turn)
        probs_lo(TURNS - 1, 2)
        probs_lo(TURNS - 1, 3)
        add_out(TURNS, BATCH - 1)
        out_lo(TURNS)
        add_out(TURNS + 1, BATCH - 1)

    @block.gpsimd
    def _(pool):
        def rotate(m, tt, first=False):
            pool.wait_ge(rope_parts, m * 2 + tt + 1)
            if not first:
                pool.wait_ge(stack_hi, m * 2 + tt - 1)
                pool.wait_ge(stack_lo, m * 2 + tt - 1)
            nc.gpsimd.tensor_tensor(rotated[:, tt, :], by_cos[:, tt, :], by_sin[:, tt, :], ALU.add).then_inc(rope_done, 1)

        def divide(n, h):
            s = h % 2
            pool.wait_ge(inv_done, n * GROUP + h + 1)
            pool.wait_ge(pT_ps, n * GROUP + h + 1)
            pool.sem_inc(pool_passed, 1)
            nc.gpsimd.tensor_scalar(probs[:, h, 0:P], exps[:, s, 0:P], inv_sums[:, s, 0:1], 1.0, ALU.mult, ALU.mult)
            nc.gpsimd.tensor_scalar(probs[:, h, P:3 * P], exps[:, s, P:3 * P], inv_sums[:, s, 1:2], 1.0,
                                    ALU.mult, ALU.mult).then_inc(probs_done, 1)

        def split_v(m, parity):
            hi, lo = v_hi[:, parity, :, HD:2 * HD], v_lo[:, parity, :, HD:2 * HD]
            if past(m, 2):
                pool.wait_ge(o_ps, m - 1)
            pool.wait_ge(v_read, m * 2 + 2)
            pool.sem_inc(pool_passed, 1)
            nc.gpsimd.tensor_copy(hi, v_raw[:, :, :]).then_inc(v_hi_done, 1)
            pool.wait_ge(v_hi_done, m + 1)
            nc.gpsimd.tensor_tensor(lo, v_raw[:, :, :], hi.bitcast(F32), ALU.subtract).then_inc(v_done, 1)

        def turn(n, parity, g, b, prepare, last):
            m = n + 1
            split_v(n, parity)
            if not last:
                rotate(m, 0)
            divide(n, 0)
            if not last:
                rotate(m, 1)
            divide(n, 1)
            divide(n, 2)
            divide(n, 3)

        pool.sem_inc(probs_done, 2)
        pool.sem_inc(pT_ps, GROUP)
        for z in (v_hi[:, :, :, :], v_lo[:, :, :, :]):
            ins = nc.gpsimd.memset(z.bitcast(F32), 0.0)
        ins.then_inc(zeroed, 1)
        pool.wait_ge(zeroed, 1)
        rotate(0, 0, True)
        rotate(0, 1, True)
        turns(pool, turn)


def route(nc, ctx, t, x_all, r):

    def sb(name, shape, dt=F32):
        return ctx.enter_context(nc.sbuf_tensor(name, shape, dt))

    def sem(name):
        return ctx.enter_context(nc.semaphore(name))

    TE = TILES * EXPERTS
    SPAN = 4
    SPANS = TILES // SPAN
    at = 2 * P + 2 * TE + (BLOCKS + 1) * EXPERTS
    EE = EXPERTS * EXPERTS
    consts = sb("route_tables", [P, at + P + 2 * TILES + EE + 1])
    before, ones = consts[:, 0:P], consts[:, P:2 * P]
    rev = consts[:, 2 * P:2 * P + TE].rearrange("p (t e) -> p t e", e=EXPERTS)
    steps = consts[:, 2 * P + TE:2 * P + 2 * TE].rearrange("p (e t) -> p e t", e=EXPERTS)
    starts = consts[:, 2 * P + 2 * TE:at].rearrange("p (b e) -> p b e", e=EXPERTS)
    lanes, groups, lane = consts[:, at:at + P], consts[:, at + P:at + P + 2 * TILES], consts[:, at + P + 2 * TILES + EE:]
    experts_before = consts[:, at + P + 2 * TILES:at + P + 2 * TILES + EE].rearrange("p (e f) -> p e f", f=EXPERTS)
    before_16 = sb("before_16", [P, P], BF16)
    ones_16 = sb("ones_16", [P, P], BF16)
    ident = sb("route_ident", [P, P])
    gate = sb("gate_in", [P, KT, EXPERTS])

    stats = r["stats"]
    moments = sb("moments2", [P, TILES, 2])
    rstd = sb("rstd2", [P, TILES])
    newton = sb("newton2", [P, 2, TILES])
    half = TILES * EMB
    xn = r["w_out"][:, 0:half].rearrange("p (t e) -> p t e", e=EMB)
    w_raw, piece_in = r["w_raw"], r["piece_in"]
    used = half + RAW * PIECE
    lT = r["w_out"][0:EXPERTS, used:used + 2 * SPAN * P].rearrange("p (i c) -> p i c", i=2)
    xT = sb("xT2", [P, KT, SPAN * P])
    logits = sb("logits", [P, TILES, EXPERTS])
    others = sb("others", [P, TILES, EXPERTS])
    equal = sb("equal", [P, TILES, EXPERTS])
    hot = [sb("hot1", [P, TILES, EXPERTS]), sb("hot2", [P, TILES, EXPERTS])]
    both = sb("both", [P, TILES, EXPERTS], BF16)
    best = sb("best", [P, 2, TILES])
    code = sb("code", [P, TILES])
    gap = sb("gap", [P, TILES])
    blocks_before = sb("blocks_before", [P, EXPERTS, EXPERTS])
    full = sb("full", [P, EXPERTS, TILES])
    blocks = sb("blocks", [P, EXPERTS])
    first_row = sb("first_row", [P, EXPERTS])
    place = sb("place", [P, TILES, EXPERTS])
    chosen = sb("chosen", [P, TILES, EXPERTS])
    row = sb("row", [P, 2, TILES])
    later = sb("later", [P, BLOCKS + 1, EXPERTS])
    owner = sb("owner", [P, BLOCKS + 1])
    rows = sb("rows", [P, 2 * TILES], I32)
    row_part = sb("row_part", [P, 2, 2 * TILES], I32)
    row_block = sb("row_block", [P, 2 * TILES])
    row_lane = sb("row_lane", [P, 2 * TILES])
    lane_hot = sb("lane_hot", [P, 2 * TILES, P], BF16)
    block_codes = sb("block_codes", [P, 2 * TILES, 2, BLOCKS], BF16)
    pair_of = sb("pair_of", [P, 2, BLOCKS])

    tr_bank = [[ctx.enter_context(nc.psum_tensor(f"tr{i}_{k}", [P, SPAN * P], F32)) for k in range(KT)] for i in range(2)]
    lT_bank = ctx.enter_context(nc.psum_tensor("lT_bank", [P, SPAN * P], F32))
    logit_bank = ctx.enter_context(nc.psum_tensor("logit_bank", [P, 512], F32))
    rank_bank = ctx.enter_context(nc.psum_tensor("rank_bank", [P, 512], F32))
    pair_bank = ctx.enter_context(nc.psum_tensor("pair_bank", [P, 512], F32))

    consts_in = sem("route_consts_in")
    step = sem("route_step")
    xn_done = sem("xn2_done")
    xT_ps = sem("xT2_ps")
    xT_done = sem("xT2_done")
    lT_ps = sem("lT_ps")
    lT_done = sem("lT_done")
    logits_ps = sem("logits_ps")
    both_done = sem("both_done")
    ranks_ps = sem("ranks_ps")
    gap_done = sem("gap_done")
    exp_done = sem("gap_exp_done")
    block_hot_done = sem("block_hot_done")
    block_lane_done = sem("block_lane_done")
    lane_hot_done = sem("lane_hot_done")
    pairs_ps = sem("pairs_ps")
    xn_out = sem("xn_out")
    piece_hi_done = sem("piece_hi_done")
    piece_split = sem("piece_split")

    block = ctx.enter_context(nc.Block())

    @block.sync
    def _(sp):
        sp.dma_start(consts[:, :], t["route_consts"]).then_inc(consts_in, 16)
        sp.dma_start(ident[:, :], t["attn_consts"][:, 2 * TT * HD + 2 * P:]).then_inc(consts_in, 16)
        sp.dma_start(gate[:, :, :], t["gate"].rearrange("p (k e) -> p k e", k=KT)).then_inc(consts_in, 16)
        for i in range(RAW, PIECES):
            sp.wait_ge(piece_split, i - RAW + 1)
            sp.dma_start(w_raw[:, i % RAW, :], t["w_in"][:, i * PIECE:(i + 1) * PIECE]).then_inc(piece_in[i % RAW], 16)
        sp.wait_ge(xn_out, 16 * SPANS)
        sp.wait_ge(xT_ps, KT * SPANS)
        sp.dma_start(r["w_out"][:, 0:half], t["w_out"][:, 0:half]).then_inc(r["w_out_in"], 16)
        sp.wait_ge(piece_split, PIECES)
        sp.wait_ge(logits_ps, SPANS)
        sp.dma_start(r["w_out"][:, half:2 * half], t["w_out"][:, half:2 * half]).then_inc(r["w_out_in"], 16)

    @block.tensor
    def _(pe):
        def transposes(i):
            pe.wait_ge(xn_done, SPAN * (i + 1))
            for k in range(KT):
                if i >= 2:
                    pe.wait_ge(xT_done, (i - 2) * KT + k + 1)
                for tile in range(SPAN):
                    mm = nc.tensor.transpose(tr_bank[i % 2][k][:, tile * P:(tile + 1) * P],
                                             xn[:, SPAN * i + tile, k * P:(k + 1) * P], ident[:, :])
                mm.then_inc(xT_ps, 1)

        def gate_logits(i):
            if i >= 1:
                pe.wait_ge(lT_done, i)
            for k in range(KT):
                pe.wait_ge(xT_done, i * KT + k + 1)
                nc.tensor.matmul(lT_bank[0:EXPERTS, :], gate[:, k, :], xT[:, k, :],
                                 start=(k == 0), stop=(k == KT - 1)).then_inc(lT_ps, 1)

        def back(i):
            pe.wait_ge(lT_done, i + 1)
            for tile in range(SPAN):
                at = (SPAN * i + tile) * EXPERTS
                mm = nc.tensor.transpose(logit_bank[:, at:at + EXPERTS], lT[:, i % 2, tile * P:(tile + 1) * P],
                                         ident[0:EXPERTS, 0:EXPERTS])
            mm.then_inc(logits_ps, 1)

        pe.wait_ge(consts_in, 48)
        transposes(0)
        for i in range(SPANS):
            if i < SPANS - 1:
                transposes(i + 1)
            gate_logits(i)
            if i >= 1:
                back(i - 1)
        back(SPANS - 1)
        pe.wait_ge(both_done, 1)
        nc.tensor.matmul(rank_bank[:, 0:TE], before_16[:, :], both[:, :, :].rearrange("p t e -> p (t e)"), start=True,
                         stop=False, skip_group_check=True)
        for tile in range(TILES):
            after = TILES - tile
            m = both[:, tile, :].rearrange("p (o e) -> p o e", o=1).to_broadcast([P, after, EXPERTS])
            mm = nc.tensor.matmul(rank_bank[:, (tile + 1) * EXPERTS:TE + EXPERTS].rearrange("p (t e) -> p t e", e=EXPERTS),
                                  ones_16[:, :], m, start=False, stop=(tile == TILES - 1), skip_group_check=True)
        mm.then_inc(ranks_ps, 1)
        pe.wait_ge(block_lane_done, 1)
        for i in range(2 * TILES):
            pe.wait_ge(lane_hot_done, i // (TILES // 2) + 1)
            mm = nc.tensor.matmul(pair_bank[:, 0:2 * BLOCKS], lane_hot[:, i, :],
                                  block_codes[:, i, :, :].rearrange("p two b -> p (two b)"),
                                  start=(i == 0), stop=(i == 2 * TILES - 1))
        mm.then_inc(pairs_ps, 1)

    @block.scalar
    def _(act):
        def piece_hi(i):
            act.wait_ge(piece_in[i % RAW], 16 * (i // RAW + 1))
            nc.scalar.copy(r["w_hi"][:, i * PIECE:(i + 1) * PIECE], w_raw[:, i % RAW, :]).then_inc(piece_hi_done, 1)

        for i in range(5):
            piece_hi(i)
        def copy_tiles(i):
            for k in range(KT):
                act.wait_ge(xT_ps, i * KT + k + 1)
                if i >= 1:
                    act.wait_ge(lT_ps, (i - 1) * KT + k + 1)
                nc.scalar.copy(xT[:, k, :], tr_bank[i % 2][k][:, :]).then_inc(xT_done, 1)

        copy_tiles(0)
        for i in range(SPANS):
            act.wait_ge(xn_done, SPAN * (i + 1))
            tiles = slice(SPAN * i, SPAN * (i + 1))
            nc.scalar.dma_start(t["xn"].rearrange("(t p) e -> p t e", p=P)[:, tiles, :], xn[:, tiles, :]).then_inc(xn_out, 16)
            if i < SPANS - 1:
                copy_tiles(i + 1)
            act.wait_ge(lT_ps, (i + 1) * KT)
            if i >= 2:
                act.wait_ge(logits_ps, i - 1)
            nc.scalar.copy(lT[:, i % 2, :], lT_bank[0:EXPERTS, :]).then_inc(lT_done, 1)
            piece_hi(i + 5)
        for i in range(SPANS + 5, 10):
            piece_hi(i)
        act.wait_ge(gap_done, 1)
        nc.scalar.activation(gap[:, :], gap[:, :], ACT.Exp).then_inc(exp_done, 1)
        for i in range(10, PIECES):
            piece_hi(i)
        act.wait_ge(block_hot_done, 1)
        nc.scalar.activation(block_codes[:, :, 1, :], block_codes[:, :, 1, :], ACT.Copy,
                             scale=lane).then_inc(block_lane_done, 1)
        act.wait_ge(xn_out, 16 * SPANS)

    @block.gpsimd
    def _(pool):
        for i in range(PIECES):
            pool.wait_ge(piece_hi_done, i + 1)
            cols = slice(i * PIECE, (i + 1) * PIECE)
            nc.gpsimd.tensor_tensor(r["w_lo"][:, cols], w_raw[:, i % RAW, :], r["w_hi"][:, cols].bitcast(F32),
                                    ALU.subtract).then_inc(piece_split, 1)

    @block.vector
    def _(dve):
        chain = [0]

        def wait_own(ins):
            chain[0] += 1
            ins.then_inc(step, 1)
            dve.wait_ge(step, chain[0])

        for i in range(TILES - TT, TILES):
            ins = nc.vector.bn_stats(stats[:, i, :], x_all[:, i, :])
        wait_own(ins)
        for i in range(TILES):
            ins = nc.vector.bn_aggr(moments[:, i, :], stats[:, i, :])
        wait_own(ins)
        v, y, w = newton[:, 0, :], rstd[:, :], newton[:, 1, :]
        wait_own(nc.vector.tensor_scalar(v, moments[:, :, 1], EPS, None, ALU.add))
        wait_own(nc.vector.tensor_scalar(w.bitcast(I32), v.bitcast(I32), 1, None, ALU.logical_shift_right))
        wait_own(nc.vector.tensor_scalar(y.bitcast(I32), w.bitcast(I32), -1.0, RSQRT_MAGIC, ALU.mult, ALU.add))
        for i in range(4):
            wait_own(nc.vector.tensor_tensor(w, y, y, ALU.mult))
            wait_own(nc.vector.tensor_tensor(w, w, v, ALU.mult))
            wait_own(nc.vector.tensor_scalar(w, w, -0.5, 1.5, ALU.mult, ALU.add))
            wait_own(nc.vector.tensor_tensor(y, y, w, ALU.mult))
        for i in range(TILES):
            nc.vector.tensor_scalar(xn[:, i, :], x_all[:, i, :], moments[:, i, 0:1], rstd[:, i:i + 1],
                                    ALU.subtract, ALU.mult).then_inc(xn_done, 1)

        def over_experts(a):
            return a.rearrange("p (t o) -> p t o", o=1).to_broadcast([P, TILES, EXPERTS])

        def choose(c, scores):
            wait_own(nc.vector.tensor_reduce(best[:, c, :], scores, AX.X, ALU.max))
            wait_own(nc.vector.tensor_tensor(equal[:, :, :], scores, over_experts(best[:, c, :]), ALU.is_equal))
            wait_own(nc.vector.tensor_tensor(equal[:, :, :], equal[:, :, :], rev, ALU.mult))
            wait_own(nc.vector.tensor_reduce(code[:, :], equal[:, :, :], AX.X, ALU.max))
            wait_own(nc.vector.tensor_tensor(hot[c][:, :, :], rev, over_experts(code[:, :]), ALU.is_equal))

        dve.wait_ge(consts_in, 48)
        nc.vector.tensor_copy(before_16[:, :], before)
        nc.vector.tensor_copy(ones_16[:, :], ones)
        dve.wait_ge(logits_ps, SPANS)
        wait_own(nc.vector.tensor_copy(logits[:, :, :], logit_bank[:, 0:TE].rearrange("p (t e) -> p t e", e=EXPERTS)))
        dve.wait_ge(consts_in, 48)
        choose(0, logits[:, :, :])
        wait_own(nc.vector.scalar_tensor_tensor(out=others[:, :, :], in0=hot[0][:, :, :], scalar=-3e38,
                                                in1=logits[:, :, :], op0=ALU.mult, op1=ALU.add))
        choose(1, others[:, :, :])
        nc.vector.tensor_tensor(both[:, :, :], hot[0][:, :, :], hot[1][:, :, :], ALU.add).then_inc(both_done, 1)
        nc.vector.tensor_tensor(gap[:, :], best[:, 1, :], best[:, 0, :], ALU.subtract).then_inc(gap_done, 1)
        dve.wait_ge(exp_done, 1)
        wait_own(nc.vector.tensor_scalar(code[:, :], gap[:, :], 1.0, None, ALU.add))
        wait_own(nc.vector.reciprocal(r["weights"][:, 0, :], code[:, :]))
        nc.vector.tensor_tensor(r["weights"][:, 1, :], gap[:, :], r["weights"][:, 0, :], ALU.mult)

        dve.wait_ge(ranks_ps, 1)
        all_counts = rank_bank[:, TE:TE + EXPERTS].rearrange("p (e o) -> p e o", o=1).to_broadcast([P, EXPERTS, TILES])
        wait_own(nc.vector.tensor_tensor(full[:, :, :], all_counts, steps, ALU.is_gt))
        wait_own(nc.vector.tensor_reduce(blocks[:, :], full[:, :, :], AX.X, ALU.add))
        line = blocks[:, :].rearrange("p (o e) -> p o e", o=1).to_broadcast([P, EXPERTS, EXPERTS])
        wait_own(nc.vector.tensor_tensor(blocks_before[:, :, :], line, experts_before, ALU.mult))
        wait_own(nc.vector.tensor_reduce(first_row[:, :], blocks_before[:, :, :], AX.X, ALU.add))
        wait_own(nc.vector.tensor_scalar(first_row[:, :], first_row[:, :], float(P), None, ALU.mult))
        firsts = first_row[:, :].rearrange("p (o e) -> p o e", o=1).to_broadcast([P, TILES, EXPERTS])
        wait_own(nc.vector.tensor_tensor(place[:, :, :], rank_bank[:, 0:TE].rearrange("p (t e) -> p t e", e=EXPERTS),
                                         firsts, ALU.add))
        for c in range(2):
            wait_own(nc.vector.tensor_tensor(chosen[:, :, :], hot[c][:, :, :], place[:, :, :], ALU.mult))
            wait_own(nc.vector.tensor_reduce(row[:, c, :], chosen[:, :, :], AX.X, ALU.add))
        wait_own(nc.vector.tensor_copy(rows[:, :], row[:, :, :].rearrange("p c t -> p (c t)")))
        nc.vector.tensor_scalar(row_part[:, 0, :], rows[:, :], 7, None, ALU.logical_shift_right)
        wait_own(nc.vector.tensor_scalar(row_part[:, 1, :], rows[:, :], P - 1, None, ALU.bitwise_and))
        nc.vector.tensor_copy(row_block[:, :], row_part[:, 0, :])
        wait_own(nc.vector.tensor_copy(row_lane[:, :], row_part[:, 1, :]))

        def spread(a, n):
            return a.rearrange("p (t o) -> p t o", o=1).to_broadcast([P, a.shape[1], n])

        blocks_line = starts[:, 0:BLOCKS, 0].rearrange("p (o b) -> p o b", o=1).to_broadcast([P, 2 * TILES, BLOCKS])
        wait_own(nc.vector.tensor_scalar(row_block[:, :], row_block[:, :], float(P), None, ALU.mult))
        block_hot = block_codes[:, :, 1, :]
        wait_own(nc.vector.tensor_tensor(block_hot, blocks_line, spread(row_block[:, :], BLOCKS), ALU.is_equal))
        nc.vector.tensor_tensor(block_codes[:, :, 0, :], block_hot, spread(groups, BLOCKS),
                                ALU.mult).then_inc(block_hot_done, 1)
        lanes_line = lanes.rearrange("p (o q) -> p o q", o=1).to_broadcast([P, TILES // 2, P])
        for i in range(0, 2 * TILES, TILES // 2):
            nc.vector.tensor_tensor(lane_hot[:, i:i + TILES // 2, :], lanes_line, spread(row_lane[:, i:i + TILES // 2], P),
                                    ALU.is_equal).then_inc(lane_hot_done, 1)
        bounds = first_row[:, :].rearrange("p (o e) -> p o e", o=1).to_broadcast([P, BLOCKS + 1, EXPERTS])
        wait_own(nc.vector.tensor_tensor(later[:, :, :], starts, bounds, ALU.is_ge))
        wait_own(nc.vector.tensor_reduce(owner[:, :], later[:, :, :], AX.X, ALU.add))
        nc.vector.tensor_scalar(r["owners"][:, :], owner[:, :], -1.0, None, ALU.add)
        dve.wait_ge(pairs_ps, 1)
        wait_own(nc.vector.tensor_scalar(pair_of[:, 0, :], pair_bank[:, 0:BLOCKS], float(P), None, ALU.mult))
        wait_own(nc.vector.tensor_tensor(pair_of[:, 0, :], pair_of[:, 0, :], pair_bank[:, BLOCKS:2 * BLOCKS], ALU.add))
        wait_own(nc.vector.tensor_scalar(pair_of[:, 0, :], pair_of[:, 0, :], lane, None, ALU.max))
        nc.vector.tensor_copy(r["to_pair"][:, :], pair_of[:, 0, :])
        wait_own(nc.vector.tensor_scalar(pair_of[:, 1, :], pair_of[:, 0, :], float(TOKENS - P), None, ALU.add))
        wait_own(nc.vector.tensor_copy(r["from_token"][:, :], pair_of[:, 1, :]))
        wait_own(nc.vector.tensor_scalar(r["from_token"][:, :], r["from_token"][:, :], TOKENS - 1, None, ALU.bitwise_and))


def experts(nc, ctx, t, x_all, r):

    def sb(name, shape, dt=F32):
        return ctx.enter_context(nc.sbuf_tensor(name, shape, dt))

    def sem(name):
        return ctx.enter_context(nc.semaphore(name))

    w_hi, w_lo, w_out = r["w_hi"], r["w_lo"], r["w_out"]
    from_now = sb("from_now", [P, RING], U32)
    to_now = sb("to_now", [P, RING], U32)
    ident = sb("experts_ident", [P, P])
    xs = sb("xs", [P, RING, EMB])
    xT_hi = sb("xsT_hi", [P, RING, KT * P], F32R)
    xT_lo = sb("xsT_lo", [P, RING, KT * P], F32R)
    act_h = sb("act_h", [P, MLP])
    gated = sb("gated", [P, MLP])
    gT = sb("gT", [P, MT * P])
    y = sb("y", [P, RING, EMB])

    def bank(name):
        return ctx.enter_context(nc.psum_tensor(name, [P, 512], F32))

    tx, h0, h1, tg, yb = bank("tx"), bank("h0"), bank("h1"), bank("tg"), bank("yb")

    ident_in = sem("experts_ident_in")
    xs_in = [sem(f"xs_in{p}") for p in range(RING)]
    xT_ps = sem("xsT_ps")
    xT_hi_done = sem("xsT_hi_done")
    xT_lo_done = sem("xsT_lo_done")
    h0_ps = sem("h0_ps")
    h1_ps = sem("h1_ps")
    silu_done = sem("silu_done")
    gated_done = sem("gated_done")
    gT_ps = sem("gT_ps")
    gT_done = sem("gT_done")
    yb_ps = sem("yb_ps")
    y_done = sem("y_done")
    y_out = [sem(f"y_out{p}") for p in range(RING)]
    pool_passed = sem("experts_pool_passed")
    from_ready = sem("from_ready")
    to_ready = sem("to_ready")

    block = ctx.enter_context(nc.Block())

    def passes(eng, turn):
        for p in range(RING):
            turn(0, p)
        with eng.Fori(1, BLOCKS // RING - 1) as q:
            for p in range(RING):
                turn(q, p)
        for p in range(RING):
            turn(BLOCKS // RING - 1, p)

    def after(q, p, n=1):
        return q + (p + n) // RING, (p + n) % RING

    def is_block(q, p, j):
        return isinstance(q, int) and q * RING + p == j

    @block.sync
    def _(sp):
        sp.dma_start(ident[:, :], t["attn_consts"][:, 2 * TT * HD + 2 * P:]).then_inc(ident_in, 16)
        for p in range(RING):
            sp.wait_ge(y_out[p], 16 * BLOCKS // RING)

    @block.tensor
    def _(pe):
        def x_transposes(q, p, first=False):
            j = q * RING + p
            pe.wait_ge(xs_in[p], q * 16 + 16)
            if not first:
                pe.wait_ge(xT_lo_done, j)
            for k in range(KT):
                mm = nc.tensor.transpose(tx[:, k * P:(k + 1) * P], xs[:, p, k * P:(k + 1) * P], ident[:, :])
            mm.then_inc(xT_ps, 1)

        def hidden(j, p, expert, which):
            ps, done = ((h0, h0_ps), (h1, h1_ps))[which]
            n = 0
            for k in range(KT):
                for x, w in ((xT_hi, w_hi), (xT_hi, w_lo), (xT_lo, w_hi)):
                    mm = nc.tensor.matmul(ps[:, :], x[:, p, k * P:(k + 1) * P],
                                          w[:, bass.ds(expert * WI + (which * KT + k) * MLP, MLP)],
                                          start=(n == 0), stop=(n == 3 * KT - 1))
                    n += 1
            mm.then_inc(done, 1)

        def g_transposes(j):
            pe.wait_ge(gated_done, j + 1)
            for k in range(MT):
                mm = nc.tensor.transpose(tg[:, k * P:(k + 1) * P], gated[:, k * P:(k + 1) * P], ident[:, :])
            mm.then_inc(gT_ps, 1)

        def output(j, expert, first=False):
            pe.wait_ge(gT_done, j + 1)
            if not first:
                pe.wait_ge(y_done, j)
            for k in range(MT):
                mm = nc.tensor.matmul(yb[:, 0:EMB], gT[:, k * P:(k + 1) * P], w_out[:, bass.ds(expert * WO + k * EMB, EMB)],
                                      start=(k == 0), stop=(k == MT - 1))
            mm.then_inc(yb_ps, 1)

        def owner(j):
            return pe.value_load(r["owners"][0:1, bass.ds(j, 1)], min_val=0, max_val=EXPERTS - 1)

        def turn(q, p):
            j = q * RING + p
            if is_block(q, p, 0):
                hidden(0, 0, owner(0), 0)
                hidden(0, 0, owner(0), 1)
                x_transposes(0, 1)
                pe.wait_ge(r["w_out_in"], 32)
                return
            expert, last_expert = owner(j), owner(j - 1)
            pe.wait_ge(xT_lo_done, j + 1)
            pe.wait_ge(gated_done, j)
            hidden(j, p, expert, 0)
            g_transposes(j - 1)
            hidden(j, p, expert, 1)
            if not is_block(q, p, BLOCKS - 1):
                x_transposes(*after(q, p))
            output(j - 1, last_expert)

        pe.wait_ge(ident_in, 16)
        x_transposes(0, 0, True)
        pe.wait_ge(xT_lo_done, 1)
        passes(pe, turn)
        g_transposes(BLOCKS - 1)
        output(BLOCKS - 1, owner(BLOCKS - 1))

    @block.scalar
    def _(act):
        def x_copy(j, p):
            act.wait_ge(xT_ps, j + 1)
            nc.scalar.copy(xT_hi[:, p, :], tx[:, 0:KT * P]).then_inc(xT_hi_done, 1)

        def silu(j):
            act.wait_ge(h0_ps, j + 1)
            nc.scalar.activation(act_h[:, :], h0[:, :], SILU).then_inc(silu_done, 1)

        def g_copy(j):
            act.wait_ge(gT_ps, j + 1)
            nc.scalar.copy(gT[:, :], tg[:, :]).then_inc(gT_done, 1)

        def turn(q, p):
            j = q * RING + p
            if not is_block(q, p, 0):
                act.wait_ge(gated_done, j)
            silu(j)
            if not is_block(q, p, 0):
                g_copy(j - 1)
            if not is_block(q, p, BLOCKS - 1):
                x_copy(j + 1, (p + 1) % RING)

        x_copy(0, 0)
        passes(act, turn)
        g_copy(BLOCKS - 1)

    @block.vector
    def _(dve):
        def gate_rows(j, first=False):
            dve.wait_ge(silu_done, j + 1)
            dve.wait_ge(h1_ps, j + 1)
            if not first:
                dve.wait_ge(gT_ps, j)
            nc.vector.tensor_tensor(gated[:, :], h1[:, :], act_h[:, :], ALU.mult).then_inc(gated_done, 1)

        def x_lo(j, p):
            dve.wait_ge(xT_hi_done, j + 1)
            nc.vector.tensor_tensor(xT_lo[:, p, :], tx[:, 0:KT * P], xT_hi[:, p, :].bitcast(F32),
                                    ALU.subtract).then_inc(xT_lo_done, 1)

        def y_copy(q, p):
            dve.wait_ge(yb_ps, q * RING + p + 1)
            if not isinstance(q, int) or q > 0:
                dve.wait_ge(y_out[p], q * 16)
            nc.vector.tensor_copy(y[:, p, :], yb[:, 0:EMB]).then_inc(y_done, 1)

        def turn(q, p):
            if not is_block(q, p, BLOCKS - 1):
                gate_rows(q * RING + p + 1)
                if not is_block(q, p, BLOCKS - 2):
                    x_lo(q * RING + p + 2, (p + 2) % RING)
            y_copy(q, p)

        x_lo(0, 0)
        gate_rows(0, True)
        x_lo(1, 1)
        passes(dve, turn)

    @block.gpsimd
    def _(pool):
        def gather(q, p):
            j = q * RING + p
            if not isinstance(q, int) or q > 0:
                pool.wait_ge(xT_ps, j - RING + 1)
                pool.sem_inc(pool_passed, 1)
            nc.gpsimd.tensor_copy(from_now[:, p:p + 1], r["from_token"][:, bass.ds(j, 1)]).then_inc(from_ready, 1)
            pool.wait_ge(from_ready, j + 1)
            pool.sem_inc(pool_passed, 1)
            pool.indirect_dma_start(
                out=xs[:, p, :], out_offset=None, in_=t["xn"],
                in_offset=bass.IndirectOffsetOnAxis(ap=from_now[:, p:p + 1], axis=0)).then_inc(xs_in[p], 16)

        def scatter(q, p):
            j = q * RING + p
            pool.wait_ge(y_done, j + 1)
            if not is_block(q, p, 0):
                pool.wait_ge(y_out[(p - 1) % RING], (q + 1 if p else q) * 16)
            pool.sem_inc(pool_passed, 1)
            nc.gpsimd.tensor_copy(to_now[:, p:p + 1], r["to_pair"][:, bass.ds(j, 1)]).then_inc(to_ready, 1)
            pool.wait_ge(to_ready, j + 1)
            pool.sem_inc(pool_passed, 1)
            pool.indirect_dma_start(
                out=t["y_pairs"], out_offset=bass.IndirectOffsetOnAxis(ap=to_now[:, p:p + 1], axis=0),
                in_=y[:, p, :], in_offset=None).then_inc(y_out[p], 16)

        def turn(q, p):
            if not (isinstance(q, int) and q == BLOCKS // RING - 1):
                gather(q + 1, p)
            scatter(q, p)

        for p in range(RING):
            gather(0, p)
        passes(pool, turn)


def combine(nc, ctx, t, x_all, r):
    LOADS = 8
    SPAN = TILES // LOADS
    ya = ctx.enter_context(nc.sbuf_tensor("ya", [P, 2, TILES, EMB], F32))
    pairs_in = [ctx.enter_context(nc.semaphore(f"pairs_in{i}")) for i in range(LOADS)]
    weighed = ctx.enter_context(nc.semaphore("weighed"))
    summed = ctx.enter_context(nc.semaphore("summed"))
    stored = ctx.enter_context(nc.semaphore("stored"))
    pairs = t["y_pairs"][P:, :].rearrange("(c t p) e -> p c t e", c=2, p=P)
    block = ctx.enter_context(nc.Block())

    def load(queue, i, c):
        tiles = slice(i * SPAN, (i + 1) * SPAN)
        queue.dma_start(ya[:, c, tiles, :], pairs[:, c, tiles, :]).then_inc(pairs_in[i], 16)

    @block.sync
    def _(sp):
        for i in range(LOADS):
            load(sp, i, 0)
        for i in range(TILES):
            sp.wait_ge(summed, i + 1)
            sp.dma_start(t["out"].rearrange("b (t p) e -> (b t) p e", p=P)[i], x_all[:, i, :]).then_inc(stored, 16)
        sp.wait_ge(stored, 16 * TILES)

    @block.scalar
    def _(act):
        for i in range(LOADS):
            load(act, i, 1)

    @block.vector
    def _(dve):
        def add(i, c, done):
            xt = x_all[:, i, :]
            nc.vector.scalar_tensor_tensor(out=xt, in0=ya[:, c, i, :], scalar=r["weights"][:, c, i:i + 1], in1=xt,
                                           op0=ALU.mult, op1=ALU.add).then_inc(done, 1)

        for i in range(TILES + 1):
            if i < TILES:
                dve.wait_ge(pairs_in[i // SPAN], 32)
                add(i, 0, weighed)
            if i >= 1:
                dve.wait_ge(weighed, i)
                add(i - 1, 1, summed)


def program(nc, t):
    t = dict(t)
    t["xn"] = nc.dram_tensor("xn_rows", [TOKENS, EMB], F32).ap()
    t["y_pairs"] = nc.dram_tensor("y_pairs", [P + PAIRS_ALL, EMB], F32).ap()
    with ExitStack() as outer:
        x_all = outer.enter_context(nc.sbuf_tensor("x_all", [P, TILES, EMB], F32))
        r = {
            "stats": outer.enter_context(nc.sbuf_tensor("stats2", [P, TILES, 6], F32)),
            "to_pair": outer.enter_context(nc.sbuf_tensor("to_pair", [P, BLOCKS], U32)),
            "from_token": outer.enter_context(nc.sbuf_tensor("from_token", [P, BLOCKS], U32)),
            "weights": outer.enter_context(nc.sbuf_tensor("weights", [P, 2, TILES], F32)),
            "owners": outer.enter_context(nc.sbuf_tensor("owners", [P, BLOCKS + 1], I32)),
        }
        r["w_out"] = outer.enter_context(nc.sbuf_tensor("experts_w_out", [P, EXPERTS * WO], F32))
        r["w_out_in"] = outer.enter_context(nc.semaphore("w_out_in"))
        r["w_raw"] = r["w_out"][:, TILES * EMB:TILES * EMB + RAW * PIECE].rearrange("p (i c) -> p i c", c=PIECE)
        r["piece_in"] = [outer.enter_context(nc.semaphore(f"piece_in{i}")) for i in range(RAW)]
        with ExitStack() as ctx:
            attention(nc, ctx, t, x_all, r)
        with ExitStack() as ctx:
            r["w_hi"] = ctx.enter_context(nc.sbuf_tensor("experts_w_hi", [P, EXPERTS * WI], F32R))
            r["w_lo"] = ctx.enter_context(nc.sbuf_tensor("experts_w_lo", [P, EXPERTS * WI], F32R))
            with ExitStack() as part:
                route(nc, part, t, x_all, r)
            with ExitStack() as part:
                experts(nc, part, t, x_all, r)
        with ExitStack() as ctx:
            combine(nc, ctx, t, x_all, r)


def laid_out(x, wq, wk, wv, wo, gate, w0, w1, w2):
    wqT = wq.T.reshape(KT, P, KV_HEADS, GROUP * HD)
    wkT = wk.T.reshape(KT, P, KV_HEADS, HD)
    wvT = wv.T.reshape(KT, P, KV_HEADS, HD)
    w_qkv = np.concatenate([wqT, wkT, wvT], 3).transpose(1, 2, 0, 3).reshape(P, KV_HEADS, KT * GW)
    wo_t = wo.T.reshape(HEADS // 2, P, EMB).transpose(1, 0, 2).reshape(P, HEADS // 2 * EMB)
    attn, route = shape_constants()
    return {
        "x": x, "w_qkv": w_qkv, "wo": wo_t, "attn_consts": attn, "route_consts": route,
        "gate": gate.reshape(KT, P, EXPERTS).transpose(1, 0, 2).reshape(P, KT * EXPERTS),
        "w_in": np.concatenate([w0.reshape(EXPERTS, KT, P, MLP), w1.reshape(EXPERTS, KT, P, MLP)], 1)
        .transpose(2, 0, 1, 3).reshape(P, EXPERTS * 2 * KT * MLP),
        "w_out": w2.reshape(EXPERTS, MT, P, EMB).transpose(2, 0, 1, 3).reshape(P, EXPERTS * MT * EMB),
    }


def kernel(L0_attn_hidden_states, L0_attn_wq, L0_attn_wk, L0_attn_wv, L0_attn_wo, L0_attn_wq_s, L0_attn_wk_s,
           L0_attn_wv_s, L0_attn_wo_s, L0_ffn_gate_kernel, L0_ffn_w0_kernel, L0_ffn_w1_kernel, L0_ffn_wo_kernel):
    import concourse.bacc as bacc
    from concourse.bass_utils import run_bass_kernel_spmd

    arrays = laid_out(L0_attn_hidden_states, L0_attn_wq, L0_attn_wk, L0_attn_wv, L0_attn_wo,
                      L0_ffn_gate_kernel, L0_ffn_w0_kernel, L0_ffn_w1_kernel, L0_ffn_wo_kernel)
    arrays = {name: np.ascontiguousarray(a) for name, a in arrays.items()}
    nc = bacc.Bacc("TRN2", target_bir_lowering=False, num_devices=1)
    t = {name: nc.dram_tensor(name, a.shape, mybir.dt.from_np(a.dtype), kind="ExternalInput").ap()
         for name, a in arrays.items()}
    t["out"] = nc.dram_tensor("out", (BATCH, SEQ, EMB), F32, kind="ExternalOutput").ap()
    program(nc, t)
    return run_bass_kernel_spmd(nc, [arrays], core_ids=[0]).results[0]["out"]
```
